# Optimizing a Trainium2 kernel written in Bass

```python
import numpy as np
import jax
import jax.numpy as jnp

def _softmax(x, axis=-1):
    return jax.nn.softmax(x, axis=axis)
def _gelu(x):
    return jax.nn.gelu(x, approximate=True)
def _silu(x):
    return jax.nn.silu(x)
def _sigmoid(x):
    return jax.nn.sigmoid(x)
def _layernorm(x, axis=-1, eps=1e-5):
    m = jnp.mean(x, axis=axis, keepdims=True)
    v = jnp.var(x, axis=axis, keepdims=True)
    return (x - m) / jnp.sqrt(v + eps)
def _scatter_add(tgt, idx, src, axis=0):
    return tgt.at[idx].add(src)
def _segment_sum(src, seg, n):
    return jax.ops.segment_sum(src, seg, n)

kernel_name = 'mk_adj_preln_d4_adj_256_bb33f2'

def setup_inputs(seed: int = 0):
    np.random.seed(seed)
    _w = jnp.asarray
    def _rec_inputs():
        import jax
        import jax.numpy as jnp
        _gk = jax.random.key(seed)
        x = -0.0005207 + 1.001 * jax.random.normal(jax.random.fold_in(_gk, 1), (2708, 256), jnp.float32)
        _a = jax.random.bernoulli(jax.random.fold_in(_gk, 2), 0.00295421, (2708, 2708))
        _a = jnp.logical_or(_a, jnp.swapaxes(_a, -1, -2))
        _a = jnp.logical_or(_a, jnp.eye(2708, dtype=bool))
        _af = _a.astype(jnp.float32)
        _af = _af * jax.random.uniform(jax.random.fold_in(_gk, 3), (2708, 2708), jnp.float32, 0.05, 1)
        adj = _af
        return x, adj
    x, adj = _rec_inputs()
    def _L0_gnn_setup():
        import jax, jax.numpy as jnp
        import numpy as np
        import math
        N = 8192
        FIN = 256
        FOUT = 256
        key = jax.random.key(seed)
        k1, k2, k3, k4 = jax.random.split(key, 4)
        x = jax.random.normal(k1, (N, FIN), dtype=jnp.float32)
        adj = jax.random.uniform(k2, (N, N), dtype=jnp.float32)
        stdv = 1.0 / math.sqrt(FOUT)
        W = jax.random.uniform(k3, (FIN, FOUT), minval=-stdv, maxval=stdv, dtype=jnp.float32)
        b = jax.random.uniform(k4, (FOUT,), minval=-stdv, maxval=stdv, dtype=jnp.float32)
        return {'input': x, 'adj': adj, 'W': W, 'b': b}
    _L0_gnn_all = _L0_gnn_setup()
    _L0_gnn_in = {k: v for k, v in _L0_gnn_all.items() if k in ('W', 'b', )}
    del _L0_gnn_all

    def _L1_gnn_setup():
        import jax, jax.numpy as jnp
        import numpy as np
        N, IN_F, OUT_F, H = (8192, 256, 64, 4)
        NEG_SLOPE = 0.2
        key = jax.random.key(seed)
        ks = jax.random.split(key, 8)
        inputs = jax.random.normal(ks[0], (N, IN_F), dtype=jnp.float32)
        adj = (jax.random.uniform(ks[1], (N, N)) < 0.05).astype(jnp.float32)
        idx = jnp.arange(N)
        adj = adj.at[idx, idx].set(1.0)
        stdv = 1.0 / np.sqrt(H * OUT_F)
        weight = jax.random.uniform(ks[2], (IN_F, H * OUT_F), minval=-stdv, maxval=stdv, dtype=jnp.float32)
        bias = jax.random.uniform(ks[3], (1, H * OUT_F), minval=-stdv, maxval=stdv, dtype=jnp.float32)
        weight_u = jax.random.uniform(ks[4], (H, OUT_F, 1), minval=-1.0, maxval=1.0, dtype=jnp.float32)
        weight_v = jax.random.uniform(ks[5], (H, OUT_F, 1), minval=-1.0, maxval=1.0, dtype=jnp.float32)
        stdp = 1.0 / np.sqrt(IN_F)
        proj_w = jax.random.uniform(ks[6], (H * OUT_F, IN_F), minval=-stdp, maxval=stdp, dtype=jnp.float32)
        proj_b = jax.random.uniform(ks[7], (H * OUT_F,), minval=-stdp, maxval=stdp, dtype=jnp.float32)
        return {'inputs': inputs, 'adj_mat': adj, 'weight': weight, 'weight_u': weight_u, 'weight_v': weight_v, 'bias': bias, 'proj_w': proj_w, 'proj_b': proj_b}
    _L1_gnn_all = _L1_gnn_setup()
    _L1_gnn_in = {k: v for k, v in _L1_gnn_all.items() if k in ('weight', 'weight_u', 'weight_v', 'bias', 'proj_w', 'proj_b', )}
    del _L1_gnn_all

    def _L2_gnn_setup():
        import jax, jax.numpy as jnp
        import numpy as np
        N, H, HEADS = (4096, 256, 3)
        ALPHA = 0.2
        NEG_INF = -9000000000000000.0

        def _sign_adj(key, n, density):
            k1, k2 = jax.random.split(key)
            mask = jax.random.uniform(k1, (n, n)) < density
            sign = jnp.where(jax.random.uniform(k2, (n, n)) < 0.5, -1.0, 1.0)
            adj = jnp.where(mask, sign, 0.0).astype(jnp.float32)
            idx = jnp.arange(n)
            return adj.at[idx, idx].set(1.0)

        def _gru_cell(x, hstate, Wih, Whh, bih, bhh):
            gi = x @ Wih.T + bih
            gh = hstate @ Whh.T + bhh
            ir, iz, inn = jnp.split(gi, 3, axis=1)
            hr, hz, hn = jnp.split(gh, 3, axis=1)
            r = jax.nn.sigmoid(ir + hr)
            z = jax.nn.sigmoid(iz + hz)
            n = jnp.tanh(inn + r * hn)
            return (1.0 - z) * n + z * hstate

        def _gat_head(h, node_adj, edge_adj, W, a):
            hW = h @ W
            hp = (node_adj > 0).astype(hW.dtype) @ hW
            hm = (node_adj < 0).astype(hW.dtype) @ hW
            e_plus = jax.nn.leaky_relu(jnp.concatenate([hp, hm], axis=1) @ a, ALPHA)[:, 0]
            e_minus = jax.nn.leaky_relu(jnp.concatenate([hm, hp], axis=1) @ a, ALPHA)[:, 0]
            att = jnp.where(edge_adj > 0, e_plus[None, :], NEG_INF)
            att = jnp.where(edge_adj < 0, e_minus[None, :], att)
            att = jax.nn.softmax(att, axis=1)
            return att * edge_adj @ hW
        key = jax.random.key(seed)
        ks = jax.random.split(key, 16)
        std = 0.01
        gain = 1.414
        return {'h': jax.random.normal(ks[0], (N, H), jnp.float32), 'node_adj': _sign_adj(ks[1], N, 0.005), 'edge_adj': _sign_adj(ks[2], N, 0.005), 'gat_W': jax.random.normal(ks[3], (HEADS, H, H), jnp.float32) * (gain / np.sqrt(H, dtype=np.float32)), 'gat_a': jax.random.normal(ks[4], (HEADS, 2 * H, 1), jnp.float32) * 0.1, 'edge_Wih': jax.random.normal(ks[5], (3 * H, H), jnp.float32) * std, 'edge_Whh': jax.random.normal(ks[6], (3 * H, H), jnp.float32) * std, 'edge_bih': jnp.zeros((3 * H,), jnp.float32), 'edge_bhh': jnp.zeros((3 * H,), jnp.float32), 'node_Wih': jax.random.normal(ks[7], (3 * H, H), jnp.float32) * std, 'node_Whh': jax.random.normal(ks[8], (3 * H, H), jnp.float32) * std, 'node_bih': jnp.zeros((3 * H,), jnp.float32), 'node_bhh': jnp.zeros((3 * H,), jnp.float32)}
    _L2_gnn_all = _L2_gnn_setup()
    _L2_gnn_in = {k: v for k, v in _L2_gnn_all.items() if k in ('gat_W', 'gat_a', 'edge_Wih', 'edge_Whh', 'edge_bih', 'edge_bhh', 'node_Wih', 'node_Whh', 'node_bih', 'node_bhh', )}
    del _L2_gnn_all

    def _L3_gnn_setup():
        import jax, jax.numpy as jnp
        import numpy as np
        N = 8192
        DIM = 256
        HEADS = 4
        HD = DIM // HEADS
        SCALE = HD ** (-0.5)
        key = jax.random.key(seed)
        ks = jax.random.split(key, 8)
        x = jax.random.normal(ks[0], (N, DIM), dtype=jnp.float32)
        adj_matrix = jax.random.uniform(ks[1], (N, N), dtype=jnp.float32)
        attn_mask = jax.random.randint(ks[2], (N, N), 0, 2, dtype=jnp.int32)
        Wqkv = jax.random.normal(ks[3], (DIM, 3 * DIM), dtype=jnp.float32) * DIM ** (-0.5)
        bqkv = jnp.zeros((3 * DIM,), dtype=jnp.float32)
        Wout = jax.random.normal(ks[4], (DIM, DIM), dtype=jnp.float32) * DIM ** (-0.5)
        bout = jnp.zeros((DIM,), dtype=jnp.float32)
        graph_bias = jax.random.normal(ks[5], (1, 1, 1), dtype=jnp.float32) * 0.1
        return {'x': x, 'adj_matrix': adj_matrix, 'attn_mask': attn_mask, 'Wqkv': Wqkv, 'bqkv': bqkv, 'Wout': Wout, 'bout': bout, 'graph_bias': graph_bias}
    _L3_gnn_all = _L3_gnn_setup()
    _L3_gnn_in = {k: v for k, v in _L3_gnn_all.items() if k in ('Wqkv', 'bqkv', 'Wout', 'bout', 'graph_bias', )}
    del _L3_gnn_all

    return {
        "x": x,
        "adj": adj,
        "L0_gnn_W": _L0_gnn_in["W"],
        "L0_gnn_b": _L0_gnn_in["b"],
        "L1_gnn_weight": _L1_gnn_in["weight"],
        "L1_gnn_weight_u": _L1_gnn_in["weight_u"],
        "L1_gnn_weight_v": _L1_gnn_in["weight_v"],
        "L1_gnn_bias": _L1_gnn_in["bias"],
        "L1_gnn_proj_w": _L1_gnn_in["proj_w"],
        "L1_gnn_proj_b": _L1_gnn_in["proj_b"],
        "L2_gnn_gat_W": _L2_gnn_in["gat_W"],
        "L2_gnn_gat_a": _L2_gnn_in["gat_a"],
        "L2_gnn_edge_Wih": _L2_gnn_in["edge_Wih"],
        "L2_gnn_edge_Whh": _L2_gnn_in["edge_Whh"],
        "L2_gnn_edge_bih": _L2_gnn_in["edge_bih"],
        "L2_gnn_edge_bhh": _L2_gnn_in["edge_bhh"],
        "L2_gnn_node_Wih": _L2_gnn_in["node_Wih"],
        "L2_gnn_node_Whh": _L2_gnn_in["node_Whh"],
        "L2_gnn_node_bih": _L2_gnn_in["node_bih"],
        "L2_gnn_node_bhh": _L2_gnn_in["node_bhh"],
        "L3_gnn_Wqkv": _L3_gnn_in["Wqkv"],
        "L3_gnn_bqkv": _L3_gnn_in["bqkv"],
        "L3_gnn_Wout": _L3_gnn_in["Wout"],
        "L3_gnn_bout": _L3_gnn_in["bout"],
        "L3_gnn_graph_bias": _L3_gnn_in["graph_bias"],
    }

def reference(x, adj, L0_gnn_W, L0_gnn_b, L1_gnn_weight, L1_gnn_weight_u, L1_gnn_weight_v, L1_gnn_bias, L1_gnn_proj_w, L1_gnn_proj_b, L2_gnn_gat_W, L2_gnn_gat_a, L2_gnn_edge_Wih, L2_gnn_edge_Whh, L2_gnn_edge_bih, L2_gnn_edge_bhh, L2_gnn_node_Wih, L2_gnn_node_Whh, L2_gnn_node_bih, L2_gnn_node_bhh, L3_gnn_Wqkv, L3_gnn_bqkv, L3_gnn_Wout, L3_gnn_bout, L3_gnn_graph_bias):
    import jax
    import jax.numpy as jnp
    def _L0_gnn_ref(input, adj, W, b):
        import jax, jax.numpy as jnp
        import numpy as np
        import math
        N = 8192
        FIN = 256
        FOUT = 256
        A = adj + jnp.eye(adj.shape[0], dtype=adj.dtype)
        D = 1.0 / jnp.sqrt(jnp.sum(A, axis=1))
        A = A * D[:, None] * D[None, :]
        support = input @ W
        out = A @ support
        return jax.nn.relu(out + b)

    def _L1_gnn_ref(inputs, adj_mat, weight, weight_u, weight_v, bias, proj_w, proj_b):
        import jax, jax.numpy as jnp
        import numpy as np
        N, IN_F, OUT_F, H = (8192, 256, 64, 4)
        NEG_SLOPE = 0.2
        n = inputs.shape[0]
        support = (inputs @ weight).reshape(n, H, OUT_F).transpose(1, 0, 2)
        f1 = jnp.einsum('hno,ho->hn', support, weight_u[..., 0])
        f2 = jnp.einsum('hno,ho->hn', support, weight_v[..., 0])
        logits = f1[:, None, :] + f2[:, :, None]
        w = jax.nn.leaky_relu(logits, NEG_SLOPE)
        masked = w * adj_mat
        mask = adj_mat != 0.0
        neg = jnp.where(mask, masked, -jnp.inf)
        m = jnp.max(neg, axis=2, keepdims=True)
        m = jnp.where(jnp.isfinite(m), m, 0.0)
        e = jnp.where(mask, jnp.exp(neg - m), 0.0)
        denom = jnp.sum(e, axis=2, keepdims=True)
        attn = e / jnp.where(denom > 0, denom, 1.0)
        out = jnp.einsum('hnm,hmo->hno', attn, support)
        out = out.transpose(1, 0, 2).reshape(n, H * OUT_F)
        out = out + bias
        out = out + inputs @ proj_w.T + proj_b
        return out

    def _L2_gnn_ref(h, node_adj, edge_adj, gat_W, gat_a, edge_Wih, edge_Whh, edge_bih, edge_bhh, node_Wih, node_Whh, node_bih, node_bhh):
        import jax, jax.numpy as jnp
        import numpy as np
        N, H, HEADS = (4096, 256, 3)
        ALPHA = 0.2
        NEG_INF = -9000000000000000.0

        def _sign_adj(key, n, density):
            k1, k2 = jax.random.split(key)
            mask = jax.random.uniform(k1, (n, n)) < density
            sign = jnp.where(jax.random.uniform(k2, (n, n)) < 0.5, -1.0, 1.0)
            adj = jnp.where(mask, sign, 0.0).astype(jnp.float32)
            idx = jnp.arange(n)
            return adj.at[idx, idx].set(1.0)

        def _gru_cell(x, hstate, Wih, Whh, bih, bhh):
            gi = x @ Wih.T + bih
            gh = hstate @ Whh.T + bhh
            ir, iz, inn = jnp.split(gi, 3, axis=1)
            hr, hz, hn = jnp.split(gh, 3, axis=1)
            r = jax.nn.sigmoid(ir + hr)
            z = jax.nn.sigmoid(iz + hz)
            n = jnp.tanh(inn + r * hn)
            return (1.0 - z) * n + z * hstate

        def _gat_head(h, node_adj, edge_adj, W, a):
            hW = h @ W
            hp = (node_adj > 0).astype(hW.dtype) @ hW
            hm = (node_adj < 0).astype(hW.dtype) @ hW
            e_plus = jax.nn.leaky_relu(jnp.concatenate([hp, hm], axis=1) @ a, ALPHA)[:, 0]
            e_minus = jax.nn.leaky_relu(jnp.concatenate([hm, hp], axis=1) @ a, ALPHA)[:, 0]
            att = jnp.where(edge_adj > 0, e_plus[None, :], NEG_INF)
            att = jnp.where(edge_adj < 0, e_minus[None, :], att)
            att = jax.nn.softmax(att, axis=1)
            return att * edge_adj @ hW
        dn = jnp.diag(node_adj)
        de = jnp.diag(edge_adj)
        idx = jnp.arange(node_adj.shape[0])
        node_adj_norm = node_adj.at[idx, idx].add(-dn)
        edge_adj_norm = edge_adj.at[idx, idx].add(-de)
        node_support = node_adj_norm @ h
        edge_output = _gru_cell(node_support, h, edge_Wih, edge_Whh, edge_bih, edge_bhh)
        edge_support = _gat_head(h, node_adj_norm, edge_adj_norm, gat_W[0], gat_a[0])
        for i in range(1, HEADS):
            edge_support = edge_support + _gat_head(h, node_adj_norm, edge_adj_norm, gat_W[i], gat_a[i])
        edge_support = edge_support / HEADS
        node_output = _gru_cell(edge_support, h, node_Wih, node_Whh, node_bih, node_bhh)
        return de[:, None] * edge_output + dn[:, None] * node_output

    def _L3_gnn_ref(x, adj_matrix, attn_mask, Wqkv, bqkv, Wout, bout, graph_bias):
        import jax, jax.numpy as jnp
        import numpy as np
        N = 8192
        DIM = 256
        HEADS = 4
        HD = DIM // HEADS
        SCALE = HD ** (-0.5)
        n, d = x.shape
        qkv = x @ Wqkv + bqkv
        q, k, v = jnp.split(qkv, 3, axis=-1)

        def split_heads(t):
            return t.reshape(n, HEADS, HD).transpose(1, 0, 2)
        qh, kh, vh = (split_heads(q), split_heads(k), split_heads(v))
        scores = jnp.einsum('hnd,hmd->hnm', qh, kh) * SCALE
        scores = scores + graph_bias * adj_matrix[None, :, :]
        scores = jnp.where(attn_mask[None, :, :] == 0, jnp.float32(-1000000000.0), scores)
        attn = jax.nn.softmax(scores, axis=-1)
        out = jnp.einsum('hnm,hmd->hnd', attn, vh)
        out = out.transpose(1, 0, 2).reshape(n, d)
        return out @ Wout + bout

    h = jnp.maximum(_layernorm(x, axis=-1), 0.0)
    x = x + _L0_gnn_ref(h, adj, L0_gnn_W, L0_gnn_b)
    h = jnp.maximum(_layernorm(x, axis=-1), 0.0)
    x = x + _L1_gnn_ref(h, adj, L1_gnn_weight, L1_gnn_weight_u, L1_gnn_weight_v, L1_gnn_bias, L1_gnn_proj_w, L1_gnn_proj_b)
    h = jnp.maximum(_layernorm(x, axis=-1), 0.0)
    x = x + _L2_gnn_ref(h, adj, adj, L2_gnn_gat_W, L2_gnn_gat_a, L2_gnn_edge_Wih, L2_gnn_edge_Whh, L2_gnn_edge_bih, L2_gnn_edge_bhh, L2_gnn_node_Wih, L2_gnn_node_Whh, L2_gnn_node_bih, L2_gnn_node_bhh)
    h = jnp.maximum(_layernorm(x, axis=-1), 0.0)
    x = x + _L3_gnn_ref(h, adj, adj, L3_gnn_Wqkv, L3_gnn_bqkv, L3_gnn_Wout, L3_gnn_bout, L3_gnn_graph_bias)
    return x


_drawn_inputs = setup_inputs


def setup_inputs(seed=0):
    import zlib

    import numpy as np

    out = dict(_drawn_inputs(seed))
    spreads = {'L2_gnn_edge_bih': (0.0, 0.469),
     'L2_gnn_edge_bhh': (0.0, 0.661),
     'L2_gnn_node_bih': (0.0, 0.384),
     'L2_gnn_node_bhh': (0.0, 0.605),
     'L3_gnn_bqkv': (0.0, 0.1),
     'L3_gnn_bout': (0.0, 0.1)}
    factors = {'L2_gnn_gat_W': 5.823,
     'L2_gnn_gat_a': 8.0,
     'L2_gnn_edge_Whh': 4.625,
     'L2_gnn_node_Wih': 6.338,
     'L2_gnn_node_Whh': 4.399}
    for name, (base, spread) in spreads.items():
        noise = np.random.default_rng([zlib.crc32(name.encode()), seed]).standard_normal(out[name].shape)
        drawn = base * np.exp(spread * noise) if base else spread * noise
        out[name] = jnp.asarray(drawn.astype(out[name].dtype))
    for name, factor in factors.items():
        out[name] = (out[name] * factor).astype(out[name].dtype)
    return out
```

```python
from contextlib import ExitStack

import concourse.bass as bass
from concourse import mybir

F32 = mybir.dt.float32
BF16 = mybir.dt.bfloat16
ALU = mybir.AluOpType
ACT = mybir.ActivationFunctionType
AX = mybir.AxisListType

P = 128
N = 2708
NT = (N + P - 1) // P
NP = NT * P
TAIL = N - (NT - 1) * P
D = 256
C = D // P
EPS = 1e-5


def rows_of(m):
    return P if m < NT - 1 else TAIL


def over_tiles(eng, body):
    body(0, 0)
    body(1, 1)
    with eng.Fori(1, NT // 2 - 1) as i:
        body(i * 2, 0)
        body(i * 2 + 1, 1)
    body(NT - 2, 0)
    body(NT - 1, 1)


def wait_reuse(eng, sem, t, per=1, depth=2):
    if isinstance(t, int):
        if t >= depth:
            eng.wait_ge(sem, (t - depth + 1) * per)
    else:
        eng.wait_ge(sem, t * per + (1 - depth) * per)


def at_tile(t, width=1):
    return bass.ds(t * width, width)


class Phase:

    def __init__(self, nc, name):
        self.nc, self.name, self.ctx, self.sems = nc, name, ExitStack(), []

    def __enter__(self):
        return self

    def __exit__(self, *a):
        said = self.ctx.__exit__(*a)
        if self.sems and a[0] is None:
            self.nc.clear_and_free_semaphores(self.sems)
            self.nc.all_engine_barrier()
        return said

    def sb(self, name, shape, dt=F32):
        return self.ctx.enter_context(self.nc.sbuf_tensor(f"{self.name}_{name}", shape, dt))

    def ps(self, name, shape, dt=F32):
        return self.ctx.enter_context(self.nc.psum_tensor(f"{self.name}_{name}", shape, dt))

    def sem(self, name):
        self.sems.append(self.nc.alloc_semaphore(f"{self.name}_{name}"))
        return self.sems[-1]

    def block(self):
        return self.ctx.enter_context(self.nc.Block())


def load_constants(nc, k, ins):
    with Phase(nc, "const") as ph:
        zero_done, ident_done, x_in = ph.sem("zero_done"), ph.sem("ident_done"), ph.sem("x_in")
        block = ph.block()

        @block.gpsimd
        def _(pool):
            nc.gpsimd.memset(k.ident[:, :], 0.0).then_inc(zero_done, 1)
            nc.gpsimd.memset(k.offdiag[:, :], 1.0).then_inc(zero_done, 1)
            nc.gpsimd.memset(k.ones[:, :], 1.0)
            nc.gpsimd.memset(k.eps[:, :], EPS)
            pool.wait_ge(zero_done, 2)
            nc.gpsimd.affine_select(out=k.ident[:, :], in_=k.ident[:, :], compare_op=ALU.not_equal,
                                    fill=1.0, base=0, pattern=[[-1, P]], channel_multiplier=1)
            nc.gpsimd.affine_select(out=k.offdiag[:, :], in_=k.offdiag[:, :],
                                    compare_op=ALU.not_equal, fill=0.0, base=0,
                                    pattern=[[-1, P]], channel_multiplier=1)

        @block.sync
        def _(sp):
            sp.dma_start(k.x[:, :, :], ins["x"]).then_inc(x_in, 16)
            sp.dma_start(k.diag[:, :], ins["diag"]).then_inc(x_in, 16)
            sp.wait_ge(x_in, 32)


def degrees(nc, k, ins):
    with Phase(nc, "deg") as ph:
        a = ph.sb("a_rows", [P, 4, N])
        deg = ph.sb("deg", [P, NT])
        root = ph.sb("root", [P, NT])
        row_in = [ph.sem(f"row_in{j}") for j in range(4)]
        act_sum, dve_sum = ph.sem("act_sum"), ph.sem("dve_sum")
        rooted = ph.sem("rooted")
        block = ph.block()

        @block.sync
        def _(sp):
            for t in range(NT):
                if t >= 4:
                    sp.wait_ge(act_sum if t % 2 == 0 else dve_sum, t // 2 - 1)
                sp.dma_start(a[:, t % 4, :], ins["a_rows"][t]).then_inc(row_in[t % 4], 16)

        @block.scalar
        def _(act):
            for t in range(0, NT, 2):
                act.wait_ge(row_in[t % 4], 16 * (t // 4 + 1))
                nc.scalar.activation(a[:, t % 4, :], a[:, t % 4, :], ACT.Copy,
                                     accum_out=deg[:, t:t + 1]).then_inc(act_sum, 1)
            act.wait_ge(act_sum, NT // 2)
            act.wait_ge(dve_sum, NT // 2)
            nc.scalar.activation(root[:, :], deg[:, :], ACT.Sqrt, bias=k.ones[:, 0:1]).then_inc(rooted, 1)

        @block.vector
        def _(dve):
            for t in range(1, NT, 2):
                dve.wait_ge(row_in[t % 4], 16 * (t // 4 + 1))
                nc.vector.reduce_sum(deg[:, t:t + 1], a[:, t % 4, :], AX.X).then_inc(dve_sum, 1)
            dve.wait_ge(rooted, 1)
            nc.vector.reciprocal(k.dis[:, :], root[:, :])


def norm_stats(nc, k, layer):
    with Phase(nc, f"norm{layer}") as ph:
        st = ph.sb("bn", [P, NT, 6])
        mv = ph.sb("mv", [P, NT, 2])
        root = ph.sb("sd", [P, NT])
        st_done, mv_done = ph.sem("st_done"), ph.sem("mv_done")
        rooted, rstd_done = ph.sem("sd_done"), ph.sem("rstd_done")
        block = ph.block()

        @block.vector
        def _(dve):
            for t in range(NT):
                nc.vector.bn_stats(st[:, t, :], k.x[:, t, :]).then_inc(st_done, 1)
            for t in range(NT):
                dve.wait_ge(st_done, t + 1)
                nc.vector.bn_aggr(mv[:, t, :], st[:, t, :]).then_inc(mv_done, 1)
            dve.wait_ge(rooted, 1)
            nc.vector.reciprocal(k.rstd[:, :], root[:, :]).then_inc(rstd_done, 1)
            dve.wait_ge(rstd_done, 1)
            nc.vector.scalar_tensor_tensor(out=k.nmr[:, :], in0=mv[:, :, 0], scalar=-1.0,
                                           in1=k.rstd[:, :], op0=ALU.mult, op1=ALU.mult)

        @block.scalar
        def _(act):
            act.wait_ge(mv_done, NT)
            nc.scalar.activation(root[:, :], mv[:, :, 1], ACT.Sqrt, bias=k.eps[:, 0:1]).then_inc(rooted, 1)


def gcn(nc, k, ins):
    with Phase(nc, "gcn") as ph:
        s_all = ph.sb("support", [P, NT, D])
        w = ph.sb("w", [P, C, D])
        b = ph.sb("b", [P, D])
        h = ph.sb("h", [P, 2, D])
        hT = ph.sb("hT", [P, 2, D])
        at = ph.sb("at", [P, 3, NP])
        u = ph.sb("u", [P, 2, D])
        ps_t = [ph.ps(f"ps_t{s}", [P, 512]) for s in range(2)]
        ps_o = [ph.ps(f"ps_o{s}", [P, 512]) for s in range(2)]
        ps_a = [ph.ps(f"ps_a{s}", [P, 512]) for s in range(2)]
        w_in, h_done, turned, hT_done, mul_done, s_done = (
            ph.sem(n) for n in ("w_in", "h_done", "turned", "hT_done", "mul_done", "s_done"))
        at_in = [ph.sem(f"at_in{s}") for s in range(2)]
        agg, own, biased, relued, x_done = (ph.sem(n) for n in ("agg", "own", "biased", "relued", "x_done"))
        block = ph.block()

        @block.sync
        def _(sp):
            sp.dma_start(w[:, :, :], ins["w0"]).then_inc(w_in, 16)
            sp.dma_start(b[:, :], ins["b0"]).then_inc(w_in, 16)

            def body(t, s):
                wait_reuse(sp, agg, t)
                sp.dma_start(at[:, s, :], ins["at"][at_tile(t), :, :]).then_inc(at_in[s], 16)
            over_tiles(sp, body)

        @block.scalar
        def _(act):
            def normed(t, s):
                wait_reuse(act, turned, t)
                nc.scalar.activation(h[:, s, :], k.x[:, at_tile(t), :], ACT.Relu,
                                     bias=k.nmr[:, at_tile(t)], scale=k.rstd[:, at_tile(t)]).then_inc(h_done, 1)
            over_tiles(act, normed)

            def out(t, s):
                act.wait_ge(biased, t + 1)
                nc.scalar.activation(u[:, s, :], u[:, s, :], ACT.Relu).then_inc(relued, 1)
            over_tiles(act, out)

        @block.tensor
        def _(pe):
            def turn(t, s):
                pe.wait_ge(h_done, t + 1)
                wait_reuse(pe, hT_done, t)
                for c in range(C):
                    mm = nc.tensor.transpose(ps_t[s][:, c * P:(c + 1) * P], h[:, s, c * P:(c + 1) * P], k.ident[:, :])
                mm.then_inc(turned, 1)

            def body(t, s):
                if not (isinstance(t, int) and t == NT - 1):
                    turn(t + 1, 1 - s)
                pe.wait_ge(hT_done, t + 1)
                wait_reuse(pe, s_done, t)
                for c in range(C):
                    mm = nc.tensor.matmul(ps_o[s][:, 0:D], hT[:, s, c * P:(c + 1) * P], w[:, c, :],
                                          start=(c == 0), stop=(c == C - 1))
                mm.then_inc(mul_done, 1)
            pe.wait_ge(w_in, 32)
            turn(0, 0)
            over_tiles(pe, body)
            pe.wait_ge(s_done, NT)

            def aggregate(t, s):
                wait_in(pe, at_in[s], t, s)
                wait_reuse(pe, own, t)
                for m in range(NT):
                    mm = nc.tensor.matmul(ps_a[s][:, 0:D], at[0:rows_of(m), s, m * P:(m + 1) * P],
                                          s_all[0:rows_of(m), m, :], start=(m == 0), stop=(m == NT - 1))
                mm.then_inc(agg, 1)
            over_tiles(pe, aggregate)

        @block.vector
        def _(dve):
            def body(t, s):
                dve.wait_ge(turned, t + 1)
                wait_reuse(dve, mul_done, t)
                nc.vector.tensor_copy(hT[:, s, :], ps_t[s][:, 0:D]).then_inc(hT_done, 1)
                dve.wait_ge(mul_done, t + 1)
                nc.vector.tensor_scalar(s_all[:, at_tile(t), :], ps_o[s][:, 0:D], k.dis[:, at_tile(t)], None,
                                        ALU.mult).then_inc(s_done, 1)
            over_tiles(dve, body)
            dve.wait_ge(s_done, NT)

            def out(t, s):
                dve.wait_ge(agg, t + 1)
                wait_reuse(dve, x_done, t)
                nc.vector.tensor_tensor(u[:, s, :], ps_a[s][:, 0:D], s_all[:, at_tile(t), :], ALU.add).then_inc(own, 1)
                dve.wait_ge(own, t + 1)
                nc.vector.scalar_tensor_tensor(out=u[:, s, :], in0=u[:, s, :], scalar=k.dis[:, at_tile(t)],
                                               in1=b[:, :], op0=ALU.mult, op1=ALU.add).then_inc(biased, 1)
                dve.wait_ge(relued, t + 1)
                nc.vector.tensor_tensor(k.x[:, at_tile(t), :], k.x[:, at_tile(t), :], u[:, s, :],
                                        ALU.add).then_inc(x_done, 1)
            over_tiles(dve, out)


def wait_in(eng, sem, t, s):
    if isinstance(t, int):
        eng.wait_ge(sem, 16 * (t // 2 + 1))
    else:
        eng.wait_ge(sem, t * 8 + (16 - 8 * s))


BIG = 2.0 ** 126
SLOPE = 0.2
FLOOR = -(2.0 ** 125)
CHUNKS = ((0, 8), (8, 8), (16, 6))


def wait_count(eng, sem, t, per, off):
    if not isinstance(t, int) or per * t + off > 0:
        eng.wait_ge(sem, t * per + off)


def wait_apart(eng, sem, t, per, off):
    wait_count(eng, sem, t, per, off)
    if not isinstance(t, int):
        eng.nop(nofuse=True)


def last(t):
    return isinstance(t, int) and t == NT - 1


def diag_rows(nc, k, dve, pe, act, cols, count, dst, diag, ps, sems):
    diag_done, spread_done, rows_done = sems

    def on_dve():
        def body(t, s):
            wait_reuse(dve, spread_done, t)
            nc.vector.tensor_tensor(diag[:, s, :, :], k.ident[:, :].unsqueeze(1).to_broadcast([P, count, P]),
                                    cols(t).unsqueeze(2).to_broadcast([P, count, P]), ALU.mult).then_inc(diag_done, 1)
        over_tiles(dve, body)

    def on_pe():
        def body(t, s):
            pe.wait_ge(diag_done, t + 1)
            wait_reuse(pe, rows_done, t)
            nc.tensor.matmul(ps[s][:, 0:count * P], k.ones[:, :],
                             diag[:, s, :, :].rearrange("p c n -> p (c n)"), start=True, stop=True).then_inc(spread_done, 1)
        over_tiles(pe, body)

    def on_act():
        def body(t, s):
            act.wait_ge(spread_done, t + 1)
            nc.scalar.activation(dst[:, :, bass.ds(t * P, P)],
                                 ps[s][:, 0:count * P].rearrange("p (c n) -> p c n", c=count),
                                 ACT.Copy).then_inc(rows_done, 1)
        over_tiles(act, body)
    return on_dve, on_pe, on_act


def gat(nc, k, ins):
    H, O = 4, D // 4
    with Phase(nc, "gat") as keep:
        f1_rows = keep.sb("f1_rows", [P, H, NP])
        f12 = keep.sb("f12", [P, NT, 2 * H])
        v = keep.sb("v", [P, NT, D])
        gat_in(nc, k, ins, f1_rows, f12, v, H, O)
        gat_attend(nc, k, ins, f1_rows, f12, v, H, O)


def gat_in(nc, k, ins, f1_rows, f12, v, H, O):
    with Phase(nc, "gat_in") as ph:
        w = ph.sb("w", [P, C, D + 2 * H])
        w_prod = ph.sb("w_prod", [P, 2, C, D])
        pw = ph.sb("pw", [P, C, D])
        uv = ph.sb("uv", [P, 2, D])
        b = ph.sb("b", [P, 2, D])
        bias = ph.sb("bias", [P, D])
        h = ph.sb("h", [P, 2, D])
        hT = ph.sb("hT", [P, 2, D])
        diag = ph.sb("diag", [P, 2, H, P])
        ps_t = [ph.ps(f"ps_t{s}", [P, 512]) for s in range(2)]
        ps_v = [ph.ps(f"ps_v{s}", [P, 512]) for s in range(2)]
        ps_r = [ph.ps(f"ps_r{s}", [P, 512]) for s in range(2)]
        ps_f = [ph.ps(f"ps_f{s}", [P, 512]) for s in range(2)]
        w_in, uv_prod, uv_done, bias_done = (ph.sem(n) for n in ("w_in", "uv_prod", "uv_done", "bias_done"))
        h_done, turned, hT_done, mul_done = (ph.sem(n) for n in ("h_done", "turned", "hT_done", "mul_done"))
        v_done, f_done, x_done, xb_done = (ph.sem(n) for n in ("v_done", "f_done", "x_done", "xb_done"))
        sems = [ph.sem(n) for n in ("diag_done", "spread_done", "rows_done")]
        block = ph.block()

        @block.sync
        def _(sp):
            sp.dma_start(w[:, :, 0:D], ins["w1"]).then_inc(w_in, 16)
            sp.dma_start(pw[:, :, :], ins["pw1"]).then_inc(w_in, 16)
            sp.dma_start(uv[:, :, :], ins["uv1"]).then_inc(w_in, 16)
            sp.dma_start(b[:, :, :], ins["b1"]).then_inc(w_in, 16)

        @block.scalar
        def _(act):
            def normed(t, s):
                wait_reuse(act, turned, t)
                nc.scalar.activation(h[:, s, :], k.x[:, at_tile(t), :], ACT.Relu,
                                     bias=k.nmr[:, at_tile(t)], scale=k.rstd[:, at_tile(t)]).then_inc(h_done, 1)

            def body(t, s):
                if not last(t):
                    normed(t + 1, 1 - s)
                act.wait_ge(mul_done, t + 1)
                nc.scalar.activation(v[:, at_tile(t), :], ps_v[s][:, 0:D], ACT.Copy).then_inc(v_done, 1)
                nc.scalar.activation(f12[:, at_tile(t), :], ps_v[s][:, D:D + 2 * H], ACT.Copy).then_inc(f_done, 1)
            normed(0, 0)
            over_tiles(act, body)
            diag_rows(nc, k, None, None, act, None, H, f1_rows, diag, ps_f, sems)[2]()

        @block.tensor
        def _(pe):
            def turn(t, s):
                pe.wait_ge(h_done, t + 1)
                wait_reuse(pe, hT_done, t)
                for c in range(C):
                    mm = nc.tensor.transpose(ps_t[s][:, c * P:(c + 1) * P], h[:, s, c * P:(c + 1) * P], k.ident[:, :])
                mm.then_inc(turned, 1)

            def body(t, s):
                if not last(t):
                    turn(t + 1, 1 - s)
                pe.wait_ge(hT_done, t + 1)
                wait_reuse(pe, f_done, t)
                for c in range(C):
                    nc.tensor.matmul(ps_v[s][:, 0:D + 2 * H], hT[:, s, c * P:(c + 1) * P], w[:, c, :],
                                     start=(c == 0), stop=(c == C - 1))
                wait_reuse(pe, x_done, t)
                for c in range(C):
                    mm = nc.tensor.matmul(ps_r[s][:, 0:D], hT[:, s, c * P:(c + 1) * P], pw[:, c, :],
                                          start=(c == 0), stop=(c == C - 1))
                mm.then_inc(mul_done, 1)
            pe.wait_ge(w_in, 64)
            turn(0, 0)
            pe.wait_ge(uv_done, 2)
            over_tiles(pe, body)
            diag_rows(nc, k, None, pe, None, None, H, f1_rows, diag, ps_f, sems)[1]()

        @block.vector
        def _(dve):
            dve.wait_ge(w_in, 64)
            for j in range(2):
                nc.vector.tensor_tensor(w_prod[:, j, :, :], w[:, :, 0:D],
                                        uv[:, j, :].unsqueeze(1).to_broadcast([P, C, D]), ALU.mult).then_inc(uv_prod, 1)
            for j in range(2):
                dve.wait_ge(uv_prod, j + 1)
                nc.vector.reduce_sum(w[:, :, D + j * H:D + (j + 1) * H],
                                     w_prod[:, j, :, :].rearrange("p c (h o) -> p c h o", h=H), AX.X).then_inc(uv_done, 1)
            nc.vector.tensor_tensor(bias[:, :], b[:, 0, :], b[:, 1, :], ALU.add).then_inc(bias_done, 1)
            dve.wait_ge(bias_done, 1)

            def body(t, s):
                dve.wait_ge(turned, t + 1)
                wait_reuse(dve, mul_done, t)
                nc.vector.tensor_copy(hT[:, s, :], ps_t[s][:, 0:D]).then_inc(hT_done, 1)
                dve.wait_ge(mul_done, t + 1)
                nc.vector.tensor_tensor(k.x[:, at_tile(t), :], k.x[:, at_tile(t), :], ps_r[s][:, 0:D],
                                        ALU.add).then_inc(x_done, 1)
                dve.wait_ge(x_done, t + 1)
                nc.vector.tensor_tensor(k.x[:, at_tile(t), :], k.x[:, at_tile(t), :], bias[:, :],
                                        ALU.add).then_inc(xb_done, 1)
            over_tiles(dve, body)
            dve.wait_ge(f_done, NT)
            diag_rows(nc, k, dve, None, None, lambda t: f12[:, at_tile(t), 0:H].rearrange("p a h -> p (a h)"),
                      H, f1_rows, diag, ps_f, sems)[0]()


def gat_attend(nc, k, ins, f1_rows, f12, v, H, O):
    with Phase(nc, "gat_at") as ph:
        f2_low = ph.sb("f2_low", [P, NT, H])
        low_ready = ph.sem("low_ready")
        a = ph.sb("a", [P, 2, N])
        mask = ph.sb("mask", [P, 2, N], BF16)
        z = ph.sb("z", [P, H, NP])
        pT = ph.sb("pT", [P, 2, NP])
        row_max = ph.sb("row_max", [P, H])
        neg_max = ph.sb("neg_max", [P, H])
        den = ph.sb("den", [P, 2, H])
        den_safe = ph.sb("den_safe", [P, 2, H])
        inv = ph.sb("inv", [P, 2, H])
        o = ph.sb("o", [P, 2, H, O])
        ps_p = [ph.ps(f"ps_p{c}", [P, 1024]) for c in range(3)]
        ps_o = [ph.ps(f"ps_o{s}", [P, 512]) for s in range(2)]
        a_in = [ph.sem(f"a_in{s}") for s in range(2)]
        (mask_done, pad_done, low_done, leaky_done, mult_done, max_done, neg_done, p_done, turned, pT_done, pv_done,
         safe_done, inv_done, o_done, x_done) = (
            ph.sem(n) for n in ("mask_done", "pad_done", "low_done", "leaky_done", "mult_done", "max_done", "neg_done", "p_done",
                                "turned", "pT_done", "pv_done", "safe_done", "inv_done", "o_done", "x_done"))
        block = ph.block()

        def shifted(t, s, h, by):
            over, h = (h + by) // H, (h + by) % H
            if isinstance(t, int) and not 0 <= t + over < NT:
                return None
            return (t + over, (s + over) % 2, h) if over else (t, s, h)

        def do(stage, at):
            if at is not None:
                stage(*at)

        @block.sync
        def _(sp):
            def body(t, s):
                wait_reuse(sp, mask_done, t)
                wait_reuse(sp, mult_done, t, per=H)
                sp.dma_start(a[:, s, :], ins["a_rows"][at_tile(t), :, :]).then_inc(a_in[s], 16)
            over_tiles(sp, body)

        @block.gpsimd
        def _(pool):
            nc.gpsimd.memset(z[:, :, N:NP], 0.0).then_inc(pad_done, 1)

        @block.scalar
        def _(act):
            def low_branch(t, s, h):
                wait_count(act, turned, t, 3 * H, 3 * (h + 1 - H))
                nc.scalar.activation(z[:, h, 0:N], f1_rows[:, h, 0:N], ACT.Identity, scale=SLOPE,
                                     bias=f2_low[:, at_tile(t), h:h + 1].rearrange("p a h -> p (a h)")).then_inc(
                                         low_done, 1)

            def evacuate(t, s, h):
                wait_count(act, pv_done, t, H, h - 1)
                for c in range(3):
                    m0, n = CHUNKS[c]
                    wait_count(act, turned, t, 3 * H, 3 * h + c + 1)
                    nc.scalar.activation(pT[:, h % 2, m0 * P:(m0 + n) * P], ps_p[c][:, 0:n * P],
                                         ACT.Copy).then_inc(pT_done, 1)

            def body(t, s):
                for h in range(H):
                    do(low_branch, shifted(t, s, h, 2))
                    do(evacuate, shifted(t, s, h, -1))
                    wait_count(act, neg_done, t, H, h + 1)
                    nc.scalar.activation(z[:, h, 0:N], z[:, h, 0:N], ACT.Exp,
                                         bias=neg_max[:, h:h + 1],
                                         accum_out=den[:, s, h:h + 1]).then_inc(p_done, 1)
            act.wait_ge(low_ready, 1)
            low_branch(0, 0, 0)
            low_branch(0, 0, 1)
            over_tiles(act, body)
            evacuate(NT - 1, 1, H - 1)

        @block.tensor
        def _(pe):
            def values(t, s, h):
                wait_count(pe, pT_done, t, 3 * H, 3 * h + 3)
                if h == 0:
                    wait_reuse(pe, o_done, t)
                for m in range(NT):
                    mm = nc.tensor.matmul(ps_o[s][:, h * O:(h + 1) * O], pT[:, h % 2, m * P:(m + 1) * P],
                                          v[:, m, h * O:(h + 1) * O], start=(m == 0), stop=(m == NT - 1))
                mm.then_inc(pv_done, 1)

            def body(t, s):
                for h in range(H):
                    do(values, shifted(t, s, h, -1))
                    wait_count(pe, p_done, t, H, h + 1)
                    for c, (m0, n) in enumerate(CHUNKS):
                        for m in range(m0, m0 + n):
                            mm = nc.tensor.transpose(ps_p[c][:, (m - m0) * P:(m - m0 + 1) * P],
                                                     z[:, h, m * P:(m + 1) * P], k.ident[:, :])
                        mm.then_inc(turned, 1)
            pe.wait_ge(pad_done, 1)
            over_tiles(pe, body)
            values(NT - 1, 1, H - 1)

        @block.vector
        def _(dve):
            def make_mask(t, s):
                wait_in(dve, a_in[s], t, s)
                nc.vector.tensor_scalar(mask[:, s, :], a[:, s, :], 0.0, -BIG, ALU.is_equal,
                                        ALU.mult).then_inc(mask_done, 1)

            def logits(t, s, h):
                if h == 0:
                    make_mask(t, s)
                wait_count(dve, low_done, t, H, h + 1)
                nc.vector.scalar_tensor_tensor(out=z[:, h, 0:N], in0=f1_rows[:, h, 0:N],
                                               scalar=f12[:, at_tile(t), H + h:H + h + 1].rearrange("p a h -> p (a h)"),
                                               in1=z[:, h, 0:N], op0=ALU.add, op1=ALU.max).then_inc(leaky_done, 1)
                wait_count(dve, leaky_done, t, H, h + 1)
                nc.vector.tensor_tensor(z[:, h, 0:N], z[:, h, 0:N], a[:, s, :], ALU.mult).then_inc(mult_done, 1)
                if h == 0:
                    wait_count(dve, mask_done, t, 1, 1)
                wait_apart(dve, mult_done, t, H, h + 1)
                nc.vector.tensor_tensor_reduce(out=z[:, h, 0:N], in0=z[:, h, 0:N], in1=mask[:, s, :], scale=1.0,
                                               scalar=-2 * BIG, op0=ALU.add, op1=ALU.max,
                                               accum_out=row_max[:, h:h + 1]).then_inc(max_done, 1)
                wait_count(dve, max_done, t, H, h + 1)
                nc.vector.tensor_scalar(neg_max[:, h:h + 1], row_max[:, h:h + 1], FLOOR, -1.0, ALU.max,
                                        ALU.mult).then_inc(neg_done, 1)

            def finish(t, s):
                wait_count(dve, p_done, t, H, H)
                nc.vector.tensor_scalar(den_safe[:, s, :], den[:, s, :], 0.5, None, ALU.max).then_inc(safe_done, 1)
                dve.wait_ge(safe_done, t + 1)
                nc.vector.reciprocal(inv[:, s, :], den_safe[:, s, :]).then_inc(inv_done, 1)
                dve.wait_ge(inv_done, t + 1)
                wait_count(dve, pv_done, t, H, H)
                nc.vector.tensor_tensor(o[:, s, :, :], ps_o[s][:, 0:D].rearrange("p (h o) -> p h o", h=H),
                                        inv[:, s, :].unsqueeze(2).to_broadcast([P, H, O]), ALU.mult).then_inc(o_done, 1)
                dve.wait_ge(o_done, t + 1)
                nc.vector.tensor_tensor(k.x[:, at_tile(t), :], k.x[:, at_tile(t), :],
                                        o[:, s, :, :].rearrange("p h o -> p (h o)").unsqueeze(1), ALU.add).then_inc(x_done, 1)

            def body(t, s):
                for h in range(H):
                    do(logits, shifted(t, s, h, 1))
                    if h == 1 and not (isinstance(t, int) and t == 0):
                        finish(t - 1, 1 - s)
            nc.vector.tensor_scalar(f2_low[:, :, :], f12[:, :, H:2 * H], SLOPE, None, ALU.mult).then_inc(low_ready, 1)
            logits(0, 0, 0)
            over_tiles(dve, body)
            finish(NT - 1, 1)


HEADS = 3


class Gru:

    def __init__(self, nc, k, ph, ins, name, depth):
        self.nc, self.k, self.depth, self.ins, self.name = nc, k, depth, ins, name
        self.inp, self.hid = ph.sb("inp", [P, 2, D]), ph.sb("hid", [P, 2, D])
        self.wi, self.wh = ph.sb("wi", [P, C, 3 * D]), ph.sb("wh", [P, C, 3 * D])
        self.bi, self.bh = ph.sb("bi", [P, 3 * D]), ph.sb("bh", [P, 3 * D])
        self.b_rz = ph.sb("b_rz", [P, 2 * D])
        self.b_n = ph.sb("b_n", [P, 2 * D])
        self.kept = ph.sb("kept", [P, 2, 4 * P])
        self.rz, self.nn = ph.sb("rz", [P, 2, 2 * D]), ph.sb("nn", [P, 2, 2 * D])
        self.cell = ph.sb("cell", [P, 2, D])
        self.ps_t = [ph.ps(f"ps_gt{s}", [P, 512]) for s in range(depth)]
        self.ps_rz = [ph.ps(f"ps_rz{s}", [P, 512]) for s in range(depth)]
        self.ps_n = [ph.ps(f"ps_n{s}", [P, 512]) for s in range(depth)]
        self.w_in, self.inp_ready, self.hid_ready = ph.sem("gw_in"), ph.sem("inp_ready"), ph.sem("hid_ready")
        self.turned, self.kept_done, self.gates_done = ph.sem("g_turned"), ph.sem("kept_done"), ph.sem("gates_done")
        self.b_done, self.rz_done, self.n_done = ph.sem("b_done"), ph.sem("rz_done"), ph.sem("n_done")
        self.rz_tanh, self.gated, self.reset_done = ph.sem("rz_tanh"), ph.sem("gated"), ph.sem("reset_done")
        self.cand_done, self.cand_tanh = ph.sem("cand_done"), ph.sem("cand_tanh")
        self.diff_done, self.zdiff_done = ph.sem("diff_done"), ph.sem("zdiff_done")
        self.cell_done, self.x_done = ph.sem("cell_done"), ph.sem("gx_done")

    def load(self, sp):
        sp.dma_start(self.wi[:, :, :], self.ins[f"{self.name}_wih"]).then_inc(self.w_in, 16)
        sp.dma_start(self.wh[:, :, :], self.ins[f"{self.name}_whh"]).then_inc(self.w_in, 16)
        sp.dma_start(self.bi[:, :], self.ins[f"{self.name}_bih"]).then_inc(self.w_in, 16)
        sp.dma_start(self.bh[:, :], self.ins[f"{self.name}_bhh"]).then_inc(self.w_in, 16)

    def biases(self, dve):
        dve.wait_ge(self.w_in, 64)
        self.nc.vector.tensor_tensor(self.b_rz[:, :], self.bi[:, 0:2 * D], self.bh[:, 0:2 * D], ALU.add).then_inc(self.b_done, 1)
        self.nc.vector.tensor_copy(self.b_n[:, 0:D], self.bi[:, 2 * D:3 * D]).then_inc(self.b_done, 1)
        self.nc.vector.tensor_copy(self.b_n[:, D:2 * D], self.bh[:, 2 * D:3 * D]).then_inc(self.b_done, 1)
        dve.wait_ge(self.b_done, 3)

    def pe_turn(self, pe, t, s):
        pe.wait_ge(self.inp_ready, t + 1)
        pe.wait_ge(self.hid_ready, t + 1)
        wait_reuse(pe, self.kept_done, t, depth=self.depth)
        for c in range(4):
            src = (self.inp, self.hid)[c // 2]
            mm = self.nc.tensor.transpose(self.ps_t[s % self.depth][:, c * P:(c + 1) * P],
                                          src[:, s, (c % 2) * P:(c % 2 + 1) * P], self.k.ident[:, :])
        mm.then_inc(self.turned, 1)

    def act_keep(self, act, t, s):
        act.wait_ge(self.turned, t + 1)
        wait_reuse(act, self.gates_done, t)
        self.nc.scalar.activation(self.kept[:, s, :], self.ps_t[s % self.depth][:, :], ACT.Copy).then_inc(self.kept_done, 1)

    def pe_gates(self, pe, t, s):
        d = s % self.depth
        pe.wait_ge(self.kept_done, t + 1)
        wait_reuse(pe, self.rz_done, t, depth=self.depth)
        for c in range(4):
            w = (self.wi, self.wh)[c // 2]
            self.nc.tensor.matmul(self.ps_rz[d][:, :], self.kept[:, s, c * P:(c + 1) * P], w[:, c % 2, 0:2 * D],
                                  start=(c == 0), stop=(c == 3))
        wait_reuse(pe, self.n_done, t, depth=self.depth)
        for c in range(4):
            w = (self.wi, self.wh)[c // 2]
            mm = self.nc.tensor.matmul(self.ps_n[d][:, (c // 2) * D:(c // 2 + 1) * D],
                                       self.kept[:, s, c * P:(c + 1) * P], w[:, c % 2, 2 * D:3 * D],
                                       start=(c % 2 == 0), stop=(c % 2 == 1))
        mm.then_inc(self.gates_done, 1)

    def act_gates(self, act, t, s):
        act.wait_ge(self.rz_done, t + 1)
        self.nc.scalar.activation(self.rz[:, s, :], self.rz[:, s, :], ACT.Tanh, scale=0.5).then_inc(self.rz_tanh, 1)

    def act_candidate(self, act, t, s):
        act.wait_ge(self.cand_done, t + 1)
        self.nc.scalar.activation(self.nn[:, s, 0:D], self.nn[:, s, 0:D], ACT.Tanh).then_inc(self.cand_tanh, 1)

    def dve(self, dve, t, s):
        v, k, d = self.nc.vector, self.k, s % self.depth
        rz, nn, cell, h = self.rz[:, s, :], self.nn[:, s, :], self.cell[:, s, :], self.hid[:, s, :]
        dve.wait_ge(self.gates_done, t + 1)
        v.tensor_tensor(rz, self.ps_rz[d][:, :], self.b_rz[:, :], ALU.add).then_inc(self.rz_done, 1)
        v.tensor_tensor(nn, self.ps_n[d][:, :], self.b_n[:, :], ALU.add).then_inc(self.n_done, 1)
        dve.wait_ge(self.rz_tanh, t + 1)
        v.tensor_scalar(rz, rz, 0.5, 0.5, ALU.mult, ALU.add).then_inc(self.gated, 1)
        dve.wait_ge(self.n_done, t + 1)
        dve.wait_ge(self.gated, t + 1)
        v.tensor_tensor(cell, self.rz[:, s, 0:D], self.nn[:, s, D:2 * D], ALU.mult).then_inc(self.reset_done, 1)
        dve.wait_ge(self.reset_done, t + 1)
        v.tensor_tensor(self.nn[:, s, 0:D], self.nn[:, s, 0:D], cell, ALU.add).then_inc(self.cand_done, 1)
        dve.wait_ge(self.cand_tanh, t + 1)
        v.tensor_tensor(cell, h, self.nn[:, s, 0:D], ALU.subtract).then_inc(self.diff_done, 1)
        dve.wait_ge(self.diff_done, t + 1)
        v.tensor_tensor(cell, cell, self.rz[:, s, D:2 * D], ALU.mult).then_inc(self.zdiff_done, 1)
        dve.wait_ge(self.zdiff_done, t + 1)
        v.tensor_tensor(cell, cell, self.nn[:, s, 0:D], ALU.add).then_inc(self.cell_done, 1)
        dve.wait_ge(self.cell_done, t + 1)
        v.scalar_tensor_tensor(out=k.x[:, at_tile(t), :], in0=cell.unsqueeze(1), scalar=k.diag[:, at_tile(t)],
                               in1=k.x[:, at_tile(t), :], op0=ALU.mult, op1=ALU.add).then_inc(self.x_done, 1)


def signed_gat(nc, k, ins):
    with Phase(nc, "sg") as keep:
        h = keep.sb("h", [P, NT, D])
        e = keep.sb("e", [P, NT, 2, HEADS])
        with Phase(nc, "sg_u") as keep_u:
            u3 = keep_u.sb("u3", [P, NT, 2 * HEADS, 3], BF16)
            signed_in(nc, k, ins, h, u3)
            signed_support(nc, k, ins, h, u3, e)
        es = keep.sb("es", [P, NT, D])
        for i in range(HEADS):
            signed_head(nc, k, ins, i, h, e, es)
        signed_node(nc, k, ins, h, es)


def signed_in(nc, k, ins, h, u3):
    J = 2 * HEADS
    with Phase(nc, "sg_in") as ph:
        w = ph.sb("w", [P, HEADS, C, D])
        av = ph.sb("av", [P, HEADS, 2, D])
        prod = ph.sb("prod", [P, J, C, D])
        wa = ph.sb("wa", [P, C, J])
        hs = ph.sb("hs", [P, 2, D])
        hT = ph.sb("hT", [P, 2, D])
        u = ph.sb("u", [P, NT, J])
        rest = ph.sb("rest", [P, 2, NT, J])
        ps_t = [ph.ps(f"ps_t{s}", [P, 512]) for s in range(2)]
        ps_u = [ph.ps(f"ps_u{s}", [P, 512]) for s in range(2)]
        w_in, prod_done, wa_done, h_done, turned = (ph.sem(n) for n in ("w_in", "prod_done", "wa_done", "h_done", "turned"))
        hT_done, mul_done, u_done, kept, split = (ph.sem(n) for n in ("hT_done", "mul_done", "u_done", "kept", "split"))
        block = ph.block()

        @block.sync
        def _(sp):
            sp.dma_start(w[:, :, :, :], ins["w2"]).then_inc(w_in, 16)
            sp.dma_start(av[:, :, :, :], ins["a2"]).then_inc(w_in, 16)

        @block.scalar
        def _(act):
            def normed(t, s):
                wait_reuse(act, turned, t)
                wait_reuse(act, kept, t)
                nc.scalar.activation(hs[:, s, :], k.x[:, at_tile(t), :], ACT.Relu,
                                     bias=k.nmr[:, at_tile(t)], scale=k.rstd[:, at_tile(t)]).then_inc(h_done, 1)
            over_tiles(act, normed)

        @block.tensor
        def _(pe):
            def turn(t, s):
                pe.wait_ge(h_done, t + 1)
                wait_reuse(pe, hT_done, t)
                for c in range(C):
                    mm = nc.tensor.transpose(ps_t[s][:, c * P:(c + 1) * P], hs[:, s, c * P:(c + 1) * P], k.ident[:, :])
                mm.then_inc(turned, 1)

            def body(t, s):
                if not last(t):
                    turn(t + 1, 1 - s)
                pe.wait_ge(hT_done, t + 1)
                wait_reuse(pe, u_done, t)
                for c in range(C):
                    mm = nc.tensor.matmul(ps_u[s][:, 0:J], hT[:, s, c * P:(c + 1) * P], wa[:, c, :],
                                          start=(c == 0), stop=(c == C - 1))
                mm.then_inc(mul_done, 1)
            turn(0, 0)
            pe.wait_ge(wa_done, J)
            over_tiles(pe, body)

        @block.vector
        def _(dve):
            dve.wait_ge(w_in, 32)
            for j in range(J):
                nc.vector.tensor_tensor(prod[:, j, :, :], w[:, j // 2, :, :],
                                        av[:, j // 2, j % 2, :].unsqueeze(1).to_broadcast([P, C, D]),
                                        ALU.mult).then_inc(prod_done, 1)
            for j in range(J):
                dve.wait_ge(prod_done, j + 1)
                nc.vector.reduce_sum(wa[:, :, j], prod[:, j, :, :], AX.X).then_inc(wa_done, 1)

            def body(t, s):
                dve.wait_ge(turned, t + 1)
                wait_reuse(dve, mul_done, t)
                nc.vector.tensor_copy(hT[:, s, :], ps_t[s][:, 0:D]).then_inc(hT_done, 1)
                nc.vector.tensor_copy(h[:, at_tile(t), :], hs[:, s, :].unsqueeze(1)).then_inc(kept, 1)
                dve.wait_ge(mul_done, t + 1)
                nc.vector.tensor_copy(u[:, at_tile(t), :], ps_u[s][:, 0:J].unsqueeze(1)).then_inc(u_done, 1)
            over_tiles(dve, body)
            dve.wait_ge(u_done, NT)
            nc.vector.tensor_copy(u3[:, :, :, 0], u[:, :, :]).then_inc(split, 1)
            dve.wait_ge(split, 1)
            nc.vector.tensor_tensor(rest[:, 0, :, :], u[:, :, :], u3[:, :, :, 0], ALU.subtract).then_inc(split, 1)
            dve.wait_ge(split, 2)
            nc.vector.tensor_copy(u3[:, :, :, 1], rest[:, 0, :, :]).then_inc(split, 1)
            dve.wait_ge(split, 3)
            nc.vector.tensor_tensor(rest[:, 1, :, :], rest[:, 0, :, :], u3[:, :, :, 1], ALU.subtract).then_inc(split, 1)
            dve.wait_ge(split, 4)
            nc.vector.tensor_copy(u3[:, :, :, 2], rest[:, 1, :, :])


def signed_support(nc, k, ins, h, u3, e):
    J = 2 * HEADS
    with Phase(nc, "sg_sup") as ph:
        at = ph.sb("at", [P, 2, NT, P])
        sign = ph.sb("sign", [P, 2, 2, NT, P], BF16)
        sums = ph.sb("sums", [P, 2, 2, J])
        pre = ph.sb("pre", [P, 2, 2, HEADS])
        ps_a = [ph.ps(f"ps_a{s}", [P, 512]) for s in range(2)]
        ps_e = [ph.ps(f"ps_e{s}", [P, 512]) for s in range(2)]
        gru = Gru(nc, k, ph, ins, "edge", depth=1)
        at_in = [ph.sem(f"at_in{s}") for s in range(2)]
        cut, pos_done, neg_done, agg, e_mul = (ph.sem(n) for n in ("cut", "pos_done", "neg_done", "agg", "e_mul"))
        sum_done, plus_done, minus_done, e_done = (ph.sem(n) for n in ("sum_done", "plus_done", "minus_done", "e_done"))
        block = ph.block()

        @block.sync
        def _(sp):
            gru.load(sp)

            def body(t, s):
                wait_reuse(sp, agg, t)
                wait_reuse(sp, neg_done, t)
                sp.dma_start(at[:, s, :, :].rearrange("p m n -> p (m n)"), ins["at"][at_tile(t), :, :]).then_inc(at_in[s], 16)
            over_tiles(sp, body)

        @block.gpsimd
        def _(pool):
            def body(t, s):
                wait_reuse(pool, gru.x_done, t)
                nc.gpsimd.tensor_copy(gru.hid[:, s, :].unsqueeze(1), h[:, at_tile(t), :]).then_inc(gru.hid_ready, 1)
            over_tiles(pool, body)

        @block.tensor
        def _(pe):
            def body(t, s):
                pe.wait_ge(cut, t + 1)
                wait_reuse(pe, gru.inp_ready, t)
                for m in range(NT):
                    mm = nc.tensor.matmul(ps_a[s][:, 0:D], at[0:rows_of(m), s, m, :], h[0:rows_of(m), m, :],
                                          start=(m == 0), stop=(m == NT - 1))
                mm.then_inc(agg, 1)
                pe.wait_ge(pos_done, t + 1)
                pe.wait_ge(neg_done, t + 1)
                wait_reuse(pe, sum_done, t)
                for g in range(2):
                    for m in range(NT):
                        mm = nc.tensor.matmul(ps_e[s][:, g * 3 * J:(g + 1) * 3 * J], sign[0:rows_of(m), s, g, m, :],
                                              u3[0:rows_of(m), m, :, :].rearrange("p j c -> p (j c)"),
                                              start=(m == 0), stop=(m == NT - 1))
                mm.then_inc(e_mul, 1)
                if not (isinstance(t, int) and t == 0):
                    gru.pe_gates(pe, t - 1, 1 - s)
                gru.pe_turn(pe, t, s)
            pe.wait_ge(gru.w_in, 64)
            over_tiles(pe, body)
            gru.pe_gates(pe, NT - 1, 1)

        @block.scalar
        def _(act):
            def body(t, s):
                act.wait_ge(agg, t + 1)
                wait_reuse(act, gru.turned, t)
                nc.scalar.activation(gru.inp[:, s, :], ps_a[s][:, 0:D], ACT.Copy).then_inc(gru.inp_ready, 1)
                if not (isinstance(t, int) and t == 0):
                    gru.act_gates(act, t - 1, 1 - s)
                    gru.act_candidate(act, t - 1, 1 - s)
                gru.act_keep(act, t, s)
            over_tiles(act, body)
            gru.act_gates(act, NT - 1, 1)
            gru.act_candidate(act, NT - 1, 1)

        @block.vector
        def _(dve):
            def prepare(t, s):
                wait_in(dve, at_in[s], t, s)
                nc.vector.tensor_tensor(at[:, s, at_tile(t), :], at[:, s, at_tile(t), :], k.offdiag[:, :].unsqueeze(1),
                                        ALU.mult).then_inc(cut, 1)
                dve.wait_ge(cut, t + 1)
                wait_reuse(dve, e_mul, t)
                nc.vector.tensor_scalar(sign[:, s, 0, :, :], at[:, s, :, :], 0.0, None, ALU.is_gt).then_inc(pos_done, 1)
                nc.vector.tensor_scalar(sign[:, s, 1, :, :], at[:, s, :, :], 0.0, None, ALU.is_lt).then_inc(neg_done, 1)

            def logits(t, s):
                dve.wait_ge(e_mul, t + 1)
                nc.vector.reduce_sum(sums[:, s, :, :], ps_e[s][:, 0:6 * J].rearrange("p (g j c) -> p g j c", g=2, j=J),
                                     AX.X).then_inc(sum_done, 1)
                dve.wait_ge(sum_done, t + 1)
                by = sums[:, s, :, :].rearrange("p g (i a) -> p g i a", a=2)
                nc.vector.tensor_tensor(pre[:, s, 0, :], by[:, 0, :, 0], by[:, 1, :, 1], ALU.add).then_inc(plus_done, 1)
                nc.vector.tensor_tensor(pre[:, s, 1, :], by[:, 1, :, 0], by[:, 0, :, 1], ALU.add).then_inc(minus_done, 1)
                dve.wait_ge(plus_done, t + 1)
                dve.wait_ge(minus_done, t + 1)
                nc.vector.scalar_tensor_tensor(out=e[:, at_tile(t), :, :], in0=pre[:, s, :, :].unsqueeze(1), scalar=SLOPE,
                                               in1=pre[:, s, :, :].unsqueeze(1), op0=ALU.mult, op1=ALU.max).then_inc(e_done, 1)

            def body(t, s):
                if not last(t):
                    prepare(t + 1, 1 - s)
                if not (isinstance(t, int) and t == 0):
                    gru.dve(dve, t - 1, 1 - s)
                logits(t, s)
            gru.biases(dve)
            prepare(0, 0)
            over_tiles(dve, body)
            gru.dve(dve, NT - 1, 1)


def signed_head(nc, k, ins, i, h, e, es):
    with Phase(nc, f"sg{i}") as keep:
        rows = keep.sb("rows", [P, 2, NP])
        v = keep.sb("v", [P, NT, D])
        with Phase(nc, f"sg{i}_in") as ph:
            w = ph.sb("w", [P, C, D])
            hs = ph.sb("hs", [P, 2, D])
            hT = ph.sb("hT", [P, 2, D])
            diag = ph.sb("diag", [P, 2, 2, P])
            ps_t = [ph.ps(f"ps_t{s}", [P, 512]) for s in range(2)]
            ps_v = [ph.ps(f"ps_v{s}", [P, 512]) for s in range(2)]
            ps_f = [ph.ps(f"ps_f{s}", [P, 512]) for s in range(2)]
            w_in, h_done, turned, hT_done, mul_done, v_done = (
                ph.sem(n) for n in ("w_in", "h_done", "turned", "hT_done", "mul_done", "v_done"))
            sems = [ph.sem(n) for n in ("diag_done", "spread_done", "rows_done")]
            block = ph.block()

            @block.sync
            def _(sp):
                sp.dma_start(w[:, :, :], ins["w2"][:, i, :, :]).then_inc(w_in, 16)

            @block.scalar
            def _(act):
                def fixed(t, s):
                    wait_reuse(act, turned, t)
                    nc.scalar.activation(hs[:, s, :].unsqueeze(1), h[:, at_tile(t), :], ACT.Copy).then_inc(h_done, 1)

                def body(t, s):
                    if not last(t):
                        fixed(t + 1, 1 - s)
                    act.wait_ge(mul_done, t + 1)
                    nc.scalar.activation(v[:, at_tile(t), :], ps_v[s][:, 0:D].unsqueeze(1), ACT.Copy).then_inc(v_done, 1)
                fixed(0, 0)
                over_tiles(act, body)
                diag_rows(nc, k, None, None, act, None, 2, rows, diag, ps_f, sems)[2]()

            @block.tensor
            def _(pe):
                def turn(t, s):
                    pe.wait_ge(h_done, t + 1)
                    wait_reuse(pe, hT_done, t)
                    for c in range(C):
                        mm = nc.tensor.transpose(ps_t[s][:, c * P:(c + 1) * P], hs[:, s, c * P:(c + 1) * P], k.ident[:, :])
                    mm.then_inc(turned, 1)

                def body(t, s):
                    if not last(t):
                        turn(t + 1, 1 - s)
                    pe.wait_ge(hT_done, t + 1)
                    wait_reuse(pe, v_done, t)
                    for c in range(C):
                        mm = nc.tensor.matmul(ps_v[s][:, 0:D], hT[:, s, c * P:(c + 1) * P], w[:, c, :],
                                              start=(c == 0), stop=(c == C - 1))
                    mm.then_inc(mul_done, 1)
                turn(0, 0)
                pe.wait_ge(w_in, 16)
                over_tiles(pe, body)
                diag_rows(nc, k, None, pe, None, None, 2, rows, diag, ps_f, sems)[1]()

            @block.vector
            def _(dve):
                def body(t, s):
                    dve.wait_ge(turned, t + 1)
                    wait_reuse(dve, mul_done, t)
                    nc.vector.tensor_copy(hT[:, s, :], ps_t[s][:, 0:D]).then_inc(hT_done, 1)
                over_tiles(dve, body)
                diag_rows(nc, k, dve, None, None,
                          lambda t: e[:, at_tile(t), :, i:i + 1].rearrange("p a g i -> p (a g i)"),
                          2, rows, diag, ps_f, sems)[0]()
        signed_attend(nc, k, ins, i, rows, v, es)


def signed_attend(nc, k, ins, i, rows, v, es):
    with Phase(nc, f"sg{i}_at") as ph:
        a = ph.sb("a", [P, 2, N])
        mask = ph.sb("mask", [P, 2, N], BF16)
        minus = ph.sb("minus", [P, N])
        z = ph.sb("z", [P, 2, NP])
        pT = ph.sb("pT", [P, 2, NP])
        two_max = ph.sb("two_max", [P, 2, 2])
        neg_max = ph.sb("neg_max", [P, 2])
        row_max = ph.sb("row_max", [P, 2])
        den = ph.sb("den", [P, 2])
        den_safe = ph.sb("den_safe", [P, 2])
        inv = ph.sb("inv", [P, 2])
        ps_p = [ph.ps(f"ps_p{c}", [P, 1024]) for c in range(3)]
        ps_o = [ph.ps(f"ps_o{s}", [P, 512]) for s in range(2)]
        a_in = [ph.sem(f"a_in{s}") for s in range(2)]
        pad_done, cut, pos_mask, neg_mask, plus_done, minus_done, joined = (
            ph.sem(n) for n in ("pad_done", "cut", "pos_mask", "neg_mask", "plus_done", "minus_done", "joined"))
        max_done, neg_done, p_done, scaled, turned, pT_done, pv_done = (
            ph.sem(n) for n in ("max_done", "neg_done", "p_done", "scaled", "turned", "pT_done", "pv_done"))
        safe_done, inv_done, es_done = (ph.sem(n) for n in ("safe_done", "inv_done", "es_done"))
        block = ph.block()

        @block.sync
        def _(sp):
            def body(t, s):
                wait_reuse(sp, scaled, t)
                sp.dma_start(a[:, s, :], ins["a_rows"][at_tile(t), :, :]).then_inc(a_in[s], 16)
            over_tiles(sp, body)

        @block.gpsimd
        def _(pool):
            nc.gpsimd.memset(z[:, :, N:NP], 0.0).then_inc(pad_done, 1)

        @block.scalar
        def _(act):
            def exps(t, s):
                wait_reuse(act, safe_done, t)
                act.wait_ge(neg_done, t + 1)
                nc.scalar.activation(z[:, s, 0:N], z[:, s, 0:N], ACT.Exp, bias=neg_max[:, s:s + 1],
                                     accum_out=den[:, s:s + 1]).then_inc(p_done, 1)

            def body(t, s):
                if not last(t):
                    exps(t + 1, 1 - s)
                wait_reuse(act, pv_done, t)
                for c, (m0, n) in enumerate(CHUNKS):
                    wait_count(act, turned, t, 3, c + 1)
                    nc.scalar.activation(pT[:, s, m0 * P:(m0 + n) * P], ps_p[c][:, 0:n * P],
                                         ACT.Copy).then_inc(pT_done, 1)
            exps(0, 0)
            over_tiles(act, body)

        @block.tensor
        def _(pe):
            def turn(t, s):
                pe.wait_ge(scaled, t + 1)
                for c, (m0, n) in enumerate(CHUNKS):
                    wait_count(pe, pT_done, t, 3, c + 1 - 3)
                    for m in range(m0, m0 + n):
                        mm = nc.tensor.transpose(ps_p[c][:, (m - m0) * P:(m - m0 + 1) * P],
                                                 z[:, s, m * P:(m + 1) * P], k.ident[:, :])
                    mm.then_inc(turned, 1)

            def body(t, s):
                if not last(t):
                    turn(t + 1, 1 - s)
                wait_reuse(pe, es_done, t)
                for c, (m0, n) in enumerate(CHUNKS):
                    wait_count(pe, pT_done, t, 3, c + 1)
                    for m in range(m0, m0 + n):
                        mm = nc.tensor.matmul(ps_o[s][:, 0:D], pT[:, s, m * P:(m + 1) * P], v[:, m, :],
                                              start=(m == 0), stop=(m == NT - 1))
                mm.then_inc(pv_done, 1)
            pe.wait_ge(pad_done, 1)
            turn(0, 0)
            over_tiles(pe, body)

        @block.vector
        def _(dve):
            def logits(t, s):
                wait_in(dve, a_in[s], t, s)
                if last(t):
                    block_diag, off = a[:, s, t * P:N], k.offdiag[:, 0:N - t * P]
                else:
                    block_diag, off = a[:, s, bass.ds(t * P, P)], k.offdiag[:, :]
                nc.vector.tensor_tensor(block_diag, block_diag, off, ALU.mult).then_inc(cut, 1)
                dve.wait_ge(cut, t + 1)
                wait_reuse(dve, minus_done, t, depth=1)
                nc.vector.tensor_scalar(mask[:, 0, :], a[:, s, :], 0.0, -BIG, ALU.is_le, ALU.mult).then_inc(pos_mask, 1)
                nc.vector.tensor_scalar(mask[:, 1, :], a[:, s, :], 0.0, -BIG, ALU.is_ge, ALU.mult).then_inc(neg_mask, 1)
                wait_count(dve, turned, t, 3, 3 - 6)
                wait_apart(dve, pos_mask, t, 1, 1)
                nc.vector.tensor_tensor_reduce(out=z[:, s, 0:N], in0=rows[:, 0, 0:N], in1=mask[:, 0, :], scale=1.0,
                                               scalar=-2 * BIG, op0=ALU.add, op1=ALU.max,
                                               accum_out=two_max[:, s, 0:1]).then_inc(plus_done, 1)
                wait_reuse(dve, joined, t, depth=1)
                wait_apart(dve, neg_mask, t, 1, 1)
                nc.vector.tensor_tensor_reduce(out=minus[:, :], in0=rows[:, 1, 0:N], in1=mask[:, 1, :], scale=1.0,
                                               scalar=-2 * BIG, op0=ALU.add, op1=ALU.max,
                                               accum_out=two_max[:, s, 1:2]).then_inc(minus_done, 1)
                dve.wait_ge(plus_done, t + 1)
                dve.wait_ge(minus_done, t + 1)
                nc.vector.tensor_tensor(z[:, s, 0:N], z[:, s, 0:N], minus[:, :], ALU.max).then_inc(joined, 1)
                nc.vector.reduce_max(row_max[:, s:s + 1], two_max[:, s, :], AX.X).then_inc(max_done, 1)
                dve.wait_ge(max_done, t + 1)
                nc.vector.tensor_scalar(neg_max[:, s:s + 1], row_max[:, s:s + 1], FLOOR, -1.0, ALU.max,
                                        ALU.mult).then_inc(neg_done, 1)

            def scale(t, s):
                dve.wait_ge(p_done, t + 1)
                nc.vector.tensor_tensor(z[:, s, 0:N], z[:, s, 0:N], a[:, s, :], ALU.mult).then_inc(scaled, 1)

            def finish(t, s):
                nc.vector.tensor_scalar(den_safe[:, s:s + 1], den[:, s:s + 1], 0.5, float(HEADS), ALU.max,
                                        ALU.mult).then_inc(safe_done, 1)
                dve.wait_ge(safe_done, t + 1)
                nc.vector.reciprocal(inv[:, s:s + 1], den_safe[:, s:s + 1]).then_inc(inv_done, 1)
                dve.wait_ge(inv_done, t + 1)
                dve.wait_ge(pv_done, t + 1)
                if i == 0:
                    nc.vector.tensor_scalar(es[:, at_tile(t), :], ps_o[s][:, 0:D].unsqueeze(1), inv[:, s:s + 1], None,
                                            ALU.mult).then_inc(es_done, 1)
                else:
                    nc.vector.scalar_tensor_tensor(out=es[:, at_tile(t), :], in0=ps_o[s][:, 0:D].unsqueeze(1),
                                                   scalar=inv[:, s:s + 1], in1=es[:, at_tile(t), :],
                                                   op0=ALU.mult, op1=ALU.add).then_inc(es_done, 1)

            def body(t, s):
                if not last(t):
                    logits(t + 1, 1 - s)
                if not (isinstance(t, int) and t == 0):
                    finish(t - 1, 1 - s)
                if not last(t):
                    scale(t + 1, 1 - s)
            logits(0, 0)
            scale(0, 0)
            over_tiles(dve, body)
            finish(NT - 1, 1)


def signed_node(nc, k, ins, h, es):
    with Phase(nc, "sg_node") as ph:
        gru = Gru(nc, k, ph, ins, "node", depth=2)
        block = ph.block()

        @block.sync
        def _(sp):
            gru.load(sp)

        @block.gpsimd
        def _(pool):
            def body(t, s):
                wait_reuse(pool, gru.x_done, t)
                nc.gpsimd.tensor_copy(gru.hid[:, s, :].unsqueeze(1), h[:, at_tile(t), :]).then_inc(gru.hid_ready, 1)
            over_tiles(pool, body)

        @block.tensor
        def _(pe):
            def body(t, s):
                if not last(t):
                    gru.pe_turn(pe, t + 1, 1 - s)
                gru.pe_gates(pe, t, s)
            pe.wait_ge(gru.w_in, 64)
            gru.pe_turn(pe, 0, 0)
            over_tiles(pe, body)

        @block.scalar
        def _(act):
            def fixed(t, s):
                wait_reuse(act, gru.turned, t)
                nc.scalar.activation(gru.inp[:, s, :].unsqueeze(1), es[:, at_tile(t), :], ACT.Copy).then_inc(gru.inp_ready, 1)

            def body(t, s):
                if not last(t):
                    fixed(t + 1, 1 - s)
                    gru.act_keep(act, t + 1, 1 - s)
                gru.act_gates(act, t, s)
                gru.act_candidate(act, t, s)
            fixed(0, 0)
            gru.act_keep(act, 0, 0)
            over_tiles(act, body)

        @block.vector
        def _(dve):
            gru.biases(dve)
            over_tiles(dve, lambda t, s: gru.dve(dve, t, s))


def masked_attention(nc, k, ins):
    H, O = 4, D // 4
    with Phase(nc, "ma") as keep:
        qT = keep.sb("qT", [P, C, NP])
        kT = keep.sb("kT", [P, C, NP])
        v = keep.sb("v", [P, NT, D])
        masked_in(nc, k, ins, qT, kT, v, H, O)
        masked_attend(nc, k, ins, qT, kT, v, H, O)


def masked_in(nc, k, ins, qT, kT, v, H, O):
    with Phase(nc, "ma_in") as ph:
        w = ph.sb("w", [P, C, 3 * D])
        b_col = ph.sb("b_col", [P, 2, C])
        b_v = ph.sb("b_v", [P, D])
        hs = ph.sb("hs", [P, 2, D])
        hT = ph.sb("hT", [P, 2, D])
        ps_t = [ph.ps(f"ps_t{s}", [P, 512]) for s in range(2)]
        ps_qk = [[ph.ps(f"ps_{n}{s}", [P, 512]) for s in range(2)] for n in "qk"]
        ps_v = [ph.ps(f"ps_v{s}", [P, 512]) for s in range(2)]
        w_in, h_done, turned, hT_done, qk_mul, v_mul, q_done, k_done, v_done = (
            ph.sem(n) for n in ("w_in", "h_done", "turned", "hT_done", "qk_mul", "v_mul", "q_done", "k_done", "v_done"))
        block = ph.block()

        @block.sync
        def _(sp):
            sp.dma_start(w[:, :, :], ins["w3"]).then_inc(w_in, 16)
            sp.dma_start(b_col[:, :, :], ins["b3_col"]).then_inc(w_in, 16)
            sp.dma_start(b_v[:, :], ins["b3_v"]).then_inc(w_in, 16)

        @block.scalar
        def _(act):
            def normed(t, s):
                wait_reuse(act, turned, t)
                nc.scalar.activation(hs[:, s, :], k.x[:, at_tile(t), :], ACT.Relu,
                                     bias=k.nmr[:, at_tile(t)], scale=k.rstd[:, at_tile(t)]).then_inc(h_done, 1)

            def body(t, s):
                if not last(t):
                    normed(t + 1, 1 - s)
                act.wait_ge(qk_mul, t + 1)
                for c in range(C):
                    ins_ = nc.scalar.activation(kT[:, c, bass.ds(t * P, P)], ps_qk[1][s][:, c * P:(c + 1) * P],
                                                ACT.Identity, bias=b_col[:, 1, c:c + 1])
                ins_.then_inc(k_done, 1)
            normed(0, 0)
            act.wait_ge(w_in, 48)
            over_tiles(act, body)

        @block.tensor
        def _(pe):
            def turn(t, s):
                pe.wait_ge(h_done, t + 1)
                wait_reuse(pe, hT_done, t)
                for c in range(C):
                    mm = nc.tensor.transpose(ps_t[s][:, c * P:(c + 1) * P], hs[:, s, c * P:(c + 1) * P], k.ident[:, :])
                mm.then_inc(turned, 1)

            def body(t, s):
                if not last(t):
                    turn(t + 1, 1 - s)
                pe.wait_ge(hT_done, t + 1)
                wait_reuse(pe, q_done, t)
                wait_reuse(pe, k_done, t)
                for f in range(2 * C):
                    for c in range(C):
                        mm = nc.tensor.matmul(ps_qk[f // C][s][:, f % C * P:(f % C + 1) * P], w[:, c, f * P:(f + 1) * P],
                                              hT[:, s, c * P:(c + 1) * P], start=(c == 0), stop=(c == C - 1))
                mm.then_inc(qk_mul, 1)
                wait_reuse(pe, v_done, t)
                for c in range(C):
                    mm = nc.tensor.matmul(ps_v[s][:, 0:D], hT[:, s, c * P:(c + 1) * P], w[:, c, 2 * D:3 * D],
                                          start=(c == 0), stop=(c == C - 1))
                mm.then_inc(v_mul, 1)
            turn(0, 0)
            pe.wait_ge(w_in, 48)
            over_tiles(pe, body)

        @block.vector
        def _(dve):
            dve.wait_ge(w_in, 48)

            def body(t, s):
                dve.wait_ge(turned, t + 1)
                wait_reuse(dve, v_mul, t)
                nc.vector.tensor_copy(hT[:, s, :], ps_t[s][:, 0:D]).then_inc(hT_done, 1)
                dve.wait_ge(qk_mul, t + 1)
                for c in range(C):
                    ins_ = nc.vector.tensor_scalar(qT[:, c, bass.ds(t * P, P)], ps_qk[0][s][:, c * P:(c + 1) * P],
                                                   b_col[:, 0, c:c + 1], float(O) ** -0.5, ALU.add, ALU.mult)
                ins_.then_inc(q_done, 1)
                dve.wait_ge(v_mul, t + 1)
                nc.vector.tensor_tensor(v[:, at_tile(t), :], ps_v[s][:, 0:D].unsqueeze(1), b_v[:, :].unsqueeze(1),
                                        ALU.add).then_inc(v_done, 1)
            over_tiles(dve, body)


COLS = 512
PIECES = [(j * COLS, min(COLS, N - j * COLS)) for j in range((N + COLS - 1) // COLS)]
QUADS = [(m, min(4, NT - m)) for m in range(0, NT, 4)]
RING = 3


def masked_attend(nc, k, ins, qT, kT, v, H, O):
    NPC, NQ = len(PIECES), len(QUADS)
    assert NPC % RING == 0 and NQ % RING == 0
    with Phase(nc, "ma_at") as ph:
        a = ph.sb("a", [P, 2, N])
        mask = ph.sb("mask", [P, N], BF16)
        q = ph.sb("q", [P, 2, C, P])
        z = ph.sb("z", [P, 2, NP])
        pT = ph.sb("pT", [P, 2, NP])
        gb = ph.sb("gb", [P, 1])
        wo = ph.sb("wo", [P, C, D])
        b_o = ph.sb("b_o", [P, D])
        part_max = ph.sb("part_max", [P, 2, NPC])
        row_max = ph.sb("row_max", [P, 2])
        neg_max = ph.sb("neg_max", [P, 2])
        den = ph.sb("den", [P, 2, H])
        inv = ph.sb("inv", [P, 2, H])
        o = ph.sb("o", [P, 2, D])
        oT = ph.sb("oT", [P, 2, D])
        ps_s = [ph.ps(f"ps_s{r}", [P, COLS]) for r in range(RING)]
        ps_p = [ph.ps(f"ps_p{r}", [P, 4 * P]) for r in range(RING)]
        ps_o = [ph.ps(f"ps_o{s}", [P, 512]) for s in range(2)]
        a_in = [ph.sem(f"a_in{s}") for s in range(2)]
        (w_in, pad_done, xb_done, q_done, mask_done, bias_done, scored, summed, max_done, neg_done, p_done, turned) = (
            ph.sem(n) for n in ("w_in", "pad_done", "xb_done", "q_done", "mask_done", "bias_done", "scored", "summed",
                                "max_done", "neg_done", "p_done", "turned"))
        pT_act, pT_dve, pv_done, inv_done, o_done, o_turned, oT_done, out_done, x_done = (
            ph.sem(n) for n in ("pT_act", "pT_dve", "pv_done", "inv_done", "o_done", "o_turned", "oT_done", "out_done",
                                "x_done"))
        block = ph.block()

        def shifted(t, s, h, by):
            over, h = (h + by) // H, (h + by) % H
            if isinstance(t, int) and not 0 <= t + over < NT:
                return None
            return (t + over, (s + over) % 2, h) if over else (t, s, h)

        def do(stage, at):
            if at is not None:
                stage(*at)

        @block.sync
        def _(sp):
            sp.dma_start(gb[:, :], ins["gb"]).then_inc(w_in, 16)
            sp.dma_start(wo[:, :, :], ins["w_out"]).then_inc(w_in, 16)
            sp.dma_start(b_o[:, :], ins["b_out"]).then_inc(w_in, 16)

            def body(t, s):
                wait_count(sp, summed, t, H * NPC, H * NPC - 2 * H * NPC)
                sp.dma_start(a[:, s, :], ins["a_rows"][at_tile(t), :, :]).then_inc(a_in[s], 16)
            over_tiles(sp, body)

        @block.gpsimd
        def _(pool):
            nc.gpsimd.memset(z[:, :, N:NP], 0.0).then_inc(pad_done, 1)

            def body(t, s):
                wait_count(pool, scored, t, H * NPC, H * NPC - 2 * H * NPC)
                nc.gpsimd.tensor_copy(q[:, s, :, :], qT[:, :, bass.ds(t * P, P)]).then_inc(q_done, 1)
            over_tiles(pool, body)

        @block.scalar
        def _(act):
            def exps(t, s, h):
                wait_count(act, neg_done, t, H, h + 1)
                if h == 0:
                    wait_reuse(act, inv_done, t)
                nc.scalar.activation(z[:, h % 2, 0:N], z[:, h % 2, 0:N], ACT.Exp, bias=neg_max[:, h % 2:h % 2 + 1],
                                     accum_out=den[:, s, h:h + 1]).then_inc(p_done, 1)

            def evacuate(t, s, h):
                wait_count(act, pv_done, t, H, h + 1 - 2)
                for c in range(0, NQ, 2):
                    m0, n = QUADS[c]
                    wait_count(act, turned, t, NQ * H, NQ * h + c + 1)
                    nc.scalar.activation(pT[:, h % 2, m0 * P:(m0 + n) * P], ps_p[c % RING][:, 0:n * P],
                                         ACT.Copy).then_inc(pT_act, 1)

            def keep_o(t, s):
                act.wait_ge(o_turned, t + 1)
                wait_reuse(act, out_done, t)
                nc.scalar.activation(oT[:, s, :], ps_o[s][:, D:2 * D], ACT.Copy).then_inc(oT_done, 1)

            def body(t, s):
                for h in range(H):
                    exps(t, s, h)
                    evacuate(t, s, h)
                    if h == 2 and not (isinstance(t, int) and t == 0):
                        keep_o(t - 1, 1 - s)
            over_tiles(act, body)
            keep_o(NT - 1, 1)

        @block.tensor
        def _(pe):
            def scores(t, s, h):
                if h == 0:
                    pe.wait_ge(q_done, t + 1)
                rows = slice((h % 2) * O, (h % 2 + 1) * O)
                for j, (c0, n) in enumerate(PIECES):
                    wait_count(pe, summed, t, H * NPC, NPC * h + j + 1 - RING)
                    nc.tensor.matmul(ps_s[j % RING][:, 0:n], q[rows, s, h // 2, :], kT[rows, h // 2, c0:c0 + n],
                                     start=True, stop=True).then_inc(scored, 1)

            def done_before(c):
                b = c - RING
                return (b + 1) // 2 if b % 2 else b // 2 + 1

            def turn(t, s, h):
                wait_count(pe, p_done, t, H, h + 1)
                for c, (m0, n) in enumerate(QUADS):
                    wait_count(pe, pT_act if c % 2 else pT_dve, t, (NQ // 2) * H, (NQ // 2) * h + done_before(c))
                    for m in range(m0, m0 + n):
                        mm = nc.tensor.transpose(ps_p[c % RING][:, (m - m0) * P:(m - m0 + 1) * P],
                                                 z[:, h % 2, m * P:(m + 1) * P], k.ident[:, :])
                    mm.then_inc(turned, 1)

            def values(t, s, h):
                wait_count(pe, pT_act, t, (NQ // 2) * H, (NQ // 2) * (h + 1))
                wait_count(pe, pT_dve, t, (NQ // 2) * H, (NQ // 2) * (h + 1))
                if h == 0:
                    wait_reuse(pe, x_done, t)
                for m in range(NT):
                    mm = nc.tensor.matmul(ps_o[s][:, h * O:(h + 1) * O], pT[:, h % 2, m * P:(m + 1) * P],
                                          v[:, m, h * O:(h + 1) * O], start=(m == 0), stop=(m == NT - 1))
                mm.then_inc(pv_done, 1)

            def turn_o(t, s):
                pe.wait_ge(o_done, t + 1)
                for c in range(C):
                    mm = nc.tensor.transpose(ps_o[s][:, D + c * P:D + (c + 1) * P], o[:, s, c * P:(c + 1) * P], k.ident[:, :])
                mm.then_inc(o_turned, 1)

            def project(t, s):
                pe.wait_ge(oT_done, t + 1)
                for c in range(C):
                    mm = nc.tensor.matmul(ps_o[s][:, 0:D], oT[:, s, c * P:(c + 1) * P], wo[:, c, :],
                                          start=(c == 0), stop=(c == C - 1))
                mm.then_inc(out_done, 1)

            def body(t, s):
                for h in range(H):
                    do(scores, shifted(t, s, h, 1))
                    turn(t, s, h)
                    do(values, shifted(t, s, h, -1))
                    if h == 1 and not (isinstance(t, int) and t == 0):
                        turn_o(t - 1, 1 - s)
                    if h == 2 and not (isinstance(t, int) and t == 0):
                        project(t - 1, 1 - s)
            pe.wait_ge(w_in, 48)
            pe.wait_ge(pad_done, 1)
            scores(0, 0, 0)
            over_tiles(pe, body)
            values(NT - 1, 1, H - 1)
            turn_o(NT - 1, 1)
            project(NT - 1, 1)

        @block.vector
        def _(dve):
            def bias(t, s):
                wait_in(dve, a_in[s], t, s)
                wait_reuse(dve, bias_done, t, depth=1)
                nc.vector.tensor_scalar(mask[:, :], a[:, s, :], 0.0, -BIG, ALU.is_equal, ALU.mult).then_inc(mask_done, 1)
                dve.wait_ge(mask_done, t + 1)
                nc.vector.scalar_tensor_tensor(out=a[:, s, :], in0=a[:, s, :], scalar=gb[:, 0:1], in1=mask[:, :],
                                               op0=ALU.mult, op1=ALU.add).then_inc(bias_done, 1)

            def logits(t, s, h):
                if h == 0:
                    bias(t, s)
                    dve.wait_ge(bias_done, t + 1)
                wait_count(dve, turned, t, NQ * H, NQ * (h + 1 - 2))
                for j, (c0, n) in enumerate(PIECES):
                    wait_apart(dve, scored, t, H * NPC, NPC * h + j + 1)
                    nc.vector.tensor_tensor_reduce(out=z[:, h % 2, c0:c0 + n], in0=ps_s[j % RING][:, 0:n],
                                                   in1=a[:, s, c0:c0 + n], scale=1.0, scalar=-2 * BIG, op0=ALU.add,
                                                   op1=ALU.max, accum_out=part_max[:, h % 2, j:j + 1]).then_inc(summed, 1)
                wait_count(dve, summed, t, H * NPC, NPC * (h + 1))
                nc.vector.reduce_max(row_max[:, h % 2:h % 2 + 1], part_max[:, h % 2, :], AX.X).then_inc(max_done, 1)
                wait_count(dve, max_done, t, H, h + 1)
                nc.vector.tensor_scalar(neg_max[:, h % 2:h % 2 + 1], row_max[:, h % 2:h % 2 + 1], -1.0, None,
                                        ALU.mult).then_inc(neg_done, 1)

            def evacuate(t, s, h):
                wait_count(dve, pv_done, t, H, h + 1 - 2)
                for c in range(1, NQ, 2):
                    m0, n = QUADS[c]
                    wait_count(dve, turned, t, NQ * H, NQ * h + c + 1)
                    nc.vector.tensor_copy(pT[:, h % 2, m0 * P:(m0 + n) * P], ps_p[c % RING][:, 0:n * P]).then_inc(pT_dve, 1)

            def normalise(t, s):
                wait_count(dve, p_done, t, H, H)
                nc.vector.reciprocal(inv[:, s, :], den[:, s, :]).then_inc(inv_done, 1)
                dve.wait_ge(inv_done, t + 1)
                wait_count(dve, pv_done, t, H, H)
                wait_reuse(dve, o_turned, t)
                nc.vector.tensor_tensor(o[:, s, :].rearrange("p (h o) -> p h o", h=H),
                                        ps_o[s][:, 0:D].rearrange("p (h o) -> p h o", h=H),
                                        inv[:, s, :].unsqueeze(2).to_broadcast([P, H, O]), ALU.mult).then_inc(o_done, 1)

            def finish(t, s):
                dve.wait_ge(out_done, t + 1)
                nc.vector.tensor_tensor(k.x[:, at_tile(t), :], k.x[:, at_tile(t), :], ps_o[s][:, 0:D].unsqueeze(1),
                                        ALU.add).then_inc(x_done, 1)
                dve.wait_ge(x_done, t + 1)
                nc.vector.tensor_tensor(k.x[:, at_tile(t), :], k.x[:, at_tile(t), :], b_o[:, :].unsqueeze(1),
                                        ALU.add).then_inc(xb_done, 1)

            def body(t, s):
                for h in range(H):
                    do(logits, shifted(t, s, h, 1))
                    evacuate(t, s, h)
                    if h == 0 and not (isinstance(t, int) and t == 0):
                        normalise(t - 1, 1 - s)
                    if h == 3 and not (isinstance(t, int) and t == 0):
                        finish(t - 1, 1 - s)
            dve.wait_ge(w_in, 48)
            logits(0, 0, 0)
            over_tiles(dve, body)
            normalise(NT - 1, 1)
            finish(NT - 1, 1)


class Kept:
    pass


def program(nc, ins, out):
    k = Kept()
    with ExitStack() as ctx:
        def sb(name, shape, dt=F32):
            return ctx.enter_context(nc.sbuf_tensor(name, shape, dt))
        k.x = sb("x", [P, NT, D])
        k.ident = sb("ident", [P, P])
        k.offdiag = sb("offdiag", [P, P])
        k.ones = sb("ones", [P, P])
        k.eps = sb("eps", [P, 1])
        k.dis = sb("dis", [P, NT])
        k.diag = sb("diag", [P, NT])
        k.rstd = sb("rstd", [P, NT])
        k.nmr = sb("nmr", [P, NT])
        load_constants(nc, k, ins)
        degrees(nc, k, ins)
        norm_stats(nc, k, 0)
        gcn(nc, k, ins)
        norm_stats(nc, k, 1)
        gat(nc, k, ins)
        norm_stats(nc, k, 2)
        signed_gat(nc, k, ins)
        norm_stats(nc, k, 3)
        masked_attention(nc, k, ins)
        with Phase(nc, "store") as ph:
            stored = ph.sem("stored")
            block = ph.block()

            @block.sync
            def _(sp):
                sp.dma_start(out, k.x[:, :, :]).then_inc(stored, 16)
                sp.wait_ge(stored, 16)


def kernel(**inputs):
    import numpy as np
    import concourse.bacc as bacc
    from concourse.bass_utils import run_bass_kernel_spmd

    x, adj = np.asarray(inputs["x"]), np.asarray(inputs["adj"])

    def rows(a, width):
        return np.ascontiguousarray(np.asarray(a).reshape(-1, P, width).transpose(1, 0, 2))

    def spread(a):
        a = np.asarray(a).reshape(1, -1)
        return np.ascontiguousarray(np.broadcast_to(a, (P, a.shape[1])))

    def stack(*vectors):
        return np.ascontiguousarray(np.stack([spread(v) for v in vectors], axis=1))

    adj_rows = np.zeros((NP, N), adj.dtype)
    adj_rows[:N] = adj
    adj_sq = np.zeros((NP, NP), adj.dtype)
    adj_sq[:N, :N] = adj
    x_pad = np.zeros((NP, D), x.dtype)
    x_pad[:N] = x
    arrays = {
        "x": rows(x_pad, D),
        "a_rows": adj_rows.reshape(NT, P, N),
        "at": np.ascontiguousarray(adj_sq.reshape(NT, P, NT, P).transpose(0, 3, 2, 1)).reshape(NT, P, NP),
        "w0": rows(inputs["L0_gnn_W"], D),
        "b0": spread(inputs["L0_gnn_b"]),
        "w1": rows(inputs["L1_gnn_weight"], D),
        "pw1": rows(np.asarray(inputs["L1_gnn_proj_w"]).T, D),
        "uv1": stack(inputs["L1_gnn_weight_u"], inputs["L1_gnn_weight_v"]),
        "b1": stack(inputs["L1_gnn_bias"], inputs["L1_gnn_proj_b"]),
    }
    diag = np.zeros((NP,), adj.dtype)
    diag[:N] = np.diagonal(adj)
    arrays["diag"] = np.ascontiguousarray(diag.reshape(NT, P).T)
    gat_w = np.asarray(inputs["L2_gnn_gat_W"])
    arrays["w2"] = np.ascontiguousarray(gat_w.reshape(HEADS, C, P, D).transpose(2, 0, 1, 3))
    gat_a = np.asarray(inputs["L2_gnn_gat_a"]).reshape(1, HEADS, 2, D)
    arrays["a2"] = np.ascontiguousarray(np.broadcast_to(gat_a, (P, HEADS, 2, D)))
    for cell in ("edge", "node"):
        for part in ("ih", "hh"):
            arrays[f"{cell}_w{part}"] = rows(np.asarray(inputs[f"L2_gnn_{cell}_W{part}"]).T, 3 * D)
            arrays[f"{cell}_b{part}"] = spread(inputs[f"L2_gnn_{cell}_b{part}"])
    arrays["w3"] = rows(inputs["L3_gnn_Wqkv"], 3 * D)
    bqkv = np.asarray(inputs["L3_gnn_bqkv"])
    arrays["b3_col"] = np.ascontiguousarray(bqkv[:2 * D].reshape(2, C, P).transpose(2, 0, 1))
    arrays["b3_v"] = spread(bqkv[2 * D:])
    arrays["gb"] = spread(inputs["L3_gnn_graph_bias"])
    arrays["w_out"] = rows(inputs["L3_gnn_Wout"], D)
    arrays["b_out"] = spread(inputs["L3_gnn_bout"])
    nc = bacc.Bacc("TRN2", target_bir_lowering=False, num_devices=1)
    ins = {n: nc.dram_tensor(f"in_{n}", a.shape, mybir.dt.from_np(a.dtype), kind="ExternalInput").ap()
           for n, a in arrays.items()}
    out = nc.dram_tensor("out_x", (P, NT, D), F32, kind="ExternalOutput").ap()
    program(nc, ins, out)
    r = run_bass_kernel_spmd(nc, [{f"in_{n}": a for n, a in arrays.items()}], core_ids=[0])
    got = r.results[0]["out_x"]
    return np.ascontiguousarray(got.transpose(1, 0, 2).reshape(NP, D)[:N])
```

```python
from contextlib import ExitStack

import concourse.bass as bass
from concourse import mybir

F32 = mybir.dt.float32
BF16 = mybir.dt.bfloat16
ALU = mybir.AluOpType
ACT = mybir.ActivationFunctionType
AX = mybir.AxisListType

P = 128
N = 2708
NT = (N + P - 1) // P
NP = NT * P
TAIL = N - (NT - 1) * P
D = 256
C = D // P
EPS = 1e-5


def rows_of(m):
    return P if m < NT - 1 else TAIL


def over_tiles(eng, body):
    body(0, 0)
    body(1, 1)
    with eng.Fori(1, NT // 2 - 1) as i:
        body(i * 2, 0)
        body(i * 2 + 1, 1)
    body(NT - 2, 0)
    body(NT - 1, 1)


def loop_ahead(eng, body):
    body(0, 0)
    body(1, 1)
    with eng.Fori(1, NT // 2 - 2) as i:
        body(i * 2, 0)
        body(i * 2 + 1, 1)
    for t in range(NT - 4, NT):
        body(t, t % 2)


def wait_reuse(eng, sem, t, per=1, depth=2):
    if isinstance(t, int):
        if t >= depth:
            eng.wait_ge(sem, (t - depth + 1) * per)
    else:
        eng.wait_ge(sem, t * per + (1 - depth) * per)


def at_tile(t, width=1):
    return bass.ds(t * width, width)


class Phase:

    def __init__(self, nc, name):
        self.nc, self.name, self.ctx, self.sems = nc, name, ExitStack(), []

    def __enter__(self):
        return self

    def __exit__(self, *a):
        said = self.ctx.__exit__(*a)
        if self.sems and a[0] is None:
            self.nc.clear_and_free_semaphores(self.sems)
            self.nc.all_engine_barrier()
        return said

    def sb(self, name, shape, dt=F32):
        return self.ctx.enter_context(self.nc.sbuf_tensor(f"{self.name}_{name}", shape, dt))

    def ps(self, name, shape, dt=F32):
        return self.ctx.enter_context(self.nc.psum_tensor(f"{self.name}_{name}", shape, dt))

    def sem(self, name):
        self.sems.append(self.nc.alloc_semaphore(f"{self.name}_{name}"))
        return self.sems[-1]

    def block(self):
        return self.ctx.enter_context(self.nc.Block())


def load_constants(nc, k, ins):
    with Phase(nc, "const") as ph:
        zero_done, ident_done, x_in = ph.sem("zero_done"), ph.sem("ident_done"), ph.sem("x_in")
        block = ph.block()

        @block.gpsimd
        def _(pool):
            nc.gpsimd.memset(k.ident[:, :], 0.0).then_inc(zero_done, 1)
            nc.gpsimd.memset(k.offdiag[:, :], 1.0).then_inc(zero_done, 1)
            nc.gpsimd.memset(k.ones[:, :], 1.0)
            nc.gpsimd.memset(k.eps[:, :], EPS)
            pool.wait_ge(zero_done, 2)
            nc.gpsimd.affine_select(out=k.ident[:, :], in_=k.ident[:, :], compare_op=ALU.not_equal,
                                    fill=1.0, base=0, pattern=[[-1, P]], channel_multiplier=1)
            nc.gpsimd.affine_select(out=k.offdiag[:, :], in_=k.offdiag[:, :],
                                    compare_op=ALU.not_equal, fill=0.0, base=0,
                                    pattern=[[-1, P]], channel_multiplier=1)

        @block.sync
        def _(sp):
            sp.dma_start(k.x[:, :, :], ins["x"]).then_inc(x_in, 16)
            sp.dma_start(k.diag[:, :], ins["diag"]).then_inc(x_in, 16)
            sp.wait_ge(x_in, 32)


def degrees(nc, k, ins):
    with Phase(nc, "deg") as ph:
        a = ph.sb("a_rows", [P, 4, N])
        deg = ph.sb("deg", [P, NT])
        root = ph.sb("root", [P, NT])
        row_in = [ph.sem(f"row_in{j}") for j in range(4)]
        act_sum, dve_sum = ph.sem("act_sum"), ph.sem("dve_sum")
        rooted = ph.sem("rooted")
        block = ph.block()

        @block.sync
        def _(sp):
            for t in range(NT):
                if t >= 4:
                    sp.wait_ge(act_sum if t % 2 == 0 else dve_sum, t // 2 - 1)
                sp.dma_start(a[:, t % 4, :], ins["a_rows"][t]).then_inc(row_in[t % 4], 16)

        @block.scalar
        def _(act):
            for t in range(0, NT, 2):
                act.wait_ge(row_in[t % 4], 16 * (t // 4 + 1))
                nc.scalar.activation(a[:, t % 4, :], a[:, t % 4, :], ACT.Copy,
                                     accum_out=deg[:, t:t + 1]).then_inc(act_sum, 1)
            act.wait_ge(act_sum, NT // 2)
            act.wait_ge(dve_sum, NT // 2)
            nc.scalar.activation(root[:, :], deg[:, :], ACT.Sqrt, bias=k.ones[:, 0:1]).then_inc(rooted, 1)

        @block.vector
        def _(dve):
            for t in range(1, NT, 2):
                dve.wait_ge(row_in[t % 4], 16 * (t // 4 + 1))
                nc.vector.reduce_sum(deg[:, t:t + 1], a[:, t % 4, :], AX.X).then_inc(dve_sum, 1)
            dve.wait_ge(rooted, 1)
            nc.vector.reciprocal(k.dis[:, :], root[:, :])


def norm_stats(nc, k, layer):
    with Phase(nc, f"norm{layer}") as ph:
        st = ph.sb("bn", [P, NT, 6])
        mv = ph.sb("mv", [P, NT, 2])
        root = ph.sb("sd", [P, NT])
        st_done, mv_done = ph.sem("st_done"), ph.sem("mv_done")
        rooted, rstd_done = ph.sem("sd_done"), ph.sem("rstd_done")
        block = ph.block()

        @block.vector
        def _(dve):
            for t in range(NT):
                nc.vector.bn_stats(st[:, t, :], k.x[:, t, :]).then_inc(st_done, 1)
            for t in range(NT):
                dve.wait_ge(st_done, t + 1)
                nc.vector.bn_aggr(mv[:, t, :], st[:, t, :]).then_inc(mv_done, 1)
            dve.wait_ge(rooted, 1)
            nc.vector.reciprocal(k.rstd[:, :], root[:, :]).then_inc(rstd_done, 1)
            dve.wait_ge(rstd_done, 1)
            nc.vector.scalar_tensor_tensor(out=k.nmr[:, :], in0=mv[:, :, 0], scalar=-1.0,
                                           in1=k.rstd[:, :], op0=ALU.mult, op1=ALU.mult)

        @block.scalar
        def _(act):
            act.wait_ge(mv_done, NT)
            nc.scalar.activation(root[:, :], mv[:, :, 1], ACT.Sqrt, bias=k.eps[:, 0:1]).then_inc(rooted, 1)


def gcn(nc, k, ins):
    with Phase(nc, "gcn") as ph:
        s_all = ph.sb("support", [P, NT, D])
        w = ph.sb("w", [P, C, D])
        b = ph.sb("b", [P, D])
        h = ph.sb("h", [P, 2, D])
        hT = ph.sb("hT", [P, 2, D])
        at = ph.sb("at", [P, 3, NP])
        u = ph.sb("u", [P, 2, D])
        ps_t = [ph.ps(f"ps_t{s}", [P, 512]) for s in range(2)]
        ps_o = [ph.ps(f"ps_o{s}", [P, 512]) for s in range(2)]
        ps_a = [ph.ps(f"ps_a{s}", [P, 512]) for s in range(2)]
        w_in, h_done, turned, hT_done, mul_done, s_done = (
            ph.sem(n) for n in ("w_in", "h_done", "turned", "hT_done", "mul_done", "s_done"))
        at_in = [ph.sem(f"at_in{s}") for s in range(2)]
        agg, own, biased, relued, x_done = (ph.sem(n) for n in ("agg", "own", "biased", "relued", "x_done"))
        block = ph.block()

        @block.sync
        def _(sp):
            sp.dma_start(w[:, :, :], ins["w0"]).then_inc(w_in, 16)
            sp.dma_start(b[:, :], ins["b0"]).then_inc(w_in, 16)

            def body(t, s):
                wait_reuse(sp, agg, t)
                sp.dma_start(at[:, s, :], ins["at"][at_tile(t), :, :]).then_inc(at_in[s], 16)
            over_tiles(sp, body)

        @block.scalar
        def _(act):
            def normed(t, s):
                wait_reuse(act, turned, t)
                nc.scalar.activation(h[:, s, :], k.x[:, at_tile(t), :], ACT.Relu,
                                     bias=k.nmr[:, at_tile(t)], scale=k.rstd[:, at_tile(t)]).then_inc(h_done, 1)
            over_tiles(act, normed)

            def out(t, s):
                act.wait_ge(biased, t + 1)
                nc.scalar.activation(u[:, s, :], u[:, s, :], ACT.Relu).then_inc(relued, 1)
            over_tiles(act, out)

        @block.tensor
        def _(pe):
            def turn(t, s):
                pe.wait_ge(h_done, t + 1)
                wait_reuse(pe, hT_done, t)
                for c in range(C):
                    mm = nc.tensor.transpose(ps_t[s][:, c * P:(c + 1) * P], h[:, s, c * P:(c + 1) * P], k.ident[:, :])
                mm.then_inc(turned, 1)

            def body(t, s):
                if not (isinstance(t, int) and t == NT - 1):
                    turn(t + 1, 1 - s)
                pe.wait_ge(hT_done, t + 1)
                wait_reuse(pe, s_done, t)
                for c in range(C):
                    mm = nc.tensor.matmul(ps_o[s][:, 0:D], hT[:, s, c * P:(c + 1) * P], w[:, c, :],
                                          start=(c == 0), stop=(c == C - 1))
                mm.then_inc(mul_done, 1)
            pe.wait_ge(w_in, 32)
            turn(0, 0)
            over_tiles(pe, body)
            pe.wait_ge(s_done, NT)

            def aggregate(t, s):
                wait_in(pe, at_in[s], t, s)
                wait_reuse(pe, own, t)
                for m in range(NT):
                    mm = nc.tensor.matmul(ps_a[s][:, 0:D], at[0:rows_of(m), s, m * P:(m + 1) * P],
                                          s_all[0:rows_of(m), m, :], start=(m == 0), stop=(m == NT - 1))
                mm.then_inc(agg, 1)
            over_tiles(pe, aggregate)

        @block.vector
        def _(dve):
            def body(t, s):
                dve.wait_ge(turned, t + 1)
                wait_reuse(dve, mul_done, t)
                nc.vector.tensor_copy(hT[:, s, :], ps_t[s][:, 0:D]).then_inc(hT_done, 1)
                dve.wait_ge(mul_done, t + 1)
                nc.vector.tensor_scalar(s_all[:, at_tile(t), :], ps_o[s][:, 0:D], k.dis[:, at_tile(t)], None,
                                        ALU.mult).then_inc(s_done, 1)
            over_tiles(dve, body)
            dve.wait_ge(s_done, NT)

            def out(t, s):
                dve.wait_ge(agg, t + 1)
                wait_reuse(dve, x_done, t)
                nc.vector.tensor_tensor(u[:, s, :], ps_a[s][:, 0:D], s_all[:, at_tile(t), :], ALU.add).then_inc(own, 1)
                dve.wait_ge(own, t + 1)
                nc.vector.scalar_tensor_tensor(out=u[:, s, :], in0=u[:, s, :], scalar=k.dis[:, at_tile(t)],
                                               in1=b[:, :], op0=ALU.mult, op1=ALU.add).then_inc(biased, 1)
                dve.wait_ge(relued, t + 1)
                nc.vector.tensor_tensor(k.x[:, at_tile(t), :], k.x[:, at_tile(t), :], u[:, s, :],
                                        ALU.add).then_inc(x_done, 1)
            over_tiles(dve, out)


def wait_in(eng, sem, t, s):
    if isinstance(t, int):
        eng.wait_ge(sem, 16 * (t // 2 + 1))
    else:
        eng.wait_ge(sem, t * 8 + (16 - 8 * s))


BIG = 2.0 ** 126
SLOPE = 0.2
FLOOR = -(2.0 ** 125)
CHUNKS = ((0, 8), (8, 8), (16, 6))


def wait_count(eng, sem, t, per, off):
    if not isinstance(t, int) or per * t + off > 0:
        eng.wait_ge(sem, t * per + off)


def wait_apart(eng, sem, t, per, off):
    wait_count(eng, sem, t, per, off)
    if not isinstance(t, int):
        eng.nop(nofuse=True)


def last(t):
    return isinstance(t, int) and t == NT - 1


def diag_rows(nc, k, dve, pe, act, cols, count, dst, diag, ps, sems):
    diag_done, spread_done, rows_done = sems

    def on_dve():
        def body(t, s):
            wait_reuse(dve, spread_done, t)
            nc.vector.tensor_tensor(diag[:, s, :, :], k.ident[:, :].unsqueeze(1).to_broadcast([P, count, P]),
                                    cols(t).unsqueeze(2).to_broadcast([P, count, P]), ALU.mult).then_inc(diag_done, 1)
        over_tiles(dve, body)

    def on_pe():
        def body(t, s):
            pe.wait_ge(diag_done, t + 1)
            wait_reuse(pe, rows_done, t)
            nc.tensor.matmul(ps[s][:, 0:count * P], k.ones[:, :],
                             diag[:, s, :, :].rearrange("p c n -> p (c n)"), start=True, stop=True).then_inc(spread_done, 1)
        over_tiles(pe, body)

    def on_act():
        def body(t, s):
            act.wait_ge(spread_done, t + 1)
            nc.scalar.activation(dst[:, :, bass.ds(t * P, P)],
                                 ps[s][:, 0:count * P].rearrange("p (c n) -> p c n", c=count),
                                 ACT.Copy).then_inc(rows_done, 1)
        over_tiles(act, body)
    return on_dve, on_pe, on_act


def gat(nc, k, ins):
    H, O = 4, D // 4
    with Phase(nc, "gat") as keep:
        f1_rows = keep.sb("f1_rows", [P, H, NP])
        f12 = keep.sb("f12", [P, NT, 2 * H])
        v = keep.sb("v", [P, NT, D])
        gat_in(nc, k, ins, f1_rows, f12, v, H, O)
        gat_attend(nc, k, ins, f1_rows, f12, v, H, O)


def gat_in(nc, k, ins, f1_rows, f12, v, H, O):
    with Phase(nc, "gat_in") as ph:
        w = ph.sb("w", [P, C, D + 2 * H])
        w_prod = ph.sb("w_prod", [P, 2, C, D])
        pw = ph.sb("pw", [P, C, D])
        uv = ph.sb("uv", [P, 2, D])
        b = ph.sb("b", [P, 2, D])
        bias = ph.sb("bias", [P, D])
        h = ph.sb("h", [P, 2, D])
        hT = ph.sb("hT", [P, 2, D])
        diag = ph.sb("diag", [P, 2, H, P])
        ps_t = [ph.ps(f"ps_t{s}", [P, 512]) for s in range(2)]
        ps_v = [ph.ps(f"ps_v{s}", [P, 512]) for s in range(2)]
        ps_r = [ph.ps(f"ps_r{s}", [P, 512]) for s in range(2)]
        ps_f = [ph.ps(f"ps_f{s}", [P, 512]) for s in range(2)]
        w_in, uv_prod, uv_done, bias_done = (ph.sem(n) for n in ("w_in", "uv_prod", "uv_done", "bias_done"))
        h_done, turned, hT_done, mul_done = (ph.sem(n) for n in ("h_done", "turned", "hT_done", "mul_done"))
        v_done, f_done, x_done, xb_done = (ph.sem(n) for n in ("v_done", "f_done", "x_done", "xb_done"))
        sems = [ph.sem(n) for n in ("diag_done", "spread_done", "rows_done")]
        block = ph.block()

        @block.sync
        def _(sp):
            sp.dma_start(w[:, :, 0:D], ins["w1"]).then_inc(w_in, 16)
            sp.dma_start(pw[:, :, :], ins["pw1"]).then_inc(w_in, 16)
            sp.dma_start(uv[:, :, :], ins["uv1"]).then_inc(w_in, 16)
            sp.dma_start(b[:, :, :], ins["b1"]).then_inc(w_in, 16)

        @block.scalar
        def _(act):
            def normed(t, s):
                wait_reuse(act, turned, t)
                nc.scalar.activation(h[:, s, :], k.x[:, at_tile(t), :], ACT.Relu,
                                     bias=k.nmr[:, at_tile(t)], scale=k.rstd[:, at_tile(t)]).then_inc(h_done, 1)

            def body(t, s):
                if not last(t):
                    normed(t + 1, 1 - s)
                act.wait_ge(mul_done, t + 1)
                nc.scalar.activation(v[:, at_tile(t), :], ps_v[s][:, 0:D], ACT.Copy).then_inc(v_done, 1)
                nc.scalar.activation(f12[:, at_tile(t), :], ps_v[s][:, D:D + 2 * H], ACT.Copy).then_inc(f_done, 1)
            normed(0, 0)
            over_tiles(act, body)
            diag_rows(nc, k, None, None, act, None, H, f1_rows, diag, ps_f, sems)[2]()

        @block.tensor
        def _(pe):
            def turn(t, s):
                pe.wait_ge(h_done, t + 1)
                wait_reuse(pe, hT_done, t)
                for c in range(C):
                    mm = nc.tensor.transpose(ps_t[s][:, c * P:(c + 1) * P], h[:, s, c * P:(c + 1) * P], k.ident[:, :])
                mm.then_inc(turned, 1)

            def body(t, s):
                if not last(t):
                    turn(t + 1, 1 - s)
                pe.wait_ge(hT_done, t + 1)
                wait_reuse(pe, f_done, t)
                for c in range(C):
                    nc.tensor.matmul(ps_v[s][:, 0:D + 2 * H], hT[:, s, c * P:(c + 1) * P], w[:, c, :],
                                     start=(c == 0), stop=(c == C - 1))
                wait_reuse(pe, x_done, t)
                for c in range(C):
                    mm = nc.tensor.matmul(ps_r[s][:, 0:D], hT[:, s, c * P:(c + 1) * P], pw[:, c, :],
                                          start=(c == 0), stop=(c == C - 1))
                mm.then_inc(mul_done, 1)
            pe.wait_ge(w_in, 64)
            turn(0, 0)
            pe.wait_ge(uv_done, 2)
            over_tiles(pe, body)
            diag_rows(nc, k, None, pe, None, None, H, f1_rows, diag, ps_f, sems)[1]()

        @block.vector
        def _(dve):
            dve.wait_ge(w_in, 64)
            for j in range(2):
                nc.vector.tensor_tensor(w_prod[:, j, :, :], w[:, :, 0:D],
                                        uv[:, j, :].unsqueeze(1).to_broadcast([P, C, D]), ALU.mult).then_inc(uv_prod, 1)
            for j in range(2):
                dve.wait_ge(uv_prod, j + 1)
                nc.vector.reduce_sum(w[:, :, D + j * H:D + (j + 1) * H],
                                     w_prod[:, j, :, :].rearrange("p c (h o) -> p c h o", h=H), AX.X).then_inc(uv_done, 1)
            nc.vector.tensor_tensor(bias[:, :], b[:, 0, :], b[:, 1, :], ALU.add).then_inc(bias_done, 1)
            dve.wait_ge(bias_done, 1)

            def body(t, s):
                dve.wait_ge(turned, t + 1)
                wait_reuse(dve, mul_done, t)
                nc.vector.tensor_copy(hT[:, s, :], ps_t[s][:, 0:D]).then_inc(hT_done, 1)
                dve.wait_ge(mul_done, t + 1)
                nc.vector.tensor_tensor(k.x[:, at_tile(t), :], k.x[:, at_tile(t), :], ps_r[s][:, 0:D],
                                        ALU.add).then_inc(x_done, 1)
                dve.wait_ge(x_done, t + 1)
                nc.vector.tensor_tensor(k.x[:, at_tile(t), :], k.x[:, at_tile(t), :], bias[:, :],
                                        ALU.add).then_inc(xb_done, 1)
            over_tiles(dve, body)
            dve.wait_ge(f_done, NT)
            diag_rows(nc, k, dve, None, None, lambda t: f12[:, at_tile(t), 0:H].rearrange("p a h -> p (a h)"),
                      H, f1_rows, diag, ps_f, sems)[0]()


def gat_attend(nc, k, ins, f1_rows, f12, v, H, O):
    with Phase(nc, "gat_at") as ph:
        f2_low = ph.sb("f2_low", [P, NT, H])
        low_ready = ph.sem("low_ready")
        a = ph.sb("a", [P, 2, N])
        mask = ph.sb("mask", [P, 2, N], BF16)
        z = ph.sb("z", [P, H, NP])
        pT = ph.sb("pT", [P, 2, NP])
        row_max = ph.sb("row_max", [P, H])
        neg_max = ph.sb("neg_max", [P, H])
        den = ph.sb("den", [P, 2, H])
        den_safe = ph.sb("den_safe", [P, 2, H])
        inv = ph.sb("inv", [P, 2, H])
        o = ph.sb("o", [P, 2, H, O])
        ps_p = [ph.ps(f"ps_p{c}", [P, 1024]) for c in range(3)]
        ps_o = [ph.ps(f"ps_o{s}", [P, 512]) for s in range(2)]
        a_in = [ph.sem(f"a_in{s}") for s in range(2)]
        (mask_done, pad_done, low_done, leaky_done, mult_done, max_done, neg_done, p_done, turned, pT_done, pv_done,
         safe_done, inv_done, o_done, x_done) = (
            ph.sem(n) for n in ("mask_done", "pad_done", "low_done", "leaky_done", "mult_done", "max_done", "neg_done", "p_done",
                                "turned", "pT_done", "pv_done", "safe_done", "inv_done", "o_done", "x_done"))
        block = ph.block()

        def shifted(t, s, h, by):
            over, h = (h + by) // H, (h + by) % H
            if isinstance(t, int) and not 0 <= t + over < NT:
                return None
            return (t + over, (s + over) % 2, h) if over else (t, s, h)

        def do(stage, at):
            if at is not None:
                stage(*at)

        @block.sync
        def _(sp):
            def body(t, s):
                wait_reuse(sp, mask_done, t)
                wait_reuse(sp, mult_done, t, per=H)
                sp.dma_start(a[:, s, :], ins["a_rows"][at_tile(t), :, :]).then_inc(a_in[s], 16)
            over_tiles(sp, body)

        @block.gpsimd
        def _(pool):
            nc.gpsimd.memset(z[:, :, N:NP], 0.0).then_inc(pad_done, 1)

        @block.scalar
        def _(act):
            def low_branch(t, s, h):
                wait_count(act, turned, t, 3 * H, 3 * (h + 1 - H))
                nc.scalar.activation(z[:, h, 0:N], f1_rows[:, h, 0:N], ACT.Identity, scale=SLOPE,
                                     bias=f2_low[:, at_tile(t), h:h + 1].rearrange("p a h -> p (a h)")).then_inc(
                                         low_done, 1)

            def evacuate(t, s, h):
                wait_count(act, pv_done, t, H, h - 1)
                for c in range(3):
                    m0, n = CHUNKS[c]
                    wait_count(act, turned, t, 3 * H, 3 * h + c + 1)
                    nc.scalar.activation(pT[:, h % 2, m0 * P:(m0 + n) * P], ps_p[c][:, 0:n * P],
                                         ACT.Copy).then_inc(pT_done, 1)

            def body(t, s):
                for h in range(H):
                    do(low_branch, shifted(t, s, h, 2))
                    do(evacuate, shifted(t, s, h, -1))
                    wait_count(act, neg_done, t, H, h + 1)
                    nc.scalar.activation(z[:, h, 0:N], z[:, h, 0:N], ACT.Exp,
                                         bias=neg_max[:, h:h + 1],
                                         accum_out=den[:, s, h:h + 1]).then_inc(p_done, 1)
            act.wait_ge(low_ready, 1)
            low_branch(0, 0, 0)
            low_branch(0, 0, 1)
            over_tiles(act, body)
            evacuate(NT - 1, 1, H - 1)

        @block.tensor
        def _(pe):
            def values(t, s, h):
                wait_count(pe, pT_done, t, 3 * H, 3 * h + 3)
                if h == 0:
                    wait_reuse(pe, o_done, t)
                for m in range(NT):
                    mm = nc.tensor.matmul(ps_o[s][:, h * O:(h + 1) * O], pT[:, h % 2, m * P:(m + 1) * P],
                                          v[:, m, h * O:(h + 1) * O], start=(m == 0), stop=(m == NT - 1))
                mm.then_inc(pv_done, 1)

            def body(t, s):
                for h in range(H):
                    do(values, shifted(t, s, h, -1))
                    wait_count(pe, p_done, t, H, h + 1)
                    for c, (m0, n) in enumerate(CHUNKS):
                        for m in range(m0, m0 + n):
                            mm = nc.tensor.transpose(ps_p[c][:, (m - m0) * P:(m - m0 + 1) * P],
                                                     z[:, h, m * P:(m + 1) * P], k.ident[:, :])
                        mm.then_inc(turned, 1)
            pe.wait_ge(pad_done, 1)
            over_tiles(pe, body)
            values(NT - 1, 1, H - 1)

        @block.vector
        def _(dve):
            def make_mask(t, s):
                wait_in(dve, a_in[s], t, s)
                nc.vector.tensor_scalar(mask[:, s, :], a[:, s, :], 0.0, -BIG, ALU.is_equal,
                                        ALU.mult).then_inc(mask_done, 1)

            def logits(t, s, h):
                if h == 0:
                    make_mask(t, s)
                wait_count(dve, low_done, t, H, h + 1)
                nc.vector.scalar_tensor_tensor(out=z[:, h, 0:N], in0=f1_rows[:, h, 0:N],
                                               scalar=f12[:, at_tile(t), H + h:H + h + 1].rearrange("p a h -> p (a h)"),
                                               in1=z[:, h, 0:N], op0=ALU.add, op1=ALU.max).then_inc(leaky_done, 1)
                wait_count(dve, leaky_done, t, H, h + 1)
                nc.vector.tensor_tensor(z[:, h, 0:N], z[:, h, 0:N], a[:, s, :], ALU.mult).then_inc(mult_done, 1)
                if h == 0:
                    wait_count(dve, mask_done, t, 1, 1)
                wait_apart(dve, mult_done, t, H, h + 1)
                nc.vector.tensor_tensor_reduce(out=z[:, h, 0:N], in0=z[:, h, 0:N], in1=mask[:, s, :], scale=1.0,
                                               scalar=-2 * BIG, op0=ALU.add, op1=ALU.max,
                                               accum_out=row_max[:, h:h + 1]).then_inc(max_done, 1)
                wait_count(dve, max_done, t, H, h + 1)
                nc.vector.tensor_scalar(neg_max[:, h:h + 1], row_max[:, h:h + 1], FLOOR, -1.0, ALU.max,
                                        ALU.mult).then_inc(neg_done, 1)

            def finish(t, s):
                wait_count(dve, p_done, t, H, H)
                nc.vector.tensor_scalar(den_safe[:, s, :], den[:, s, :], 0.5, None, ALU.max).then_inc(safe_done, 1)
                dve.wait_ge(safe_done, t + 1)
                nc.vector.reciprocal(inv[:, s, :], den_safe[:, s, :]).then_inc(inv_done, 1)
                dve.wait_ge(inv_done, t + 1)
                wait_count(dve, pv_done, t, H, H)
                nc.vector.tensor_tensor(o[:, s, :, :], ps_o[s][:, 0:D].rearrange("p (h o) -> p h o", h=H),
                                        inv[:, s, :].unsqueeze(2).to_broadcast([P, H, O]), ALU.mult).then_inc(o_done, 1)
                dve.wait_ge(o_done, t + 1)
                nc.vector.tensor_tensor(k.x[:, at_tile(t), :], k.x[:, at_tile(t), :],
                                        o[:, s, :, :].rearrange("p h o -> p (h o)").unsqueeze(1), ALU.add).then_inc(x_done, 1)

            def body(t, s):
                for h in range(H):
                    do(logits, shifted(t, s, h, 1))
                    if h == 1 and not (isinstance(t, int) and t == 0):
                        finish(t - 1, 1 - s)
            nc.vector.tensor_scalar(f2_low[:, :, :], f12[:, :, H:2 * H], SLOPE, None, ALU.mult).then_inc(low_ready, 1)
            logits(0, 0, 0)
            over_tiles(dve, body)
            finish(NT - 1, 1)


HEADS = 3


class Gru:

    def __init__(self, nc, k, ph, ins, name, h, depth):
        self.nc, self.k, self.depth, self.ins, self.name, self.h = nc, k, depth, ins, name, h
        self.inp, self.hid = ph.sb("inp", [P, 2, D]), ph.sb("hid", [P, 2, D])
        self.wi, self.wh = ph.sb("wi", [P, C, 3 * D]), ph.sb("wh", [P, C, 3 * D])
        self.bi, self.bh = ph.sb("bi", [P, 3 * D]), ph.sb("bh", [P, 3 * D])
        self.b_rz = ph.sb("b_rz", [P, 2 * D])
        self.b_n = ph.sb("b_n", [P, 2 * D])
        self.kept = ph.sb("kept", [P, 2, 4 * P])
        self.rz, self.nn = ph.sb("rz", [P, 2, 2 * D]), ph.sb("nn", [P, 2, 2 * D])
        self.cell = ph.sb("cell", [P, 2, D])
        self.ps_t = [ph.ps(f"ps_gt{s}", [P, 512]) for s in range(depth)]
        self.ps_rz = [ph.ps(f"ps_rz{s}", [P, 512]) for s in range(depth)]
        self.ps_n = [ph.ps(f"ps_n{s}", [P, 512]) for s in range(depth)]
        self.w_in, self.inp_ready, self.hid_ready = ph.sem("gw_in"), ph.sem("inp_ready"), ph.sem("hid_ready")
        self.turned, self.kept_done, self.gates_done = ph.sem("g_turned"), ph.sem("kept_done"), ph.sem("gates_done")
        self.b_done, self.rz_done, self.n_done = ph.sem("b_done"), ph.sem("rz_done"), ph.sem("n_done")
        self.rz_tanh, self.gated, self.reset_done = ph.sem("rz_tanh"), ph.sem("gated"), ph.sem("reset_done")
        self.cand_done, self.cand_tanh = ph.sem("cand_done"), ph.sem("cand_tanh")
        self.diff_done, self.zdiff_done = ph.sem("diff_done"), ph.sem("zdiff_done")
        self.cell_done, self.x_done = ph.sem("cell_done"), ph.sem("gx_done")

    def load(self, sp):
        sp.dma_start(self.wi[:, :, :], self.ins[f"{self.name}_wih"]).then_inc(self.w_in, 16)
        sp.dma_start(self.wh[:, :, :], self.ins[f"{self.name}_whh"]).then_inc(self.w_in, 16)
        sp.dma_start(self.bi[:, :], self.ins[f"{self.name}_bih"]).then_inc(self.w_in, 16)
        sp.dma_start(self.bh[:, :], self.ins[f"{self.name}_bhh"]).then_inc(self.w_in, 16)

    def biases(self, dve):
        dve.wait_ge(self.w_in, 64)
        self.nc.vector.tensor_tensor(self.b_rz[:, :], self.bi[:, 0:2 * D], self.bh[:, 0:2 * D], ALU.add).then_inc(self.b_done, 1)
        self.nc.vector.tensor_copy(self.b_n[:, 0:D], self.bi[:, 2 * D:3 * D]).then_inc(self.b_done, 1)
        self.nc.vector.tensor_copy(self.b_n[:, D:2 * D], self.bh[:, 2 * D:3 * D]).then_inc(self.b_done, 1)
        dve.wait_ge(self.b_done, 3)

    def pe_turn(self, pe, t, s):
        pe.wait_ge(self.inp_ready, t + 1)
        pe.wait_ge(self.hid_ready, t + 1)
        wait_reuse(pe, self.kept_done, t, depth=self.depth)
        for c in range(4):
            src = (self.inp, self.hid)[c // 2]
            mm = self.nc.tensor.transpose(self.ps_t[s % self.depth][:, c * P:(c + 1) * P],
                                          src[:, s, (c % 2) * P:(c % 2 + 1) * P], self.k.ident[:, :])
        mm.then_inc(self.turned, 1)

    def act_keep(self, act, t, s):
        act.wait_ge(self.turned, t + 1)
        wait_reuse(act, self.gates_done, t)
        self.nc.scalar.activation(self.kept[:, s, :], self.ps_t[s % self.depth][:, :], ACT.Copy).then_inc(self.kept_done, 1)

    def pe_gates(self, pe, t, s):
        d = s % self.depth
        pe.wait_ge(self.kept_done, t + 1)
        wait_reuse(pe, self.rz_done, t, depth=self.depth)
        for c in range(4):
            w = (self.wi, self.wh)[c // 2]
            self.nc.tensor.matmul(self.ps_rz[d][:, :], self.kept[:, s, c * P:(c + 1) * P], w[:, c % 2, 0:2 * D],
                                  start=(c == 0), stop=(c == 3))
        wait_reuse(pe, self.n_done, t, depth=self.depth)
        for c in range(4):
            w = (self.wi, self.wh)[c // 2]
            mm = self.nc.tensor.matmul(self.ps_n[d][:, (c // 2) * D:(c // 2 + 1) * D],
                                       self.kept[:, s, c * P:(c + 1) * P], w[:, c % 2, 2 * D:3 * D],
                                       start=(c % 2 == 0), stop=(c % 2 == 1))
        mm.then_inc(self.gates_done, 1)

    def act_gates(self, act, t, s):
        act.wait_ge(self.rz_done, t + 1)
        self.nc.scalar.activation(self.rz[:, s, :], self.rz[:, s, :], ACT.Tanh, scale=0.5).then_inc(self.rz_tanh, 1)

    def act_candidate(self, act, t, s):
        act.wait_ge(self.cand_done, t + 1)
        self.nc.scalar.activation(self.nn[:, s, 0:D], self.nn[:, s, 0:D], ACT.Tanh).then_inc(self.cand_tanh, 1)

    def dve(self, dve, t, s):
        v, k, d = self.nc.vector, self.k, s % self.depth
        rz, nn, cell = self.rz[:, s, :], self.nn[:, s, :], self.cell[:, s, :]
        dve.wait_ge(self.gates_done, t + 1)
        v.tensor_tensor(rz, self.ps_rz[d][:, :], self.b_rz[:, :], ALU.add).then_inc(self.rz_done, 1)
        v.tensor_tensor(nn, self.ps_n[d][:, :], self.b_n[:, :], ALU.add).then_inc(self.n_done, 1)
        dve.wait_ge(self.rz_tanh, t + 1)
        v.tensor_scalar(rz, rz, 0.5, 0.5, ALU.mult, ALU.add).then_inc(self.gated, 1)
        dve.wait_ge(self.n_done, t + 1)
        dve.wait_ge(self.gated, t + 1)
        v.tensor_tensor(cell, self.rz[:, s, 0:D], self.nn[:, s, D:2 * D], ALU.mult).then_inc(self.reset_done, 1)
        dve.wait_ge(self.reset_done, t + 1)
        v.tensor_tensor(self.nn[:, s, 0:D], self.nn[:, s, 0:D], cell, ALU.add).then_inc(self.cand_done, 1)
        dve.wait_ge(self.cand_tanh, t + 1)
        v.tensor_tensor(cell.unsqueeze(1), self.h[:, at_tile(t), :], self.nn[:, s, 0:D].unsqueeze(1), ALU.subtract).then_inc(self.diff_done, 1)
        dve.wait_ge(self.diff_done, t + 1)
        v.tensor_tensor(cell, cell, self.rz[:, s, D:2 * D], ALU.mult).then_inc(self.zdiff_done, 1)
        dve.wait_ge(self.zdiff_done, t + 1)
        v.tensor_tensor(cell, cell, self.nn[:, s, 0:D], ALU.add).then_inc(self.cell_done, 1)
        dve.wait_ge(self.cell_done, t + 1)
        v.scalar_tensor_tensor(out=k.x[:, at_tile(t), :], in0=cell.unsqueeze(1), scalar=k.diag[:, at_tile(t)],
                               in1=k.x[:, at_tile(t), :], op0=ALU.mult, op1=ALU.add).then_inc(self.x_done, 1)


def signed_gat(nc, k, ins):
    v_dram = nc.dram_tensor("sg_v", (HEADS, P, NT, D), F32).ap()
    e_dram = nc.dram_tensor("sg_e", (HEADS * 2 * NT, P), F32).ap()
    with Phase(nc, "sg") as keep:
        h = keep.sb("h", [P, NT, D])
        with Phase(nc, "sg_u") as keep_u:
            u3 = keep_u.sb("u3", [P, NT, 2 * HEADS, 3], BF16)
            signed_in(nc, k, ins, h, u3, v_dram)
            signed_support(nc, k, ins, h, u3, e_dram)
        es = keep.sb("es", [P, NT, D])
        for i in range(HEADS):
            signed_attend(nc, k, ins, i, v_dram, e_dram, es)
        signed_node(nc, k, ins, h, es)


def signed_in(nc, k, ins, h, u3, v_dram):
    J = 2 * HEADS
    with Phase(nc, "sg_in") as ph:
        w = ph.sb("w", [P, HEADS, C, D])
        av = ph.sb("av", [P, HEADS, 2, D])
        prod = ph.sb("prod", [P, J, C, D])
        wa = ph.sb("wa", [P, C, J])
        hs = ph.sb("hs", [P, 2, D])
        hT = ph.sb("hT", [P, 2, D])
        u = ph.sb("u", [P, NT, J])
        rest = ph.sb("rest", [P, 2, NT, J])
        v = ph.sb("v", [P, 4, HEADS, D])
        ps_t = [ph.ps(f"ps_t{s}", [P, 512]) for s in range(2)]
        ps_u = [ph.ps(f"ps_u{s}", [P, 512]) for s in range(2)]
        ps_v = [ph.ps(f"ps_v{s}", [P, 2, 512]) for s in range(2)]
        w_in, prod_done, wa_done, h_done, turned = (ph.sem(n) for n in ("w_in", "prod_done", "wa_done", "h_done", "turned"))
        hT_done, u_mul, v_mul, u_done, kept, split = (
            ph.sem(n) for n in ("hT_done", "u_mul", "v_mul", "u_done", "kept", "split"))
        v_act, v_dve = ph.sem("v_act"), ph.sem("v_dve")
        v_stored = [ph.sem(f"v_stored{s}") for s in range(4)]
        block = ph.block()

        @block.sync
        def _(sp):
            sp.dma_start(w[:, :, :, :], ins["w2"]).then_inc(w_in, 16)
            sp.dma_start(av[:, :, :, :], ins["a2"]).then_inc(w_in, 16)
            for t in range(NT):
                sp.wait_ge(v_act, t + 1)
                sp.wait_ge(v_dve, t + 1)
                sp.dma_start(v_dram[:, :, t, :].rearrange("i p d -> p i d"), v[:, t % 4, :, :]).then_inc(v_stored[t % 4], 16)
            for s in range(4):
                sp.wait_ge(v_stored[s], 16 * len(range(s, NT, 4)))

        @block.gpsimd
        def _(pool):
            def body(t, s):
                pool.wait_ge(h_done, t + 1)
                nc.gpsimd.tensor_copy(h[:, at_tile(t), :], hs[:, s, :].unsqueeze(1)).then_inc(kept, 1)
            over_tiles(pool, body)

        @block.scalar
        def _(act):
            def normed(t, s):
                wait_reuse(act, turned, t)
                wait_reuse(act, kept, t)
                nc.scalar.activation(hs[:, s, :], k.x[:, at_tile(t), :], ACT.Relu,
                                     bias=k.nmr[:, at_tile(t)], scale=k.rstd[:, at_tile(t)]).then_inc(h_done, 1)
            normed(0, 0)
            for t in range(NT):
                if t < NT - 1:
                    normed(t + 1, 1 - t % 2)
                act.wait_ge(v_mul, t + 1)
                if t >= 4:
                    act.wait_ge(v_stored[t % 4], 16 * (t // 4))
                nc.scalar.activation(v[:, t % 4, 0:2, :].rearrange("p i d -> p (i d)"), ps_v[t % 2][:, 0, :],
                                     ACT.Copy).then_inc(v_act, 1)

        @block.tensor
        def _(pe):
            def turn(t, s):
                pe.wait_ge(h_done, t + 1)
                wait_reuse(pe, hT_done, t)
                for c in range(C):
                    mm = nc.tensor.transpose(ps_t[s][:, c * P:(c + 1) * P], hs[:, s, c * P:(c + 1) * P], k.ident[:, :])
                mm.then_inc(turned, 1)

            def body(t, s):
                if not last(t):
                    turn(t + 1, 1 - s)
                pe.wait_ge(hT_done, t + 1)
                wait_reuse(pe, v_act, t)
                wait_reuse(pe, v_dve, t)
                for i in range(HEADS):
                    for c in range(C):
                        mm = nc.tensor.matmul(ps_v[s][:, i // 2, i % 2 * D:(i % 2 + 1) * D], hT[:, s, c * P:(c + 1) * P],
                                              w[:, i, c, :], start=(c == 0), stop=(c == C - 1))
                mm.then_inc(v_mul, 1)
                wait_reuse(pe, u_done, t)
                for c in range(C):
                    mm = nc.tensor.matmul(ps_u[s][:, 0:J], hT[:, s, c * P:(c + 1) * P], wa[:, c, :],
                                          start=(c == 0), stop=(c == C - 1))
                mm.then_inc(u_mul, 1)
            turn(0, 0)
            pe.wait_ge(w_in, 32)
            pe.wait_ge(wa_done, J)
            over_tiles(pe, body)

        @block.vector
        def _(dve):
            dve.wait_ge(w_in, 32)
            for j in range(J):
                nc.vector.tensor_tensor(prod[:, j, :, :], w[:, j // 2, :, :],
                                        av[:, j // 2, j % 2, :].unsqueeze(1).to_broadcast([P, C, D]),
                                        ALU.mult).then_inc(prod_done, 1)
            for j in range(J):
                dve.wait_ge(prod_done, j + 1)
                nc.vector.reduce_sum(wa[:, :, j], prod[:, j, :, :], AX.X).then_inc(wa_done, 1)

            def fixed(t):
                dve.wait_ge(turned, t + 1)
                wait_reuse(dve, u_mul, t)
                nc.vector.tensor_copy(hT[:, t % 2, :], ps_t[t % 2][:, 0:D]).then_inc(hT_done, 1)
            fixed(0)
            for t in range(NT):
                if t < NT - 1:
                    fixed(t + 1)
                dve.wait_ge(v_mul, t + 1)
                if t >= 4:
                    dve.wait_ge(v_stored[t % 4], 16 * (t // 4))
                nc.vector.tensor_copy(v[:, t % 4, 2, :], ps_v[t % 2][:, 1, 0:D]).then_inc(v_dve, 1)
                dve.wait_ge(u_mul, t + 1)
                nc.vector.tensor_copy(u[:, t, :], ps_u[t % 2][:, 0:J]).then_inc(u_done, 1)
            dve.wait_ge(u_done, NT)
            nc.vector.tensor_copy(u3[:, :, :, 0], u[:, :, :]).then_inc(split, 1)
            dve.wait_ge(split, 1)
            nc.vector.tensor_tensor(rest[:, 0, :, :], u[:, :, :], u3[:, :, :, 0], ALU.subtract).then_inc(split, 1)
            dve.wait_ge(split, 2)
            nc.vector.tensor_copy(u3[:, :, :, 1], rest[:, 0, :, :]).then_inc(split, 1)
            dve.wait_ge(split, 3)
            nc.vector.tensor_tensor(rest[:, 1, :, :], rest[:, 0, :, :], u3[:, :, :, 1], ALU.subtract).then_inc(split, 1)
            dve.wait_ge(split, 4)
            nc.vector.tensor_copy(u3[:, :, :, 2], rest[:, 1, :, :])


def signed_support(nc, k, ins, h, u3, e_dram):
    J = 2 * HEADS
    COLUMNS = J * NT
    with Phase(nc, "sg_sup") as ph:
        at = ph.sb("at", [P, 2, NT, P])
        sign = ph.sb("sign", [P, 2, 2, NT, P], BF16)
        sums = ph.sb("sums", [P, 2, 2, J])
        pre = ph.sb("pre", [P, 2, HEADS, 2])
        e = ph.sb("e", [P, HEADS, 2, NT])
        e_rows = ph.sb("e_rows", [COLUMNS // 2, 2, P])
        ps_a = [ph.ps(f"ps_a{s}", [P, 512]) for s in range(2)]
        ps_e = [ph.ps(f"ps_e{s}", [P, 512]) for s in range(2)]
        gru = Gru(nc, k, ph, ins, "edge", h, depth=1)
        at_in = [ph.sem(f"at_in{s}") for s in range(2)]
        cut, pos_done, neg_done, agg, e_mul = (ph.sem(n) for n in ("cut", "pos_done", "neg_done", "agg", "e_mul"))
        sum_done, plus_done, minus_done, e_done = (ph.sem(n) for n in ("sum_done", "plus_done", "minus_done", "e_done"))
        e_turned, e_kept, e_stored = (ph.sem(n) for n in ("e_turned", "e_kept", "e_stored"))
        block = ph.block()

        @block.sync
        def _(sp):
            gru.load(sp)

            def body(t, s):
                wait_reuse(sp, agg, t)
                wait_reuse(sp, neg_done, t)
                sp.dma_start(at[:, s, :, :].rearrange("p m n -> p (m n)"), ins["at"][at_tile(t), :, :]).then_inc(at_in[s], 16)
            over_tiles(sp, body)
            sp.wait_ge(e_kept, 1)
            for j in range(2):
                sp.dma_start(e_dram[j * COLUMNS // 2:(j + 1) * COLUMNS // 2, :], e_rows[:, j, :]).then_inc(e_stored, 16)
            sp.wait_ge(e_stored, 32)

        @block.gpsimd
        def _(pool):
            def body(t, s):
                wait_reuse(pool, gru.turned, t)
                nc.gpsimd.tensor_copy(gru.hid[:, s, :].unsqueeze(1), h[:, at_tile(t), :]).then_inc(gru.hid_ready, 1)
            over_tiles(pool, body)

        @block.tensor
        def _(pe):
            def body(t, s):
                pe.wait_ge(cut, t + 1)
                wait_reuse(pe, gru.inp_ready, t)
                for m in range(NT):
                    mm = nc.tensor.matmul(ps_a[s][:, 0:D], at[0:rows_of(m), s, m, :], h[0:rows_of(m), m, :],
                                          start=(m == 0), stop=(m == NT - 1))
                mm.then_inc(agg, 1)
                pe.wait_ge(pos_done, t + 1)
                pe.wait_ge(neg_done, t + 1)
                wait_reuse(pe, sum_done, t)
                for g in range(2):
                    for m in range(NT):
                        mm = nc.tensor.matmul(ps_e[s][:, g * 3 * J:(g + 1) * 3 * J], sign[0:rows_of(m), s, g, m, :],
                                              u3[0:rows_of(m), m, :, :].rearrange("p j c -> p (j c)"),
                                              start=(m == 0), stop=(m == NT - 1))
                mm.then_inc(e_mul, 1)
                if not (isinstance(t, int) and t == 0):
                    gru.pe_gates(pe, t - 1, 1 - s)
                gru.pe_turn(pe, t, s)
            pe.wait_ge(gru.w_in, 64)
            over_tiles(pe, body)
            pe.wait_ge(e_done, NT)
            for j in range(2):
                mm = nc.tensor.transpose(ps_e[0][0:COLUMNS // 2, j * P:(j + 1) * P],
                                         e[:, :, :, :].rearrange("p i g t -> p (i g t)")[:, j * COLUMNS // 2:(j + 1) * COLUMNS // 2],
                                         k.ident[:, :])
            mm.then_inc(e_turned, 1)
            gru.pe_gates(pe, NT - 1, 1)

        @block.scalar
        def _(act):
            def body(t, s):
                act.wait_ge(agg, t + 1)
                wait_reuse(act, gru.turned, t)
                nc.scalar.activation(gru.inp[:, s, :], ps_a[s][:, 0:D], ACT.Copy).then_inc(gru.inp_ready, 1)
                if not (isinstance(t, int) and t == 0):
                    gru.act_gates(act, t - 1, 1 - s)
                    gru.act_candidate(act, t - 1, 1 - s)
                gru.act_keep(act, t, s)
            over_tiles(act, body)
            act.wait_ge(e_turned, 1)
            nc.scalar.activation(e_rows[:, :, :].rearrange("p j n -> p (j n)"), ps_e[0][0:COLUMNS // 2, 0:2 * P],
                                 ACT.Copy).then_inc(e_kept, 1)
            gru.act_gates(act, NT - 1, 1)
            gru.act_candidate(act, NT - 1, 1)

        @block.vector
        def _(dve):
            def prepare(t, s):
                wait_in(dve, at_in[s], t, s)
                nc.vector.tensor_tensor(at[:, s, at_tile(t), :], at[:, s, at_tile(t), :], k.offdiag[:, :].unsqueeze(1),
                                        ALU.mult).then_inc(cut, 1)
                dve.wait_ge(cut, t + 1)
                wait_reuse(dve, e_mul, t)
                nc.vector.tensor_scalar(sign[:, s, 0, :, :], at[:, s, :, :], 0.0, None, ALU.is_gt).then_inc(pos_done, 1)
                nc.vector.tensor_scalar(sign[:, s, 1, :, :], at[:, s, :, :], 0.0, None, ALU.is_lt).then_inc(neg_done, 1)

            def logits(t, s):
                dve.wait_ge(e_mul, t + 1)
                nc.vector.reduce_sum(sums[:, s, :, :], ps_e[s][:, 0:6 * J].rearrange("p (g j c) -> p g j c", g=2, j=J),
                                     AX.X).then_inc(sum_done, 1)
                dve.wait_ge(sum_done, t + 1)
                by = sums[:, s, :, :].rearrange("p g (i a) -> p g i a", a=2)
                nc.vector.tensor_tensor(pre[:, s, :, 0], by[:, 0, :, 0], by[:, 1, :, 1], ALU.add).then_inc(plus_done, 1)
                nc.vector.tensor_tensor(pre[:, s, :, 1], by[:, 1, :, 0], by[:, 0, :, 1], ALU.add).then_inc(minus_done, 1)
                dve.wait_ge(plus_done, t + 1)
                dve.wait_ge(minus_done, t + 1)
                nc.vector.scalar_tensor_tensor(out=e[:, :, :, at_tile(t)], in0=pre[:, s, :, :].unsqueeze(3), scalar=SLOPE,
                                               in1=pre[:, s, :, :].unsqueeze(3), op0=ALU.mult, op1=ALU.max).then_inc(e_done, 1)

            def body(t, s):
                if not last(t):
                    prepare(t + 1, 1 - s)
                if not (isinstance(t, int) and t == 0):
                    gru.dve(dve, t - 1, 1 - s)
                logits(t, s)
            gru.biases(dve)
            prepare(0, 0)
            over_tiles(dve, body)
            gru.dve(dve, NT - 1, 1)


def signed_attend(nc, k, ins, i, v_dram, e_dram, es):
    with Phase(nc, f"sg{i}_at") as ph:
        rows = ph.sb("rows", [P, 2, NP])
        v = ph.sb("v", [P, NT, D])
        rows_in, v_in = [ph.sem(f"rows_in{g}") for g in range(2)], ph.sem("v_in")
        a = ph.sb("a", [P, 2, N])
        pos = ph.sb("pos", [P, N], mybir.dt.uint8)
        mask = ph.sb("mask", [P, N], BF16)
        z = ph.sb("z", [P, 2, NP])
        pT = ph.sb("pT", [P, 2, NP])
        neg_max = ph.sb("neg_max", [P, 2])
        row_max = ph.sb("row_max", [P, 2])
        den = ph.sb("den", [P, NT])
        den_safe = ph.sb("den_safe", [P, NT])
        inv = ph.sb("inv", [P, NT])
        ps_p = [ph.ps(f"ps_p{c}", [P, 1024]) for c in range(3)]
        ps_o = [ph.ps(f"ps_o{s}", [P, 512]) for s in range(2)]
        a_in = [ph.sem(f"a_in{s}") for s in range(2)]
        pad_done, cut, pos_done, mask_done, base_done, chosen = (
            ph.sem(n) for n in ("pad_done", "cut", "pos_done", "mask_done", "base_done", "chosen"))
        max_done, neg_done, p_done, scaled, turned, pT_done, pv_done = (
            ph.sem(n) for n in ("max_done", "neg_done", "p_done", "scaled", "turned", "pT_done", "pv_done"))
        safe_done, inv_done, es_done = (ph.sem(n) for n in ("safe_done", "inv_done", "es_done"))
        block = ph.block()

        def inside(t, by):
            return not isinstance(t, int) or 0 <= t + by < NT

        @block.sync
        def _(sp):
            def body(t, s):
                wait_reuse(sp, scaled, t)
                sp.dma_start(a[:, s, :], ins["a_rows"][at_tile(t), :, :]).then_inc(a_in[s], 16)
                if isinstance(t, int) and t == 0:
                    for g in (1, 0):
                        sp.dma_start(rows[:, g, :], e_dram[(2 * i + g) * NT:(2 * i + g + 1) * NT, :].rearrange(
                            "t n -> (t n)").partition_broadcast(P)).then_inc(rows_in[g], 16)
                if isinstance(t, int) and t == 1:
                    sp.dma_start(v[:, :, :], v_dram[i]).then_inc(v_in, 16)
            over_tiles(sp, body)

        @block.gpsimd
        def _(pool):
            nc.gpsimd.memset(z[:, :, N:NP], 0.0).then_inc(pad_done, 1)

        @block.scalar
        def _(act):
            def base(t, s):
                wait_count(act, turned, t, 3, 3 - 6)
                nc.scalar.activation(z[:, s, 0:N], rows[:, 1, 0:N], ACT.Copy).then_inc(base_done, 1)

            def exps(t, s):
                act.wait_ge(neg_done, t + 1)
                nc.scalar.activation(z[:, s, 0:N], z[:, s, 0:N], ACT.Exp, bias=neg_max[:, s:s + 1],
                                     accum_out=den[:, at_tile(t)]).then_inc(p_done, 1)

            def evacuate(t, s):
                wait_reuse(act, pv_done, t)
                for c, (m0, n) in enumerate(CHUNKS):
                    wait_count(act, turned, t, 3, c + 1)
                    nc.scalar.activation(pT[:, s, m0 * P:(m0 + n) * P], ps_p[c][:, 0:n * P],
                                         ACT.Copy).then_inc(pT_done, 1)

            def body(t, s):
                evacuate(t, s)
                if inside(t, 2):
                    base(t + 2, s)
                if inside(t, 1):
                    exps(t + 1, 1 - s)
            act.wait_ge(rows_in[1], 16)
            base(0, 0)
            base(1, 1)
            exps(0, 0)
            loop_ahead(act, body)

        @block.tensor
        def _(pe):
            def turn(t, s):
                pe.wait_ge(scaled, t + 1)
                for c, (m0, n) in enumerate(CHUNKS):
                    wait_count(pe, pT_done, t, 3, c + 1 - 3)
                    for m in range(m0, m0 + n):
                        mm = nc.tensor.transpose(ps_p[c][:, (m - m0) * P:(m - m0 + 1) * P],
                                                 z[:, s, m * P:(m + 1) * P], k.ident[:, :])
                    mm.then_inc(turned, 1)

            def body(t, s):
                if not last(t):
                    turn(t + 1, 1 - s)
                wait_reuse(pe, es_done, t)
                for c, (m0, n) in enumerate(CHUNKS):
                    wait_count(pe, pT_done, t, 3, c + 1)
                    for m in range(m0, m0 + n):
                        mm = nc.tensor.matmul(ps_o[s][:, 0:D], pT[:, s, m * P:(m + 1) * P], v[:, m, :],
                                              start=(m == 0), stop=(m == NT - 1))
                mm.then_inc(pv_done, 1)
            pe.wait_ge(pad_done, 1)
            turn(0, 0)
            pe.wait_ge(v_in, 16)
            over_tiles(pe, body)

        @block.vector
        def _(dve):
            def masks(t, s):
                wait_in(dve, a_in[s], t, s)
                if isinstance(t, int) and t == NT - 1:
                    block_diag, off = a[:, s, t * P:N], k.offdiag[:, 0:N - t * P]
                else:
                    block_diag, off = a[:, s, bass.ds(t * P, P)], k.offdiag[:, :]
                nc.vector.tensor_tensor(block_diag, block_diag, off, ALU.mult).then_inc(cut, 1)
                dve.wait_ge(cut, t + 1)
                wait_reuse(dve, chosen, t, depth=1)
                nc.vector.tensor_scalar(pos[:, :], a[:, s, :], 0.0, None, ALU.is_gt).then_inc(pos_done, 1)
                wait_reuse(dve, max_done, t, depth=1)
                nc.vector.tensor_scalar(mask[:, :], a[:, s, :], 0.0, -BIG, ALU.is_equal, ALU.mult).then_inc(mask_done, 1)

            def logits(t, s):
                dve.wait_ge(base_done, t + 1)
                wait_apart(dve, pos_done, t, 1, 1)
                nc.vector.copy_predicated(z[:, s, 0:N], pos[:, :], rows[:, 0, 0:N]).then_inc(chosen, 1)
                dve.wait_ge(mask_done, t + 1)
                wait_apart(dve, chosen, t, 1, 1)
                nc.vector.tensor_tensor_reduce(out=z[:, s, 0:N], in0=z[:, s, 0:N], in1=mask[:, :], scale=1.0,
                                               scalar=-2 * BIG, op0=ALU.add, op1=ALU.max,
                                               accum_out=row_max[:, s:s + 1]).then_inc(max_done, 1)
                dve.wait_ge(max_done, t + 1)
                nc.vector.tensor_scalar(neg_max[:, s:s + 1], row_max[:, s:s + 1], FLOOR, -1.0, ALU.max,
                                        ALU.mult).then_inc(neg_done, 1)

            def scale(t, s):
                dve.wait_ge(p_done, t + 1)
                nc.vector.tensor_tensor(z[:, s, 0:N], z[:, s, 0:N], a[:, s, :], ALU.mult).then_inc(scaled, 1)

            def finish(t, s):
                nc.vector.tensor_scalar(den_safe[:, at_tile(t)], den[:, at_tile(t)], 0.5, float(HEADS), ALU.max,
                                        ALU.mult).then_inc(safe_done, 1)
                dve.wait_ge(safe_done, t + 1)
                nc.vector.reciprocal(inv[:, at_tile(t)], den_safe[:, at_tile(t)]).then_inc(inv_done, 1)
                dve.wait_ge(inv_done, t + 1)
                dve.wait_ge(pv_done, t + 1)
                if i == 0:
                    nc.vector.tensor_scalar(es[:, at_tile(t), :], ps_o[s][:, 0:D].unsqueeze(1), inv[:, at_tile(t)], None,
                                            ALU.mult).then_inc(es_done, 1)
                else:
                    nc.vector.scalar_tensor_tensor(out=es[:, at_tile(t), :], in0=ps_o[s][:, 0:D].unsqueeze(1),
                                                   scalar=inv[:, at_tile(t)], in1=es[:, at_tile(t), :],
                                                   op0=ALU.mult, op1=ALU.add).then_inc(es_done, 1)

            def body(t, s):
                if inside(t, 1):
                    logits(t + 1, 1 - s)
                if inside(t, -2):
                    finish(t - 2, s)
                if inside(t, 2):
                    masks(t + 2, s)
                if inside(t, 1):
                    scale(t + 1, 1 - s)
            masks(0, 0)
            dve.wait_ge(rows_in[0], 16)
            logits(0, 0)
            masks(1, 1)
            scale(0, 0)
            loop_ahead(dve, body)
            finish(NT - 2, 0)
            finish(NT - 1, 1)


def signed_node(nc, k, ins, h, es):
    with Phase(nc, "sg_node") as ph:
        gru = Gru(nc, k, ph, ins, "node", h, depth=2)
        block = ph.block()

        @block.sync
        def _(sp):
            gru.load(sp)

        @block.gpsimd
        def _(pool):
            def body(t, s):
                wait_reuse(pool, gru.turned, t)
                nc.gpsimd.tensor_copy(gru.hid[:, s, :].unsqueeze(1), h[:, at_tile(t), :]).then_inc(gru.hid_ready, 1)
            over_tiles(pool, body)

        @block.tensor
        def _(pe):
            def body(t, s):
                if not last(t):
                    gru.pe_turn(pe, t + 1, 1 - s)
                gru.pe_gates(pe, t, s)
            pe.wait_ge(gru.w_in, 64)
            gru.pe_turn(pe, 0, 0)
            over_tiles(pe, body)

        @block.scalar
        def _(act):
            def fixed(t, s):
                wait_reuse(act, gru.turned, t)
                nc.scalar.activation(gru.inp[:, s, :].unsqueeze(1), es[:, at_tile(t), :], ACT.Copy).then_inc(gru.inp_ready, 1)

            def body(t, s):
                if not last(t):
                    fixed(t + 1, 1 - s)
                    gru.act_keep(act, t + 1, 1 - s)
                gru.act_gates(act, t, s)
                gru.act_candidate(act, t, s)
            fixed(0, 0)
            gru.act_keep(act, 0, 0)
            over_tiles(act, body)

        @block.vector
        def _(dve):
            gru.biases(dve)
            over_tiles(dve, lambda t, s: gru.dve(dve, t, s))


def masked_attention(nc, k, ins):
    H, O = 4, D // 4
    with Phase(nc, "ma") as keep:
        qT = keep.sb("qT", [P, C, NP])
        kT = keep.sb("kT", [P, C, NP])
        v = keep.sb("v", [P, NT, D])
        masked_in(nc, k, ins, qT, kT, v, H, O)
        masked_attend(nc, k, ins, qT, kT, v, H, O)


def masked_in(nc, k, ins, qT, kT, v, H, O):
    with Phase(nc, "ma_in") as ph:
        w = ph.sb("w", [P, C, 3 * D])
        b_col = ph.sb("b_col", [P, 2, C])
        b_v = ph.sb("b_v", [P, D])
        hs = ph.sb("hs", [P, 2, D])
        hT = ph.sb("hT", [P, 2, D])
        ps_t = [ph.ps(f"ps_t{s}", [P, 512]) for s in range(2)]
        ps_qk = [[ph.ps(f"ps_{n}{s}", [P, 512]) for s in range(2)] for n in "qk"]
        ps_v = [ph.ps(f"ps_v{s}", [P, 512]) for s in range(2)]
        w_in, h_done, turned, hT_done, qk_mul, v_mul, q_done, k_done, v_done = (
            ph.sem(n) for n in ("w_in", "h_done", "turned", "hT_done", "qk_mul", "v_mul", "q_done", "k_done", "v_done"))
        block = ph.block()

        @block.sync
        def _(sp):
            sp.dma_start(w[:, :, :], ins["w3"]).then_inc(w_in, 16)
            sp.dma_start(b_col[:, :, :], ins["b3_col"]).then_inc(w_in, 16)
            sp.dma_start(b_v[:, :], ins["b3_v"]).then_inc(w_in, 16)

        @block.scalar
        def _(act):
            def normed(t, s):
                wait_reuse(act, turned, t)
                nc.scalar.activation(hs[:, s, :], k.x[:, at_tile(t), :], ACT.Relu,
                                     bias=k.nmr[:, at_tile(t)], scale=k.rstd[:, at_tile(t)]).then_inc(h_done, 1)

            def body(t, s):
                if not last(t):
                    normed(t + 1, 1 - s)
                act.wait_ge(qk_mul, t + 1)
                for c in range(C):
                    ins_ = nc.scalar.activation(kT[:, c, bass.ds(t * P, P)], ps_qk[1][s][:, c * P:(c + 1) * P],
                                                ACT.Identity, bias=b_col[:, 1, c:c + 1])
                ins_.then_inc(k_done, 1)
            normed(0, 0)
            act.wait_ge(w_in, 48)
            over_tiles(act, body)

        @block.tensor
        def _(pe):
            def turn(t, s):
                pe.wait_ge(h_done, t + 1)
                wait_reuse(pe, hT_done, t)
                for c in range(C):
                    mm = nc.tensor.transpose(ps_t[s][:, c * P:(c + 1) * P], hs[:, s, c * P:(c + 1) * P], k.ident[:, :])
                mm.then_inc(turned, 1)

            def body(t, s):
                if not last(t):
                    turn(t + 1, 1 - s)
                pe.wait_ge(hT_done, t + 1)
                wait_reuse(pe, q_done, t)
                wait_reuse(pe, k_done, t)
                for f in range(2 * C):
                    for c in range(C):
                        mm = nc.tensor.matmul(ps_qk[f // C][s][:, f % C * P:(f % C + 1) * P], w[:, c, f * P:(f + 1) * P],
                                              hT[:, s, c * P:(c + 1) * P], start=(c == 0), stop=(c == C - 1))
                mm.then_inc(qk_mul, 1)
                wait_reuse(pe, v_done, t)
                for c in range(C):
                    mm = nc.tensor.matmul(ps_v[s][:, 0:D], hT[:, s, c * P:(c + 1) * P], w[:, c, 2 * D:3 * D],
                                          start=(c == 0), stop=(c == C - 1))
                mm.then_inc(v_mul, 1)
            turn(0, 0)
            pe.wait_ge(w_in, 48)
            over_tiles(pe, body)

        @block.vector
        def _(dve):
            dve.wait_ge(w_in, 48)

            def body(t, s):
                dve.wait_ge(turned, t + 1)
                wait_reuse(dve, v_mul, t)
                nc.vector.tensor_copy(hT[:, s, :], ps_t[s][:, 0:D]).then_inc(hT_done, 1)
                dve.wait_ge(qk_mul, t + 1)
                for c in range(C):
                    ins_ = nc.vector.tensor_scalar(qT[:, c, bass.ds(t * P, P)], ps_qk[0][s][:, c * P:(c + 1) * P],
                                                   b_col[:, 0, c:c + 1], float(O) ** -0.5, ALU.add, ALU.mult)
                ins_.then_inc(q_done, 1)
                dve.wait_ge(v_mul, t + 1)
                nc.vector.tensor_tensor(v[:, at_tile(t), :], ps_v[s][:, 0:D].unsqueeze(1), b_v[:, :].unsqueeze(1),
                                        ALU.add).then_inc(v_done, 1)
            over_tiles(dve, body)


COLS = 512
PIECES = [(j * COLS, min(COLS, N - j * COLS)) for j in range((N + COLS - 1) // COLS)]
QUADS = [(m, min(4, NT - m)) for m in range(0, NT, 4)]
RING = 3


def masked_attend(nc, k, ins, qT, kT, v, H, O):
    NPC, NQ = len(PIECES), len(QUADS)
    assert NPC % RING == 0 and NQ % RING == 0
    with Phase(nc, "ma_at") as ph:
        a = ph.sb("a", [P, 2, N])
        mask = ph.sb("mask", [P, N], BF16)
        q = ph.sb("q", [P, 2, C, P])
        z = ph.sb("z", [P, 2, NP])
        pT = ph.sb("pT", [P, 2, NP])
        gb = ph.sb("gb", [P, 1])
        wo = ph.sb("wo", [P, C, D])
        b_o = ph.sb("b_o", [P, D])
        part_max = ph.sb("part_max", [P, 2, NPC])
        row_max = ph.sb("row_max", [P, 2])
        neg_max = ph.sb("neg_max", [P, 2])
        den = ph.sb("den", [P, 2, H])
        inv = ph.sb("inv", [P, 2, H])
        o = ph.sb("o", [P, 2, D])
        oT = ph.sb("oT", [P, 2, D])
        ps_s = [ph.ps(f"ps_s{r}", [P, COLS]) for r in range(RING)]
        ps_p = [ph.ps(f"ps_p{r}", [P, 4 * P]) for r in range(RING)]
        ps_o = [ph.ps(f"ps_o{s}", [P, 512]) for s in range(2)]
        a_in = [ph.sem(f"a_in{s}") for s in range(2)]
        (w_in, pad_done, xb_done, q_done, mask_done, bias_done, scored, summed, max_done, neg_done, p_done, turned) = (
            ph.sem(n) for n in ("w_in", "pad_done", "xb_done", "q_done", "mask_done", "bias_done", "scored", "summed",
                                "max_done", "neg_done", "p_done", "turned"))
        pT_act, pT_dve, pv_done, inv_done, o_done, o_turned, oT_done, out_done, x_done = (
            ph.sem(n) for n in ("pT_act", "pT_dve", "pv_done", "inv_done", "o_done", "o_turned", "oT_done", "out_done",
                                "x_done"))
        block = ph.block()

        def shifted(t, s, h, by):
            over, h = (h + by) // H, (h + by) % H
            if isinstance(t, int) and not 0 <= t + over < NT:
                return None
            return (t + over, (s + over) % 2, h) if over else (t, s, h)

        def do(stage, at):
            if at is not None:
                stage(*at)

        @block.sync
        def _(sp):
            sp.dma_start(gb[:, :], ins["gb"]).then_inc(w_in, 16)
            sp.dma_start(wo[:, :, :], ins["w_out"]).then_inc(w_in, 16)
            sp.dma_start(b_o[:, :], ins["b_out"]).then_inc(w_in, 16)

            def body(t, s):
                wait_count(sp, summed, t, H * NPC, H * NPC - 2 * H * NPC)
                sp.dma_start(a[:, s, :], ins["a_rows"][at_tile(t), :, :]).then_inc(a_in[s], 16)
            over_tiles(sp, body)

        @block.gpsimd
        def _(pool):
            nc.gpsimd.memset(z[:, :, N:NP], 0.0).then_inc(pad_done, 1)

            def body(t, s):
                wait_count(pool, scored, t, H * NPC, H * NPC - 2 * H * NPC)
                nc.gpsimd.tensor_copy(q[:, s, :, :], qT[:, :, bass.ds(t * P, P)]).then_inc(q_done, 1)
            over_tiles(pool, body)

        @block.scalar
        def _(act):
            def exps(t, s, h):
                wait_count(act, neg_done, t, H, h + 1)
                if h == 0:
                    wait_reuse(act, inv_done, t)
                nc.scalar.activation(z[:, h % 2, 0:N], z[:, h % 2, 0:N], ACT.Exp, bias=neg_max[:, h % 2:h % 2 + 1],
                                     accum_out=den[:, s, h:h + 1]).then_inc(p_done, 1)

            def evacuate(t, s, h):
                wait_count(act, pv_done, t, H, h + 1 - 2)
                for c in range(0, NQ, 2):
                    m0, n = QUADS[c]
                    wait_count(act, turned, t, NQ * H, NQ * h + c + 1)
                    nc.scalar.activation(pT[:, h % 2, m0 * P:(m0 + n) * P], ps_p[c % RING][:, 0:n * P],
                                         ACT.Copy).then_inc(pT_act, 1)

            def keep_o(t, s):
                act.wait_ge(o_turned, t + 1)
                wait_reuse(act, out_done, t)
                nc.scalar.activation(oT[:, s, :], ps_o[s][:, D:2 * D], ACT.Copy).then_inc(oT_done, 1)

            def body(t, s):
                for h in range(H):
                    exps(t, s, h)
                    evacuate(t, s, h)
                    if h == 2 and not (isinstance(t, int) and t == 0):
                        keep_o(t - 1, 1 - s)
            over_tiles(act, body)
            keep_o(NT - 1, 1)

        @block.tensor
        def _(pe):
            def scores(t, s, h):
                if h == 0:
                    pe.wait_ge(q_done, t + 1)
                rows = slice((h % 2) * O, (h % 2 + 1) * O)
                for j, (c0, n) in enumerate(PIECES):
                    wait_count(pe, summed, t, H * NPC, NPC * h + j + 1 - RING)
                    nc.tensor.matmul(ps_s[j % RING][:, 0:n], q[rows, s, h // 2, :], kT[rows, h // 2, c0:c0 + n],
                                     start=True, stop=True).then_inc(scored, 1)

            def done_before(c):
                b = c - RING
                return (b + 1) // 2 if b % 2 else b // 2 + 1

            def turn(t, s, h):
                wait_count(pe, p_done, t, H, h + 1)
                for c, (m0, n) in enumerate(QUADS):
                    wait_count(pe, pT_act if c % 2 else pT_dve, t, (NQ // 2) * H, (NQ // 2) * h + done_before(c))
                    for m in range(m0, m0 + n):
                        mm = nc.tensor.transpose(ps_p[c % RING][:, (m - m0) * P:(m - m0 + 1) * P],
                                                 z[:, h % 2, m * P:(m + 1) * P], k.ident[:, :])
                    mm.then_inc(turned, 1)

            def values(t, s, h):
                wait_count(pe, pT_act, t, (NQ // 2) * H, (NQ // 2) * (h + 1))
                wait_count(pe, pT_dve, t, (NQ // 2) * H, (NQ // 2) * (h + 1))
                if h == 0:
                    wait_reuse(pe, x_done, t)
                for m in range(NT):
                    mm = nc.tensor.matmul(ps_o[s][:, h * O:(h + 1) * O], pT[:, h % 2, m * P:(m + 1) * P],
                                          v[:, m, h * O:(h + 1) * O], start=(m == 0), stop=(m == NT - 1))
                mm.then_inc(pv_done, 1)

            def turn_o(t, s):
                pe.wait_ge(o_done, t + 1)
                for c in range(C):
                    mm = nc.tensor.transpose(ps_o[s][:, D + c * P:D + (c + 1) * P], o[:, s, c * P:(c + 1) * P], k.ident[:, :])
                mm.then_inc(o_turned, 1)

            def project(t, s):
                pe.wait_ge(oT_done, t + 1)
                for c in range(C):
                    mm = nc.tensor.matmul(ps_o[s][:, 0:D], oT[:, s, c * P:(c + 1) * P], wo[:, c, :],
                                          start=(c == 0), stop=(c == C - 1))
                mm.then_inc(out_done, 1)

            def body(t, s):
                for h in range(H):
                    do(scores, shifted(t, s, h, 1))
                    turn(t, s, h)
                    do(values, shifted(t, s, h, -1))
                    if h == 1 and not (isinstance(t, int) and t == 0):
                        turn_o(t - 1, 1 - s)
                    if h == 2 and not (isinstance(t, int) and t == 0):
                        project(t - 1, 1 - s)
            pe.wait_ge(w_in, 48)
            pe.wait_ge(pad_done, 1)
            scores(0, 0, 0)
            over_tiles(pe, body)
            values(NT - 1, 1, H - 1)
            turn_o(NT - 1, 1)
            project(NT - 1, 1)

        @block.vector
        def _(dve):
            def bias(t, s):
                wait_in(dve, a_in[s], t, s)
                wait_reuse(dve, bias_done, t, depth=1)
                nc.vector.tensor_scalar(mask[:, :], a[:, s, :], 0.0, -BIG, ALU.is_equal, ALU.mult).then_inc(mask_done, 1)
                dve.wait_ge(mask_done, t + 1)
                nc.vector.scalar_tensor_tensor(out=a[:, s, :], in0=a[:, s, :], scalar=gb[:, 0:1], in1=mask[:, :],
                                               op0=ALU.mult, op1=ALU.add).then_inc(bias_done, 1)

            def logits(t, s, h):
                if h == 0:
                    bias(t, s)
                    dve.wait_ge(bias_done, t + 1)
                wait_count(dve, turned, t, NQ * H, NQ * (h + 1 - 2))
                for j, (c0, n) in enumerate(PIECES):
                    wait_apart(dve, scored, t, H * NPC, NPC * h + j + 1)
                    nc.vector.tensor_tensor_reduce(out=z[:, h % 2, c0:c0 + n], in0=ps_s[j % RING][:, 0:n],
                                                   in1=a[:, s, c0:c0 + n], scale=1.0, scalar=-2 * BIG, op0=ALU.add,
                                                   op1=ALU.max, accum_out=part_max[:, h % 2, j:j + 1]).then_inc(summed, 1)
                wait_count(dve, summed, t, H * NPC, NPC * (h + 1))
                nc.vector.reduce_max(row_max[:, h % 2:h % 2 + 1], part_max[:, h % 2, :], AX.X).then_inc(max_done, 1)
                wait_count(dve, max_done, t, H, h + 1)
                nc.vector.tensor_scalar(neg_max[:, h % 2:h % 2 + 1], row_max[:, h % 2:h % 2 + 1], -1.0, None,
                                        ALU.mult).then_inc(neg_done, 1)

            def evacuate(t, s, h):
                wait_count(dve, pv_done, t, H, h + 1 - 2)
                for c in range(1, NQ, 2):
                    m0, n = QUADS[c]
                    wait_count(dve, turned, t, NQ * H, NQ * h + c + 1)
                    nc.vector.tensor_copy(pT[:, h % 2, m0 * P:(m0 + n) * P], ps_p[c % RING][:, 0:n * P]).then_inc(pT_dve, 1)

            def normalise(t, s):
                wait_count(dve, p_done, t, H, H)
                nc.vector.reciprocal(inv[:, s, :], den[:, s, :]).then_inc(inv_done, 1)
                dve.wait_ge(inv_done, t + 1)
                wait_count(dve, pv_done, t, H, H)
                wait_reuse(dve, o_turned, t)
                nc.vector.tensor_tensor(o[:, s, :].rearrange("p (h o) -> p h o", h=H),
                                        ps_o[s][:, 0:D].rearrange("p (h o) -> p h o", h=H),
                                        inv[:, s, :].unsqueeze(2).to_broadcast([P, H, O]), ALU.mult).then_inc(o_done, 1)

            def finish(t, s):
                dve.wait_ge(out_done, t + 1)
                nc.vector.tensor_tensor(k.x[:, at_tile(t), :], k.x[:, at_tile(t), :], ps_o[s][:, 0:D].unsqueeze(1),
                                        ALU.add).then_inc(x_done, 1)
                dve.wait_ge(x_done, t + 1)
                nc.vector.tensor_tensor(k.x[:, at_tile(t), :], k.x[:, at_tile(t), :], b_o[:, :].unsqueeze(1),
                                        ALU.add).then_inc(xb_done, 1)

            def body(t, s):
                for h in range(H):
                    do(logits, shifted(t, s, h, 1))
                    evacuate(t, s, h)
                    if h == 0 and not (isinstance(t, int) and t == 0):
                        normalise(t - 1, 1 - s)
                    if h == 3 and not (isinstance(t, int) and t == 0):
                        finish(t - 1, 1 - s)
            dve.wait_ge(w_in, 48)
            logits(0, 0, 0)
            over_tiles(dve, body)
            normalise(NT - 1, 1)
            finish(NT - 1, 1)


class Kept:
    pass


def program(nc, ins, out):
    k = Kept()
    with ExitStack() as ctx:
        def sb(name, shape, dt=F32):
            return ctx.enter_context(nc.sbuf_tensor(name, shape, dt))
        k.x = sb("x", [P, NT, D])
        k.ident = sb("ident", [P, P])
        k.offdiag = sb("offdiag", [P, P])
        k.ones = sb("ones", [P, P])
        k.eps = sb("eps", [P, 1])
        k.dis = sb("dis", [P, NT])
        k.diag = sb("diag", [P, NT])
        k.rstd = sb("rstd", [P, NT])
        k.nmr = sb("nmr", [P, NT])
        load_constants(nc, k, ins)
        degrees(nc, k, ins)
        norm_stats(nc, k, 0)
        gcn(nc, k, ins)
        norm_stats(nc, k, 1)
        gat(nc, k, ins)
        norm_stats(nc, k, 2)
        signed_gat(nc, k, ins)
        norm_stats(nc, k, 3)
        masked_attention(nc, k, ins)
        with Phase(nc, "store") as ph:
            stored = ph.sem("stored")
            block = ph.block()

            @block.sync
            def _(sp):
                sp.dma_start(out, k.x[:, :, :]).then_inc(stored, 16)
                sp.wait_ge(stored, 16)


def kernel(**inputs):
    import numpy as np
    import concourse.bacc as bacc
    from concourse.bass_utils import run_bass_kernel_spmd

    x, adj = np.asarray(inputs["x"]), np.asarray(inputs["adj"])

    def rows(a, width):
        return np.ascontiguousarray(np.asarray(a).reshape(-1, P, width).transpose(1, 0, 2))

    def spread(a):
        a = np.asarray(a).reshape(1, -1)
        return np.ascontiguousarray(np.broadcast_to(a, (P, a.shape[1])))

    def stack(*vectors):
        return np.ascontiguousarray(np.stack([spread(v) for v in vectors], axis=1))

    adj_rows = np.zeros((NP, N), adj.dtype)
    adj_rows[:N] = adj
    adj_sq = np.zeros((NP, NP), adj.dtype)
    adj_sq[:N, :N] = adj
    x_pad = np.zeros((NP, D), x.dtype)
    x_pad[:N] = x
    arrays = {
        "x": rows(x_pad, D),
        "a_rows": adj_rows.reshape(NT, P, N),
        "at": np.ascontiguousarray(adj_sq.reshape(NT, P, NT, P).transpose(0, 3, 2, 1)).reshape(NT, P, NP),
        "w0": rows(inputs["L0_gnn_W"], D),
        "b0": spread(inputs["L0_gnn_b"]),
        "w1": rows(inputs["L1_gnn_weight"], D),
        "pw1": rows(np.asarray(inputs["L1_gnn_proj_w"]).T, D),
        "uv1": stack(inputs["L1_gnn_weight_u"], inputs["L1_gnn_weight_v"]),
        "b1": stack(inputs["L1_gnn_bias"], inputs["L1_gnn_proj_b"]),
    }
    diag = np.zeros((NP,), adj.dtype)
    diag[:N] = np.diagonal(adj)
    arrays["diag"] = np.ascontiguousarray(diag.reshape(NT, P).T)
    gat_w = np.asarray(inputs["L2_gnn_gat_W"])
    arrays["w2"] = np.ascontiguousarray(gat_w.reshape(HEADS, C, P, D).transpose(2, 0, 1, 3))
    gat_a = np.asarray(inputs["L2_gnn_gat_a"]).reshape(1, HEADS, 2, D)
    arrays["a2"] = np.ascontiguousarray(np.broadcast_to(gat_a, (P, HEADS, 2, D)))
    for cell in ("edge", "node"):
        for part in ("ih", "hh"):
            arrays[f"{cell}_w{part}"] = rows(np.asarray(inputs[f"L2_gnn_{cell}_W{part}"]).T, 3 * D)
            arrays[f"{cell}_b{part}"] = spread(inputs[f"L2_gnn_{cell}_b{part}"])
    arrays["w3"] = rows(inputs["L3_gnn_Wqkv"], 3 * D)
    bqkv = np.asarray(inputs["L3_gnn_bqkv"])
    arrays["b3_col"] = np.ascontiguousarray(bqkv[:2 * D].reshape(2, C, P).transpose(2, 0, 1))
    arrays["b3_v"] = spread(bqkv[2 * D:])
    arrays["gb"] = spread(inputs["L3_gnn_graph_bias"])
    arrays["w_out"] = rows(inputs["L3_gnn_Wout"], D)
    arrays["b_out"] = spread(inputs["L3_gnn_bout"])
    nc = bacc.Bacc("TRN2", target_bir_lowering=False, num_devices=1)
    ins = {n: nc.dram_tensor(f"in_{n}", a.shape, mybir.dt.from_np(a.dtype), kind="ExternalInput").ap()
           for n, a in arrays.items()}
    out = nc.dram_tensor("out_x", (P, NT, D), F32, kind="ExternalOutput").ap()
    program(nc, ins, out)
    r = run_bass_kernel_spmd(nc, [{f"in_{n}": a for n, a in arrays.items()}], core_ids=[0])
    got = r.results[0]["out_x"]
    return np.ascontiguousarray(got.transpose(1, 0, 2).reshape(NP, D)[:N])
```

```python
from contextlib import ExitStack

import concourse.bass as bass
from concourse import mybir

F32 = mybir.dt.float32
BF16 = mybir.dt.bfloat16
ALU = mybir.AluOpType
ACT = mybir.ActivationFunctionType
AX = mybir.AxisListType

P = 128
N = 2708
NT = (N + P - 1) // P
NP = NT * P
TAIL = N - (NT - 1) * P
D = 256
C = D // P
EPS = 1e-5
HEADS = 3


def rows_of(m):
    return P if m < NT - 1 else TAIL


def over_tiles(eng, body):
    body(0, 0)
    body(1, 1)
    with eng.Fori(1, NT // 2 - 1) as i:
        body(i * 2, 0)
        body(i * 2 + 1, 1)
    body(NT - 2, 0)
    body(NT - 1, 1)


def loop_ahead(eng, body):
    body(0, 0)
    body(1, 1)
    with eng.Fori(1, NT // 2 - 2) as i:
        body(i * 2, 0)
        body(i * 2 + 1, 1)
    for t in range(NT - 4, NT):
        body(t, t % 2)


def inside(t, by):
    return not isinstance(t, int) or 0 <= t + by < NT


def prefetch(sp, slots, tiles, loaded):
    for t in range(2):
        sp.dma_start(slots[:, t, :], tiles[t]).then_inc(loaded[t], 16)


def prefetched(t):
    return isinstance(t, int) and t < 2


def wait_reuse(eng, sem, t, per=1, depth=2):
    if isinstance(t, int):
        if t >= depth:
            eng.wait_ge(sem, (t - depth + 1) * per)
    else:
        eng.wait_ge(sem, t * per + (1 - depth) * per)


def at_tile(t, width=1):
    return bass.ds(t * width, width)


class Phase:

    def __init__(self, nc, name):
        self.nc, self.name, self.ctx, self.sems = nc, name, ExitStack(), []

    def __enter__(self):
        return self

    def __exit__(self, *a):
        said = self.ctx.__exit__(*a)
        if self.sems and a[0] is None:
            self.nc.clear_and_free_semaphores(self.sems)
            self.nc.all_engine_barrier()
        return said

    def sb(self, name, shape, dt=F32):
        return self.ctx.enter_context(self.nc.sbuf_tensor(f"{self.name}_{name}", shape, dt))

    def ps(self, name, shape, dt=F32):
        return self.ctx.enter_context(self.nc.psum_tensor(f"{self.name}_{name}", shape, dt))

    def sem(self, name):
        self.sems.append(self.nc.alloc_semaphore(f"{self.name}_{name}"))
        return self.sems[-1]

    def block(self):
        return self.ctx.enter_context(self.nc.Block())


def load_constants(nc, k, ins):
    with Phase(nc, "const") as ph:
        zero_done, ident_done, x_in = ph.sem("zero_done"), ph.sem("ident_done"), ph.sem("x_in")
        block = ph.block()

        @block.gpsimd
        def _(pool):
            nc.gpsimd.memset(k.ident[:, :], 0.0).then_inc(zero_done, 1)
            nc.gpsimd.memset(k.offdiag[:, :], 1.0).then_inc(zero_done, 1)
            nc.gpsimd.memset(k.ones[:, :], 1.0)
            nc.gpsimd.memset(k.eps[:, :], EPS)
            pool.wait_ge(zero_done, 2)
            nc.gpsimd.affine_select(out=k.ident[:, :], in_=k.ident[:, :], compare_op=ALU.not_equal,
                                    fill=1.0, base=0, pattern=[[-1, P]], channel_multiplier=1)
            nc.gpsimd.affine_select(out=k.offdiag[:, :], in_=k.offdiag[:, :],
                                    compare_op=ALU.not_equal, fill=0.0, base=0,
                                    pattern=[[-1, P]], channel_multiplier=1)

        @block.sync
        def _(sp):
            sp.dma_start(k.x[:, :, :], ins["x"]).then_inc(x_in, 16)
            sp.dma_start(k.diag[:, :], ins["diag"]).then_inc(x_in, 16)
            sp.wait_ge(x_in, 32)


def node_stats(nc, k, t):
    return nc.vector.bn_stats(k.bn[:, at_tile(t), :].rearrange("p a f -> p (a f)"),
                              k.x[:, at_tile(t), :].rearrange("p a d -> p (a d)"))


class Stats:

    def __init__(self, nc, k, ph, summed=False):
        self.nc, self.k, self.summed = nc, k, summed
        self.mv = ph.sb("mv", [P, NT, 2])
        self.root = ph.sb("sd", [P, NT])
        self.bn_done, self.mv_done, self.rooted = ph.sem("bn_done"), ph.sem("mv_done"), ph.sem("sd_done")
        self.rstd_done, self.done = ph.sem("rstd_done"), ph.sem("stats_done")

    def on_dve(self, dve):
        k, v = self.k, self.nc.vector
        if not self.summed:
            for t in range(NT):
                node_stats(self.nc, k, t).then_inc(self.bn_done, 1)
        for t in range(NT):
            if not self.summed:
                dve.wait_ge(self.bn_done, t + 1)
            v.bn_aggr(self.mv[:, t, :], k.bn[:, t, :]).then_inc(self.mv_done, 1)
        dve.wait_ge(self.rooted, 1)
        v.reciprocal(k.rstd[:, :], self.root[:, :]).then_inc(self.rstd_done, 1)
        dve.wait_ge(self.rstd_done, 1)
        v.scalar_tensor_tensor(out=k.nmr[:, :], in0=self.mv[:, :, 0], scalar=-1.0, in1=k.rstd[:, :],
                               op0=ALU.mult, op1=ALU.mult).then_inc(self.done, 1)

    def on_act(self, act):
        act.wait_ge(self.mv_done, NT)
        self.nc.scalar.activation(self.root[:, :], self.mv[:, :, 1], ACT.Sqrt,
                                  bias=self.k.eps[:, 0:1]).then_inc(self.rooted, 1)


def gcn(nc, k, ins):
    with Phase(nc, "gcn") as keep:
        support = keep.sb("support", [P, NT, D])
        at = keep.sb("at", [P, 2, NP])
        at_in = [keep.sem(f"at_in{s}") for s in range(2)]
        gcn_support(nc, k, ins, support, at, at_in)
        gcn_aggregate(nc, k, ins, support, at, at_in)


def gcn_support(nc, k, ins, support, at, at_in):
    R = 6
    with Phase(nc, "deg") as ph:
        a = ph.sb("a_rows", [P, R, N])
        deg = ph.sb("deg", [P, NT])
        root = ph.sb("root", [P, NT])
        w = ph.sb("w", [P, C, D])
        h = ph.sb("h", [P, 2, D])
        hT = ph.sb("hT", [P, 2, D])
        stats = Stats(nc, k, ph)
        ps_t = [ph.ps(f"ps_t{s}", [P, 512]) for s in range(2)]
        ps_o = [ph.ps(f"ps_o{s}", [P, 512]) for s in range(2)]
        w_in, h_done, turned, hT_done, mul_done, s_done = (
            ph.sem(n) for n in ("w_in", "h_done", "turned", "hT_done", "mul_done", "s_done"))
        row_in = [ph.sem(f"row_in{j}") for j in range(R)]
        act_sum, dve_sum, rooted, dis_done = (ph.sem(n) for n in ("act_sum", "dve_sum", "rooted", "dis_done"))
        block = ph.block()

        @block.sync
        def _(sp):
            sp.dma_start(w[:, :, :], ins["w0"]).then_inc(w_in, 16)
            for t in range(NT):
                if t >= R:
                    sp.wait_ge(dve_sum if t % 2 else act_sum, (t - R) // 2 + 1)
                sp.dma_start(a[:, t % R, :], ins["a_rows"][t]).then_inc(row_in[t % R], 16)
            prefetch(sp, at, ins["at"], at_in)

        @block.scalar
        def _(act):
            def normed(t):
                wait_reuse(act, turned, t)
                nc.scalar.activation(h[:, t % 2, :], k.x[:, t, :], ACT.Relu,
                                     bias=k.nmr[:, t:t + 1], scale=k.rstd[:, t:t + 1]).then_inc(h_done, 1)

            stats.on_act(act)
            act.wait_ge(stats.done, 1)
            for t in range(NT):
                normed(t)
                if t % 2 == 0:
                    act.wait_ge(row_in[t % R], 16 * (t // R + 1))
                    nc.scalar.activation(a[:, t % R, :], a[:, t % R, :], ACT.Copy,
                                         accum_out=deg[:, t:t + 1]).then_inc(act_sum, 1)
            act.wait_ge(act_sum, NT // 2)
            act.wait_ge(dve_sum, NT // 2)
            nc.scalar.activation(root[:, :], deg[:, :], ACT.Sqrt, bias=k.ones[:, 0:1]).then_inc(rooted, 1)

        @block.tensor
        def _(pe):
            def turn(t):
                pe.wait_ge(h_done, t + 1)
                wait_reuse(pe, hT_done, t)
                for c in range(C):
                    mm = nc.tensor.transpose(ps_t[t % 2][:, c * P:(c + 1) * P], h[:, t % 2, c * P:(c + 1) * P],
                                             k.ident[:, :])
                mm.then_inc(turned, 1)

            turn(0)
            pe.wait_ge(w_in, 16)
            for t in range(NT):
                if t < NT - 1:
                    turn(t + 1)
                pe.wait_ge(hT_done, t + 1)
                wait_reuse(pe, s_done, t)
                for c in range(C):
                    mm = nc.tensor.matmul(ps_o[t % 2][:, 0:D], hT[:, t % 2, c * P:(c + 1) * P], w[:, c, :],
                                          start=(c == 0), stop=(c == C - 1))
                mm.then_inc(mul_done, 1)

        @block.vector
        def _(dve):
            def fixed(t):
                dve.wait_ge(turned, t + 1)
                wait_reuse(dve, mul_done, t)
                nc.vector.tensor_copy(hT[:, t % 2, :], ps_t[t % 2][:, 0:D]).then_inc(hT_done, 1)

            stats.on_dve(dve)
            fixed(0)
            for t in range(NT):
                if t < NT - 1:
                    fixed(t + 1)
                if t % 2 == 1:
                    dve.wait_ge(row_in[t % R], 16 * (t // R + 1))
                    nc.vector.reduce_sum(deg[:, t:t + 1], a[:, t % R, :], AX.X).then_inc(dve_sum, 1)
                dve.wait_ge(mul_done, t + 1)
                nc.vector.tensor_copy(support[:, t, :], ps_o[t % 2][:, 0:D]).then_inc(s_done, 1)
            dve.wait_ge(rooted, 1)
            nc.vector.reciprocal(k.dis[:, :], root[:, :]).then_inc(dis_done, 1)
            dve.wait_ge(dis_done, 1)
            dve.wait_ge(s_done, NT)
            nc.vector.tensor_tensor(support[:, :, :], support[:, :, :],
                                    k.dis[:, :].unsqueeze(2).to_broadcast([P, NT, D]), ALU.mult)


def gcn_aggregate(nc, k, ins, support, at, at_in):
    J = 2 * HEADS
    with Phase(nc, "gcn_at") as ph:
        b = ph.sb("b", [P, D])
        u = ph.sb("u", [P, 2, D])
        w2 = ph.sb("w2", [P, HEADS, C, D])
        av = ph.sb("av", [P, HEADS, 2, D])
        prod = ph.sb("prod", [P, J, C, D])
        ps_a = [ph.ps(f"ps_a{s}", [P, 512]) for s in range(2)]
        b_in, w2_in, prod_done = ph.sem("b_in"), ph.sem("w2_in"), ph.sem("prod_done")
        agg, own, biased, relued, x_done = (ph.sem(n) for n in ("agg", "own", "biased", "relued", "x_done"))
        block = ph.block()

        @block.sync
        def _(sp):
            def body(t, s):
                if not prefetched(t):
                    wait_reuse(sp, agg, t)
                    sp.dma_start(at[:, s, :], ins["at"][at_tile(t), :, :]).then_inc(at_in[s], 16)
                if isinstance(t, int) and t == 0:
                    sp.dma_start(b[:, :], ins["b0"]).then_inc(b_in, 16)
                    sp.dma_start(w2[:, :, :, :], ins["w2"]).then_inc(w2_in, 16)
                    sp.dma_start(av[:, :, :, :], ins["a2"]).then_inc(w2_in, 16)
            over_tiles(sp, body)

        @block.scalar
        def _(act):
            def out(t, s):
                act.wait_ge(biased, t + 1)
                nc.scalar.activation(u[:, s, :], u[:, s, :], ACT.Relu).then_inc(relued, 1)
            over_tiles(act, out)

        @block.tensor
        def _(pe):
            def aggregate(t, s):
                wait_in(pe, at_in[s], t, s)
                wait_reuse(pe, own, t)
                for m in range(NT):
                    mm = nc.tensor.matmul(ps_a[s][:, 0:D], at[0:rows_of(m), s, m * P:(m + 1) * P],
                                          support[0:rows_of(m), m, :], start=(m == 0), stop=(m == NT - 1))
                mm.then_inc(agg, 1)
            over_tiles(pe, aggregate)

        @block.vector
        def _(dve):
            def out(t, s):
                dve.wait_ge(agg, t + 1)
                wait_reuse(dve, x_done, t)
                nc.vector.tensor_tensor(u[:, s, :], ps_a[s][:, 0:D], support[:, at_tile(t), :], ALU.add).then_inc(own, 1)
                dve.wait_ge(own, t + 1)
                nc.vector.scalar_tensor_tensor(out=u[:, s, :], in0=u[:, s, :], scalar=k.dis[:, at_tile(t)],
                                               in1=b[:, :], op0=ALU.mult, op1=ALU.add).then_inc(biased, 1)
                dve.wait_ge(relued, t + 1)
                nc.vector.tensor_tensor(k.x[:, at_tile(t), :], k.x[:, at_tile(t), :], u[:, s, :],
                                        ALU.add).then_inc(x_done, 1)
                dve.wait_ge(x_done, t + 1)
                node_stats(nc, k, t)

            dve.wait_ge(w2_in, 32)
            for j in range(J):
                nc.vector.tensor_tensor(prod[:, j, :, :], w2[:, j // 2, :, :],
                                        av[:, j // 2, j % 2, :].unsqueeze(1).to_broadcast([P, C, D]),
                                        ALU.mult).then_inc(prod_done, 1)
            for j in range(J):
                dve.wait_ge(prod_done, j + 1)
                nc.vector.reduce_sum(k.wa[:, :, j], prod[:, j, :, :], AX.X)
            dve.wait_ge(b_in, 16)
            over_tiles(dve, out)


def wait_in(eng, sem, t, s):
    if isinstance(t, int):
        eng.wait_ge(sem, 16 * (t // 2 + 1))
    else:
        eng.wait_ge(sem, t * 8 + (16 - 8 * s))


def wait_stored(eng, sem, t, s):
    if isinstance(t, int):
        eng.wait_ge(sem, 16 * (t // 2))
    else:
        eng.wait_ge(sem, t * 8 - 8 * s)


BIG = 2.0 ** 126
SLOPE = 0.2
FLOOR = -(2.0 ** 125)
CHUNKS = ((0, 8), (8, 8), (16, 6))


def wait_count(eng, sem, t, per, off):
    if not isinstance(t, int) or per * t + off > 0:
        eng.wait_ge(sem, t * per + off)


def wait_apart(eng, sem, t, per, off):
    wait_count(eng, sem, t, per, off)
    if not isinstance(t, int):
        eng.nop(nofuse=True)


def last(t):
    return isinstance(t, int) and t == NT - 1


def gat(nc, k, ins):
    H, O = 4, D // 4
    f_dram = nc.dram_tensor("gat_f", (NT * 2 * H, P), F32).ap()
    with Phase(nc, "gat") as keep:
        f12 = keep.sb("f12", [P, NT, 2 * H])
        v = keep.sb("v", [P, NT, D])
        a = keep.sb("a", [P, 2, N])
        a_in = [keep.sem(f"a_in{s}") for s in range(2)]
        gat_in(nc, k, ins, f_dram, f12, v, a, a_in, H, O)
        gat_attend(nc, k, ins, f_dram, f12, v, a, a_in, H, O)


def gat_in(nc, k, ins, f_dram, f12, v, a, a_in, H, O):
    COLUMNS = NT * 2 * H
    with Phase(nc, "gat_in") as ph:
        w = ph.sb("w", [P, C, D + 2 * H])
        w_prod = ph.sb("w_prod", [P, 2, C, D])
        pw = ph.sb("pw", [P, C, D])
        uv = ph.sb("uv", [P, 2, D])
        b = ph.sb("b", [P, 2, D])
        bias = ph.sb("bias", [P, D])
        h = ph.sb("h", [P, 2, D])
        hT = ph.sb("hT", [P, 2, D])
        f_rows = ph.sb("f_rows", [COLUMNS // 2, 2, P])
        ps_t = [ph.ps(f"ps_t{s}", [P, 512]) for s in range(2)]
        ps_v = [ph.ps(f"ps_v{s}", [P, 512]) for s in range(2)]
        ps_r = [ph.ps(f"ps_r{s}", [P, 512]) for s in range(2)]
        ps_f = ph.ps("ps_f", [P, 512])
        w_in, uv_prod, uv_done, bias_done = (ph.sem(n) for n in ("w_in", "uv_prod", "uv_done", "bias_done"))
        h_done, turned, hT_done, mul_done = (ph.sem(n) for n in ("h_done", "turned", "hT_done", "mul_done"))
        v_mul, v_done, f_done, x_done, xb_done = (
            ph.sem(n) for n in ("v_mul", "v_done", "f_done", "x_done", "xb_done"))
        f_turned, f_kept, f_stored = (ph.sem(n) for n in ("f_turned", "f_kept", "f_stored"))
        stats = Stats(nc, k, ph, summed=True)
        block = ph.block()

        @block.sync
        def _(sp):
            sp.dma_start(w[:, :, 0:D], ins["w1"]).then_inc(w_in, 16)
            sp.dma_start(pw[:, :, :], ins["pw1"]).then_inc(w_in, 16)
            sp.dma_start(uv[:, :, :], ins["uv1"]).then_inc(w_in, 16)
            sp.dma_start(b[:, :, :], ins["b1"]).then_inc(w_in, 16)
            prefetch(sp, a, ins["a_rows"], a_in)
            sp.wait_ge(f_kept, 1)
            for j in range(2):
                sp.dma_start(f_dram[j * COLUMNS // 2:(j + 1) * COLUMNS // 2, :], f_rows[:, j, :]).then_inc(f_stored, 16)
            sp.wait_ge(f_stored, 32)

        @block.scalar
        def _(act):
            def normed(t, s):
                wait_reuse(act, turned, t)
                nc.scalar.activation(h[:, s, :], k.x[:, at_tile(t), :], ACT.Relu,
                                     bias=k.nmr[:, at_tile(t)], scale=k.rstd[:, at_tile(t)]).then_inc(h_done, 1)

            def body(t, s):
                if inside(t, 2):
                    normed(t + 2, s)
                act.wait_ge(v_mul, t + 1)
                nc.scalar.activation(v[:, at_tile(t), :], ps_v[s][:, 0:D], ACT.Copy).then_inc(v_done, 1)
                nc.scalar.activation(f12[:, at_tile(t), :], ps_v[s][:, D:D + 2 * H], ACT.Copy).then_inc(f_done, 1)
            stats.on_act(act)
            act.wait_ge(stats.done, 1)
            normed(0, 0)
            normed(1, 1)
            loop_ahead(act, body)
            act.wait_ge(f_turned, 1)
            nc.scalar.activation(f_rows[:, :, :].rearrange("p j n -> p (j n)"), ps_f[0:COLUMNS // 2, 0:2 * P],
                                 ACT.Copy).then_inc(f_kept, 1)

        @block.tensor
        def _(pe):
            def turn(t, s):
                pe.wait_ge(h_done, t + 1)
                wait_reuse(pe, hT_done, t)
                for c in range(C):
                    mm = nc.tensor.transpose(ps_t[s][:, c * P:(c + 1) * P], h[:, s, c * P:(c + 1) * P], k.ident[:, :])
                mm.then_inc(turned, 1)

            def body(t, s):
                if not last(t):
                    turn(t + 1, 1 - s)
                pe.wait_ge(hT_done, t + 1)
                wait_reuse(pe, f_done, t)
                for c in range(C):
                    mm = nc.tensor.matmul(ps_v[s][:, 0:D + 2 * H], hT[:, s, c * P:(c + 1) * P], w[:, c, :],
                                          start=(c == 0), stop=(c == C - 1))
                mm.then_inc(v_mul, 1)
                wait_reuse(pe, x_done, t)
                for c in range(C):
                    mm = nc.tensor.matmul(ps_r[s][:, 0:D], hT[:, s, c * P:(c + 1) * P], pw[:, c, :],
                                          start=(c == 0), stop=(c == C - 1))
                mm.then_inc(mul_done, 1)
            pe.wait_ge(w_in, 64)
            turn(0, 0)
            pe.wait_ge(uv_done, 2)
            over_tiles(pe, body)
            pe.wait_ge(f_done, NT)
            for j in range(2):
                mm = nc.tensor.transpose(ps_f[0:COLUMNS // 2, j * P:(j + 1) * P],
                                         f12[:, :, :].rearrange("p t f -> p (t f)")[:, j * COLUMNS // 2:(j + 1) * COLUMNS // 2],
                                         k.ident[:, :])
            mm.then_inc(f_turned, 1)

        @block.vector
        def _(dve):
            stats.on_dve(dve)
            dve.wait_ge(w_in, 64)
            for j in range(2):
                nc.vector.tensor_tensor(w_prod[:, j, :, :], w[:, :, 0:D],
                                        uv[:, j, :].unsqueeze(1).to_broadcast([P, C, D]), ALU.mult).then_inc(uv_prod, 1)
            for j in range(2):
                dve.wait_ge(uv_prod, j + 1)
                nc.vector.reduce_sum(w[:, :, D + j * H:D + (j + 1) * H],
                                     w_prod[:, j, :, :].rearrange("p c (h o) -> p c h o", h=H), AX.X).then_inc(uv_done, 1)
            nc.vector.tensor_tensor(bias[:, :], b[:, 0, :], b[:, 1, :], ALU.add).then_inc(bias_done, 1)
            dve.wait_ge(bias_done, 1)

            def fixed(t, s):
                dve.wait_ge(turned, t + 1)
                wait_reuse(dve, mul_done, t)
                nc.vector.tensor_copy(hT[:, s, :], ps_t[s][:, 0:D]).then_inc(hT_done, 1)

            def body(t, s):
                if not last(t):
                    fixed(t + 1, 1 - s)
                dve.wait_ge(mul_done, t + 1)
                nc.vector.tensor_tensor(k.x[:, at_tile(t), :], k.x[:, at_tile(t), :], ps_r[s][:, 0:D],
                                        ALU.add).then_inc(x_done, 1)
                dve.wait_ge(x_done, t + 1)
                nc.vector.tensor_tensor(k.x[:, at_tile(t), :], k.x[:, at_tile(t), :], bias[:, :],
                                        ALU.add).then_inc(xb_done, 1)
            fixed(0, 0)
            over_tiles(dve, body)


def gat_attend(nc, k, ins, f_dram, f12, v, a, a_in, H, O):
    with Phase(nc, "gat_at") as ph:
        f1_rows = ph.sb("f1_rows", [P, H, NP])
        f2_low = ph.sb("f2_low", [P, NT, H])
        rows_in = [ph.sem(f"rows_in{h}") for h in range(H)]
        low_ready = ph.sem("low_ready")
        mask = ph.sb("mask", [P, 2, N], BF16)
        z = ph.sb("z", [P, H, NP])
        pT = ph.sb("pT", [P, 2, NP])
        row_max = ph.sb("row_max", [P, H])
        neg_max = ph.sb("neg_max", [P, H])
        den = ph.sb("den", [P, 2, H])
        den_safe = ph.sb("den_safe", [P, 2, H])
        inv = ph.sb("inv", [P, 2, H])
        o = ph.sb("o", [P, 2, H, O])
        ps_p = [ph.ps(f"ps_p{c}", [P, 1024]) for c in range(3)]
        ps_o = [ph.ps(f"ps_o{s}", [P, 512]) for s in range(2)]
        (mask_done, pad_done, low_done, leaky_done, mult_done, max_done, neg_done, p_done, turned, pT_done, pv_done,
         safe_done, inv_done, o_done, x_done) = (
            ph.sem(n) for n in ("mask_done", "pad_done", "low_done", "leaky_done", "mult_done", "max_done", "neg_done", "p_done",
                                "turned", "pT_done", "pv_done", "safe_done", "inv_done", "o_done", "x_done"))
        block = ph.block()

        def shifted(t, s, h, by):
            over, h = (h + by) // H, (h + by) % H
            if isinstance(t, int) and not 0 <= t + over < NT:
                return None
            return (t + over, (s + over) % 2, h) if over else (t, s, h)

        def do(stage, at):
            if at is not None:
                stage(*at)

        @block.sync
        def _(sp):
            def load_row(h):
                sp.dma_start(f1_rows[:, h, :].rearrange("p (t n) -> p t n", n=P), f_dram.rearrange(
                    "(t f) n -> f t n", f=2 * H)[h].partition_broadcast(P)).then_inc(rows_in[h], 16)

            def body(t, s):
                if not prefetched(t):
                    wait_reuse(sp, mask_done, t)
                    wait_reuse(sp, mult_done, t, per=H)
                    sp.dma_start(a[:, s, :], ins["a_rows"][at_tile(t), :, :]).then_inc(a_in[s], 16)
            for h in range(H):
                load_row(h)
            over_tiles(sp, body)

        @block.gpsimd
        def _(pool):
            nc.gpsimd.memset(z[:, :, N:NP], 0.0).then_inc(pad_done, 1)

        @block.scalar
        def _(act):
            def low_branch(t, s, h):
                if isinstance(t, int) and t == 0:
                    act.wait_ge(rows_in[h], 16)
                wait_count(act, turned, t, 3 * H, 3 * (h + 1 - H))
                nc.scalar.activation(z[:, h, 0:N], f1_rows[:, h, 0:N], ACT.Identity, scale=SLOPE,
                                     bias=f2_low[:, at_tile(t), h:h + 1].rearrange("p a h -> p (a h)")).then_inc(
                                         low_done, 1)

            def evacuate(t, s, h):
                wait_count(act, pv_done, t, H, h - 1)
                for c in range(3):
                    m0, n = CHUNKS[c]
                    wait_count(act, turned, t, 3 * H, 3 * h + c + 1)
                    nc.scalar.activation(pT[:, h % 2, m0 * P:(m0 + n) * P], ps_p[c][:, 0:n * P],
                                         ACT.Copy).then_inc(pT_done, 1)

            def body(t, s):
                for h in range(H):
                    do(low_branch, shifted(t, s, h, 2))
                    do(evacuate, shifted(t, s, h, -1))
                    wait_count(act, neg_done, t, H, h + 1)
                    nc.scalar.activation(z[:, h, 0:N], z[:, h, 0:N], ACT.Exp,
                                         bias=neg_max[:, h:h + 1],
                                         accum_out=den[:, s, h:h + 1]).then_inc(p_done, 1)
            act.wait_ge(low_ready, 1)
            low_branch(0, 0, 0)
            low_branch(0, 0, 1)
            over_tiles(act, body)
            evacuate(NT - 1, 1, H - 1)

        @block.tensor
        def _(pe):
            def values(t, s, h):
                wait_count(pe, pT_done, t, 3 * H, 3 * h + 3)
                if h == 0:
                    wait_reuse(pe, o_done, t)
                for m in range(NT):
                    mm = nc.tensor.matmul(ps_o[s][:, h * O:(h + 1) * O], pT[:, h % 2, m * P:(m + 1) * P],
                                          v[:, m, h * O:(h + 1) * O], start=(m == 0), stop=(m == NT - 1))
                mm.then_inc(pv_done, 1)

            def body(t, s):
                for h in range(H):
                    do(values, shifted(t, s, h, -1))
                    wait_count(pe, p_done, t, H, h + 1)
                    for c, (m0, n) in enumerate(CHUNKS):
                        for m in range(m0, m0 + n):
                            mm = nc.tensor.transpose(ps_p[c][:, (m - m0) * P:(m - m0 + 1) * P],
                                                     z[:, h, m * P:(m + 1) * P], k.ident[:, :])
                        mm.then_inc(turned, 1)
            pe.wait_ge(pad_done, 1)
            over_tiles(pe, body)
            values(NT - 1, 1, H - 1)

        @block.vector
        def _(dve):
            def make_mask(t, s):
                wait_in(dve, a_in[s], t, s)
                nc.vector.tensor_scalar(mask[:, s, :], a[:, s, :], 0.0, -BIG, ALU.is_equal,
                                        ALU.mult).then_inc(mask_done, 1)

            def leaky(t, s, h):
                wait_count(dve, low_done, t, H, h + 1)
                nc.vector.scalar_tensor_tensor(out=z[:, h, 0:N], in0=f1_rows[:, h, 0:N],
                                               scalar=f12[:, at_tile(t), H + h:H + h + 1].rearrange("p a h -> p (a h)"),
                                               in1=z[:, h, 0:N], op0=ALU.add, op1=ALU.max).then_inc(leaky_done, 1)

            def weigh(t, s, h):
                if h == 0:
                    make_mask(t, s)
                wait_count(dve, leaky_done, t, H, h + 1)
                nc.vector.tensor_tensor(z[:, h, 0:N], z[:, h, 0:N], a[:, s, :], ALU.mult).then_inc(mult_done, 1)

            def masked_max(t, s, h):
                wait_count(dve, mask_done, t, 1, 1)
                wait_apart(dve, mult_done, t, H, h + 1)
                nc.vector.tensor_tensor_reduce(out=z[:, h, 0:N], in0=z[:, h, 0:N], in1=mask[:, s, :], scale=1.0,
                                               scalar=-2 * BIG, op0=ALU.add, op1=ALU.max,
                                               accum_out=row_max[:, h:h + 1]).then_inc(max_done, 1)

            def negate(t, s, h):
                wait_count(dve, max_done, t, H, h + 1)
                nc.vector.tensor_scalar(neg_max[:, h:h + 1], row_max[:, h:h + 1], FLOOR, -1.0, ALU.max,
                                        ALU.mult).then_inc(neg_done, 1)

            def keep_sum(t, s):
                wait_count(dve, p_done, t, H, H)
                nc.vector.tensor_scalar(den_safe[:, s, :], den[:, s, :], 0.5, None, ALU.max).then_inc(safe_done, 1)

            def invert(t, s):
                dve.wait_ge(safe_done, t + 1)
                nc.vector.reciprocal(inv[:, s, :], den_safe[:, s, :]).then_inc(inv_done, 1)

            def normalise(t, s):
                dve.wait_ge(inv_done, t + 1)
                wait_count(dve, pv_done, t, H, H)
                nc.vector.tensor_tensor(o[:, s, :, :], ps_o[s][:, 0:D].rearrange("p (h o) -> p h o", h=H),
                                        inv[:, s, :].unsqueeze(2).to_broadcast([P, H, O]), ALU.mult).then_inc(o_done, 1)

            def add(t, s):
                dve.wait_ge(o_done, t + 1)
                nc.vector.tensor_tensor(k.x[:, at_tile(t), :], k.x[:, at_tile(t), :],
                                        o[:, s, :, :].rearrange("p h o -> p (h o)").unsqueeze(1), ALU.add).then_inc(x_done, 1)

            def body(t, s):
                for h in range(H):
                    before = (t - 1, 1 - s) if h == 2 and inside(t, -1) else None
                    do(leaky, shifted(t, s, h, 1))
                    do(keep_sum, before)
                    masked_max(t, s, h)
                    do(invert, before)
                    do(weigh, shifted(t, s, h, 1))
                    do(normalise, before)
                    negate(t, s, h)
                    do(add, before)
            nc.vector.tensor_scalar(f2_low[:, :, :], f12[:, :, H:2 * H], SLOPE, None, ALU.mult).then_inc(low_ready, 1)
            leaky(0, 0, 0)
            weigh(0, 0, 0)
            over_tiles(dve, body)
            for stage in (keep_sum, invert, normalise, add):
                stage(NT - 1, 1)


class Gru:

    def __init__(self, nc, k, ph, ins, name, h, depth, state, source=None):
        self.nc, self.k, self.depth, self.ins, self.name = nc, k, depth, ins, name
        self.h, self.state, self.source = h, state, source
        self.last_to_add = source is not None
        self.inp, self.hid = ph.sb("inp", [P, 2, D]), ph.sb("hid", [P, 2, D])
        self.wi, self.wh = ph.sb("wi", [P, C, 3 * D]), ph.sb("wh", [P, C, 3 * D])
        self.bi, self.bh = ph.sb("bi", [P, 3 * D]), ph.sb("bh", [P, 3 * D])
        self.b_rz = ph.sb("b_rz", [P, 2 * D])
        self.b_n = ph.sb("b_n", [P, 2 * D])
        self.kept = ph.sb("kept", [P, 2, 4 * P])
        self.rz, self.nn = ph.sb("rz", [P, 2, 2 * D]), ph.sb("nn", [P, 2, 2 * D])
        self.cell = ph.sb("cell", [P, 2, D])
        self.ps_t = [ph.ps(f"ps_gt{s}", [P, 512]) for s in range(depth)]
        self.ps_rz = [ph.ps(f"ps_rz{s}", [P, 512]) for s in range(depth)]
        self.ps_n = [ph.ps(f"ps_n{s}", [P, 512]) for s in range(depth)]
        self.w_in, self.inp_ready = ph.sem("gw_in"), ph.sem("inp_ready")
        self.hid_in, self.inp_in = ([ph.sem(f"{n}_in{s}") for s in range(2)] for n in ("hid", "inp"))
        self.turned, self.kept_done, self.gates_done = ph.sem("g_turned"), ph.sem("kept_done"), ph.sem("gates_done")
        self.b_done, self.rz_done, self.n_done = ph.sem("b_done"), ph.sem("rz_done"), ph.sem("n_done")
        self.rz_tanh, self.gated, self.reset_done = ph.sem("rz_tanh"), ph.sem("gated"), ph.sem("reset_done")
        self.cand_done, self.cand_tanh = ph.sem("cand_done"), ph.sem("cand_tanh")
        self.diff_done, self.zdiff_done = ph.sem("diff_done"), ph.sem("zdiff_done")
        self.cell_done, self.x_done = ph.sem("cell_done"), ph.sem("gx_done")

    def load(self, sp):
        sp.dma_start(self.wi[:, :, :], self.ins[f"{self.name}_wih"]).then_inc(self.w_in, 16)
        sp.dma_start(self.wh[:, :, :], self.ins[f"{self.name}_whh"]).then_inc(self.w_in, 16)
        sp.dma_start(self.bi[:, :], self.ins[f"{self.name}_bih"]).then_inc(self.w_in, 16)
        sp.dma_start(self.bh[:, :], self.ins[f"{self.name}_bhh"]).then_inc(self.w_in, 16)

    def fetch(self, sp, t, s):
        wait_reuse(sp, self.turned, t)
        sp.dma_start(self.hid[:, s, :].unsqueeze(1), self.state[:, at_tile(t), :]).then_inc(self.hid_in[s], 16)
        if self.source is not None:
            sp.dma_start(self.inp[:, s, :].unsqueeze(1), self.source[:, at_tile(t), :]).then_inc(self.inp_in[s], 16)

    def biases(self, dve):
        dve.wait_ge(self.w_in, 64)
        self.nc.vector.tensor_tensor(self.b_rz[:, :], self.bi[:, 0:2 * D], self.bh[:, 0:2 * D], ALU.add).then_inc(self.b_done, 1)
        self.nc.vector.tensor_copy(self.b_n[:, 0:D], self.bi[:, 2 * D:3 * D]).then_inc(self.b_done, 1)
        self.nc.vector.tensor_copy(self.b_n[:, D:2 * D], self.bh[:, 2 * D:3 * D]).then_inc(self.b_done, 1)
        dve.wait_ge(self.b_done, 3)

    def pe_turn(self, pe, t, s):
        if self.source is None:
            pe.wait_ge(self.inp_ready, t + 1)
        else:
            wait_in(pe, self.inp_in[s], t, s)
        wait_in(pe, self.hid_in[s], t, s)
        wait_reuse(pe, self.kept_done, t, depth=self.depth)
        for c in range(4):
            src = (self.inp, self.hid)[c // 2]
            mm = self.nc.tensor.transpose(self.ps_t[s % self.depth][:, c * P:(c + 1) * P],
                                          src[:, s, (c % 2) * P:(c % 2 + 1) * P], self.k.ident[:, :])
        mm.then_inc(self.turned, 1)

    def act_keep(self, act, t, s):
        act.wait_ge(self.turned, t + 1)
        wait_reuse(act, self.gates_done, t)
        self.nc.scalar.activation(self.kept[:, s, :], self.ps_t[s % self.depth][:, :], ACT.Copy).then_inc(self.kept_done, 1)

    def pe_gates(self, pe, t, s):
        d = s % self.depth
        pe.wait_ge(self.kept_done, t + 1)
        wait_reuse(pe, self.rz_done, t, depth=self.depth)
        for c in range(4):
            w = (self.wi, self.wh)[c // 2]
            self.nc.tensor.matmul(self.ps_rz[d][:, :], self.kept[:, s, c * P:(c + 1) * P], w[:, c % 2, 0:2 * D],
                                  start=(c == 0), stop=(c == 3))
        wait_reuse(pe, self.n_done, t, depth=self.depth)
        for c in range(4):
            w = (self.wi, self.wh)[c // 2]
            mm = self.nc.tensor.matmul(self.ps_n[d][:, (c // 2) * D:(c // 2 + 1) * D],
                                       self.kept[:, s, c * P:(c + 1) * P], w[:, c % 2, 2 * D:3 * D],
                                       start=(c % 2 == 0), stop=(c % 2 == 1))
        mm.then_inc(self.gates_done, 1)

    def act_gates(self, act, t, s):
        act.wait_ge(self.rz_done, t + 1)
        self.nc.scalar.activation(self.rz[:, s, :], self.rz[:, s, :], ACT.Tanh, scale=0.5).then_inc(self.rz_tanh, 1)

    def act_candidate(self, act, t, s):
        act.wait_ge(self.cand_done, t + 1)
        self.nc.scalar.activation(self.nn[:, s, 0:D], self.nn[:, s, 0:D], ACT.Tanh).then_inc(self.cand_tanh, 1)

    def dve(self, dve, t, s):
        v, k, d = self.nc.vector, self.k, s % self.depth
        rz, nn, cell = self.rz[:, s, :], self.nn[:, s, :], self.cell[:, s, :]
        dve.wait_ge(self.gates_done, t + 1)
        v.tensor_tensor(rz, self.ps_rz[d][:, :], self.b_rz[:, :], ALU.add).then_inc(self.rz_done, 1)
        v.tensor_tensor(nn, self.ps_n[d][:, :], self.b_n[:, :], ALU.add).then_inc(self.n_done, 1)
        if self.last_to_add and inside(t, -1):
            self.stats(dve, t - 1)
        dve.wait_ge(self.rz_tanh, t + 1)
        v.tensor_scalar(rz, rz, 0.5, 0.5, ALU.mult, ALU.add).then_inc(self.gated, 1)
        dve.wait_ge(self.n_done, t + 1)
        dve.wait_ge(self.gated, t + 1)
        v.tensor_tensor(cell, self.rz[:, s, 0:D], self.nn[:, s, D:2 * D], ALU.mult).then_inc(self.reset_done, 1)
        dve.wait_ge(self.reset_done, t + 1)
        v.tensor_tensor(self.nn[:, s, 0:D], self.nn[:, s, 0:D], cell, ALU.add).then_inc(self.cand_done, 1)
        dve.wait_ge(self.cand_tanh, t + 1)
        v.tensor_tensor(cell.unsqueeze(1), self.h[:, at_tile(t), :], self.nn[:, s, 0:D].unsqueeze(1), ALU.subtract).then_inc(self.diff_done, 1)
        dve.wait_ge(self.diff_done, t + 1)
        v.tensor_tensor(cell, cell, self.rz[:, s, D:2 * D], ALU.mult).then_inc(self.zdiff_done, 1)
        dve.wait_ge(self.zdiff_done, t + 1)
        v.tensor_tensor(cell, cell, self.nn[:, s, 0:D], ALU.add).then_inc(self.cell_done, 1)
        dve.wait_ge(self.cell_done, t + 1)
        v.scalar_tensor_tensor(out=k.x[:, at_tile(t), :], in0=cell.unsqueeze(1), scalar=k.diag[:, at_tile(t)],
                               in1=k.x[:, at_tile(t), :], op0=ALU.mult, op1=ALU.add).then_inc(self.x_done, 1)

    def stats(self, dve, t):
        dve.wait_ge(self.x_done, t + 1)
        node_stats(self.nc, self.k, t)


def signed_gat(nc, k, ins):
    h_dram = nc.dram_tensor("sg_h", (P, NT, D), F32).ap()
    v_dram = nc.dram_tensor("sg_v", (HEADS, P, NT, D), F32).ap()
    e_dram = nc.dram_tensor("sg_e", (HEADS * 2 * NT, P), F32).ap()
    pos_dram = nc.dram_tensor("sg_pos", (NT, P, N), mybir.dt.uint8).ap()
    with Phase(nc, "sg_h") as keep:
        h = keep.sb("h", [P, NT, D])
        u3 = keep.sb("u3", [P, NT, 2 * HEADS, 3], BF16)
        signed_in(nc, k, ins, h, u3, v_dram)
        signed_support(nc, k, ins, h, u3, h_dram, e_dram)
    with Phase(nc, "sg_es") as keep:
        es = keep.sb("es", [P, NT, D])
        signed_attend(nc, k, ins, v_dram, e_dram, pos_dram, es)
        signed_node(nc, k, ins, h_dram, es)


def signed_in(nc, k, ins, h, u3, v_dram):
    J = 2 * HEADS
    with Phase(nc, "sg_in") as ph:
        w = ph.sb("w", [P, HEADS, C, D])
        hs = ph.sb("hs", [P, 2, D])
        hT = ph.sb("hT", [P, 2, D])
        u = ph.sb("u", [P, NT, J])
        rest = ph.sb("rest", [P, 2, NT, J])
        v = ph.sb("v", [P, 4, HEADS, D])
        ps_t = [ph.ps(f"ps_t{s}", [P, 512]) for s in range(2)]
        ps_u = [ph.ps(f"ps_u{s}", [P, 512]) for s in range(2)]
        ps_v = [ph.ps(f"ps_v{s}", [P, 2, 512]) for s in range(2)]
        w_in, h_done, turned = (ph.sem(n) for n in ("w_in", "h_done", "turned"))
        hT_done, u_mul, v_mul, u_done, kept, split = (
            ph.sem(n) for n in ("hT_done", "u_mul", "v_mul", "u_done", "kept", "split"))
        v_act, v_dve = ph.sem("v_act"), ph.sem("v_dve")
        v_stored = [ph.sem(f"v_stored{s}") for s in range(4)]
        stats = Stats(nc, k, ph)
        block = ph.block()

        @block.sync
        def _(sp):
            sp.dma_start(w[:, :, :, :], ins["w2"]).then_inc(w_in, 16)
            for t in range(NT):
                sp.wait_ge(v_act, t + 1)
                sp.wait_ge(v_dve, t + 1)
                sp.dma_start(v_dram[:, :, t, :].rearrange("i p d -> p i d"), v[:, t % 4, :, :]).then_inc(v_stored[t % 4], 16)
            for s in range(4):
                sp.wait_ge(v_stored[s], 16 * len(range(s, NT, 4)))

        @block.gpsimd
        def _(pool):
            def body(t, s):
                pool.wait_ge(h_done, t + 1)
                nc.gpsimd.tensor_copy(h[:, at_tile(t), :], hs[:, s, :].unsqueeze(1)).then_inc(kept, 1)
            over_tiles(pool, body)

        @block.scalar
        def _(act):
            def normed(t, s):
                wait_reuse(act, turned, t)
                wait_reuse(act, kept, t)
                nc.scalar.activation(hs[:, s, :], k.x[:, at_tile(t), :], ACT.Relu,
                                     bias=k.nmr[:, at_tile(t)], scale=k.rstd[:, at_tile(t)]).then_inc(h_done, 1)
            stats.on_act(act)
            act.wait_ge(stats.done, 1)
            normed(0, 0)
            normed(1, 1)
            for t in range(NT):
                if t < NT - 2:
                    normed(t + 2, t % 2)
                act.wait_ge(v_mul, t + 1)
                if t >= 4:
                    act.wait_ge(v_stored[t % 4], 16 * (t // 4))
                nc.scalar.activation(v[:, t % 4, 0:2, :].rearrange("p i d -> p (i d)"), ps_v[t % 2][:, 0, :],
                                     ACT.Copy).then_inc(v_act, 1)

        @block.tensor
        def _(pe):
            def turn(t, s):
                pe.wait_ge(h_done, t + 1)
                wait_reuse(pe, hT_done, t)
                for c in range(C):
                    mm = nc.tensor.transpose(ps_t[s][:, c * P:(c + 1) * P], hs[:, s, c * P:(c + 1) * P], k.ident[:, :])
                mm.then_inc(turned, 1)

            def body(t, s):
                if not last(t):
                    turn(t + 1, 1 - s)
                pe.wait_ge(hT_done, t + 1)
                wait_reuse(pe, v_act, t)
                wait_reuse(pe, v_dve, t)
                for i in range(HEADS):
                    for c in range(C):
                        mm = nc.tensor.matmul(ps_v[s][:, i // 2, i % 2 * D:(i % 2 + 1) * D], hT[:, s, c * P:(c + 1) * P],
                                              w[:, i, c, :], start=(c == 0), stop=(c == C - 1))
                mm.then_inc(v_mul, 1)
                wait_reuse(pe, u_done, t)
                for c in range(C):
                    mm = nc.tensor.matmul(ps_u[s][:, 0:J], hT[:, s, c * P:(c + 1) * P], k.wa[:, c, :],
                                          start=(c == 0), stop=(c == C - 1))
                mm.then_inc(u_mul, 1)
            turn(0, 0)
            pe.wait_ge(w_in, 16)
            over_tiles(pe, body)

        @block.vector
        def _(dve):
            stats.on_dve(dve)
            def fixed(t):
                dve.wait_ge(turned, t + 1)
                wait_reuse(dve, u_mul, t)
                nc.vector.tensor_copy(hT[:, t % 2, :], ps_t[t % 2][:, 0:D]).then_inc(hT_done, 1)
            fixed(0)
            for t in range(NT):
                if t < NT - 1:
                    fixed(t + 1)
                dve.wait_ge(v_mul, t + 1)
                if t >= 4:
                    dve.wait_ge(v_stored[t % 4], 16 * (t // 4))
                nc.vector.tensor_copy(v[:, t % 4, 2, :], ps_v[t % 2][:, 1, 0:D]).then_inc(v_dve, 1)
                dve.wait_ge(u_mul, t + 1)
                nc.vector.tensor_copy(u[:, t, :], ps_u[t % 2][:, 0:J]).then_inc(u_done, 1)
            dve.wait_ge(u_done, NT)
            nc.vector.tensor_copy(u3[:, :, :, 0], u[:, :, :]).then_inc(split, 1)
            dve.wait_ge(split, 1)
            nc.vector.tensor_tensor(rest[:, 0, :, :], u[:, :, :], u3[:, :, :, 0], ALU.subtract).then_inc(split, 1)
            dve.wait_ge(split, 2)
            nc.vector.tensor_copy(u3[:, :, :, 1], rest[:, 0, :, :]).then_inc(split, 1)
            dve.wait_ge(split, 3)
            nc.vector.tensor_tensor(rest[:, 1, :, :], rest[:, 0, :, :], u3[:, :, :, 1], ALU.subtract).then_inc(split, 1)
            dve.wait_ge(split, 4)
            nc.vector.tensor_copy(u3[:, :, :, 2], rest[:, 1, :, :])


def signed_support(nc, k, ins, h, u3, h_dram, e_dram):
    J = 2 * HEADS
    COLUMNS = J * NT
    with Phase(nc, "sg_sup") as ph:
        at = ph.sb("at", [P, 2, NT, P])
        sign = ph.sb("sign", [P, 2, 2, NT, P], BF16)
        sums = ph.sb("sums", [P, 2, 2, J])
        pre = ph.sb("pre", [P, 2, HEADS, 2])
        e = ph.sb("e", [P, HEADS, 2, NT])
        e_rows = ph.sb("e_rows", [COLUMNS // 2, 2, P])
        ps_a = [ph.ps(f"ps_a{s}", [P, 512]) for s in range(2)]
        ps_e = [ph.ps(f"ps_e{s}", [P, 512]) for s in range(2)]
        gru = Gru(nc, k, ph, ins, "edge", h, depth=1, state=h)
        at_in = [ph.sem(f"at_in{s}") for s in range(2)]
        cut, pos_done, neg_done, agg, e_mul = (ph.sem(n) for n in ("cut", "pos_done", "neg_done", "agg", "e_mul"))
        sum_done, plus_done, minus_done, e_done = (ph.sem(n) for n in ("sum_done", "plus_done", "minus_done", "e_done"))
        e_turned, e_kept, e_stored, h_stored = (ph.sem(n) for n in ("e_turned", "e_kept", "e_stored", "h_stored"))
        block = ph.block()

        @block.sync
        def _(sp):
            def body(t, s):
                wait_reuse(sp, agg, t)
                wait_reuse(sp, neg_done, t)
                sp.dma_start(at[:, s, :, :].rearrange("p m n -> p (m n)"), ins["at"][at_tile(t), :, :]).then_inc(at_in[s], 16)
                gru.fetch(sp, t, s)
                if isinstance(t, int) and t == 0:
                    gru.load(sp)
                if isinstance(t, int) and t == 1:
                    sp.dma_start(h_dram, h[:, :, :]).then_inc(h_stored, 16)
            over_tiles(sp, body)
            sp.wait_ge(e_kept, 1)
            for j in range(2):
                sp.dma_start(e_dram[j * COLUMNS // 2:(j + 1) * COLUMNS // 2, :], e_rows[:, j, :]).then_inc(e_stored, 16)
            sp.wait_ge(e_stored, 32)
            sp.wait_ge(h_stored, 16)

        @block.tensor
        def _(pe):
            def body(t, s):
                pe.wait_ge(cut, t + 1)
                wait_reuse(pe, gru.inp_ready, t)
                for m in range(NT):
                    mm = nc.tensor.matmul(ps_a[s][:, 0:D], at[0:rows_of(m), s, m, :], h[0:rows_of(m), m, :],
                                          start=(m == 0), stop=(m == NT - 1))
                mm.then_inc(agg, 1)
                pe.wait_ge(pos_done, t + 1)
                pe.wait_ge(neg_done, t + 1)
                wait_reuse(pe, sum_done, t)
                for g in range(2):
                    for m in range(NT):
                        mm = nc.tensor.matmul(ps_e[s][:, g * 3 * J:(g + 1) * 3 * J], sign[0:rows_of(m), s, g, m, :],
                                              u3[0:rows_of(m), m, :, :].rearrange("p j c -> p (j c)"),
                                              start=(m == 0), stop=(m == NT - 1))
                mm.then_inc(e_mul, 1)
                if isinstance(t, int) and t == 0:
                    pe.wait_ge(gru.w_in, 64)
                else:
                    gru.pe_gates(pe, t - 1, 1 - s)
                gru.pe_turn(pe, t, s)
            over_tiles(pe, body)
            pe.wait_ge(e_done, NT)
            for j in range(2):
                mm = nc.tensor.transpose(ps_e[0][0:COLUMNS // 2, j * P:(j + 1) * P],
                                         e[:, :, :, :].rearrange("p i g t -> p (i g t)")[:, j * COLUMNS // 2:(j + 1) * COLUMNS // 2],
                                         k.ident[:, :])
            mm.then_inc(e_turned, 1)
            gru.pe_gates(pe, NT - 1, 1)

        @block.scalar
        def _(act):
            def body(t, s):
                act.wait_ge(agg, t + 1)
                wait_reuse(act, gru.turned, t)
                nc.scalar.activation(gru.inp[:, s, :], ps_a[s][:, 0:D], ACT.Copy).then_inc(gru.inp_ready, 1)
                if not (isinstance(t, int) and t == 0):
                    gru.act_gates(act, t - 1, 1 - s)
                    gru.act_candidate(act, t - 1, 1 - s)
                gru.act_keep(act, t, s)
            over_tiles(act, body)
            act.wait_ge(e_turned, 1)
            nc.scalar.activation(e_rows[:, :, :].rearrange("p j n -> p (j n)"), ps_e[0][0:COLUMNS // 2, 0:2 * P],
                                 ACT.Copy).then_inc(e_kept, 1)
            gru.act_gates(act, NT - 1, 1)
            gru.act_candidate(act, NT - 1, 1)

        @block.vector
        def _(dve):
            def prepare(t, s):
                wait_in(dve, at_in[s], t, s)
                nc.vector.tensor_tensor(at[:, s, at_tile(t), :], at[:, s, at_tile(t), :], k.offdiag[:, :].unsqueeze(1),
                                        ALU.mult).then_inc(cut, 1)
                dve.wait_ge(cut, t + 1)
                wait_reuse(dve, e_mul, t)
                nc.vector.tensor_scalar(sign[:, s, 0, :, :], at[:, s, :, :], 0.0, None, ALU.is_gt).then_inc(pos_done, 1)
                nc.vector.tensor_scalar(sign[:, s, 1, :, :], at[:, s, :, :], 0.0, None, ALU.is_lt).then_inc(neg_done, 1)

            def logits(t, s):
                dve.wait_ge(e_mul, t + 1)
                nc.vector.reduce_sum(sums[:, s, :, :], ps_e[s][:, 0:6 * J].rearrange("p (g j c) -> p g j c", g=2, j=J),
                                     AX.X).then_inc(sum_done, 1)
                dve.wait_ge(sum_done, t + 1)
                by = sums[:, s, :, :].rearrange("p g (i a) -> p g i a", a=2)
                nc.vector.tensor_tensor(pre[:, s, :, 0], by[:, 0, :, 0], by[:, 1, :, 1], ALU.add).then_inc(plus_done, 1)
                nc.vector.tensor_tensor(pre[:, s, :, 1], by[:, 1, :, 0], by[:, 0, :, 1], ALU.add).then_inc(minus_done, 1)
                dve.wait_ge(plus_done, t + 1)
                dve.wait_ge(minus_done, t + 1)
                nc.vector.scalar_tensor_tensor(out=e[:, :, :, at_tile(t)], in0=pre[:, s, :, :].unsqueeze(3), scalar=SLOPE,
                                               in1=pre[:, s, :, :].unsqueeze(3), op0=ALU.mult, op1=ALU.max).then_inc(e_done, 1)

            def body(t, s):
                if not last(t):
                    prepare(t + 1, 1 - s)
                if not (isinstance(t, int) and t == 0):
                    gru.dve(dve, t - 1, 1 - s)
                logits(t, s)
            prepare(0, 0)
            gru.biases(dve)
            over_tiles(dve, body)
            gru.dve(dve, NT - 1, 1)


def signed_attend(nc, k, ins, v_dram, e_dram, pos_dram, es):
    with Phase(nc, "sg_at") as ph:
        rows = ph.sb("rows", [P, 2, 2, NP])
        v = ph.sb("v", [P, NT, D])
        a = ph.sb("a", [P, 2, N])
        pos = ph.sb("pos", [P, 2, N], mybir.dt.uint8)
        mask = ph.sb("mask", [P, N], BF16)
        z = ph.sb("z", [P, 2, NP])
        pT = ph.sb("pT", [P, 2, NP])
        neg_max = ph.sb("neg_max", [P, 2])
        row_max = ph.sb("row_max", [P, 2])
        den = ph.sb("den", [P, NT])
        den_safe = ph.sb("den_safe", [P, NT])
        inv = ph.sb("inv", [P, NT])
        ps_p = [ph.ps(f"ps_p{c}", [P, 1024]) for c in range(3)]
        ps_o = [ph.ps(f"ps_o{s}", [P, 512]) for s in range(2)]
        rows_in = [[ph.sem(f"rows_in{i}{g}") for g in range(2)] for i in range(HEADS)]
        v_in = [ph.sem(f"v_in{c}") for c in range(len(CHUNKS))]
        a_in, pos_in, pos_stored = ([ph.sem(f"{n}{s}") for s in range(2)] for n in ("a_in", "pos_in", "pos_stored"))
        pad_done, cut, pos_done, mask_done, base_done, chosen = (
            ph.sem(n) for n in ("pad_done", "cut", "pos_done", "mask_done", "base_done", "chosen"))
        max_done, neg_done, p_done, scaled, turned, pT_done, pv_done = (
            ph.sem(n) for n in ("max_done", "neg_done", "p_done", "scaled", "turned", "pT_done", "pv_done"))
        safe_done, inv_done, es_done = (ph.sem(n) for n in ("safe_done", "inv_done", "es_done"))
        block = ph.block()

        def loop(eng, body):
            for i in range(HEADS):
                body(i, 0, 0)
                body(i, 1, 1)
                with eng.Fori(1, NT // 2 - 2) as j:
                    body(i, j * 2, 0)
                    body(i, j * 2 + 1, 1)
                for t in range(NT - 4, NT):
                    body(i, t, t % 2)

        def shifted(i, t, s, by):
            if isinstance(t, int):
                step = i * NT + t + by
                return (step // NT, step % NT, step % 2) if 0 <= step < HEADS * NT else None
            return i, t + by, (s + by) % 2

        def do(stage, at):
            if at is not None:
                stage(*at)

        @block.sync
        def _(sp):
            def load_rows(i):
                for g in (1, 0):
                    sp.dma_start(rows[:, i % 2, g, :], e_dram[(2 * i + g) * NT:(2 * i + g + 1) * NT, :].rearrange(
                        "t n -> (t n)").partition_broadcast(P)).then_inc(rows_in[i][g], 16)

            def body(i, t, s):
                n = t + i * NT
                first = isinstance(t, int) and t < 2
                wait_reuse(sp, scaled, n)
                sp.dma_start(a[:, s, :], ins["a_rows"][at_tile(t), :, :]).then_inc(a_in[s], 16)
                if i > 0:
                    wait_reuse(sp, chosen, n)
                    if i == 1 and first:
                        sp.wait_ge(pos_stored[s], 16 * (NT // 2))
                    sp.dma_start(pos[:, s, :], pos_dram[at_tile(t), :, :]).then_inc(pos_in[s], 16)
                if first and n == 0:
                    load_rows(0)
                if isinstance(t, int) and t == NT - 4 and i + 1 < HEADS:
                    if i > 0:
                        sp.wait_ge(chosen, i * NT)
                    load_rows(i + 1)
            loop(sp, body)

        @block.gpsimd
        def _(pool):
            nc.gpsimd.memset(z[:, :, N:NP], 0.0).then_inc(pad_done, 1)

        @block.scalar
        def _(act):
            def load_values(i):
                for c, (m0, m) in enumerate(CHUNKS):
                    act.dma_start(v[:, m0:m0 + m, :], v_dram[i][:, m0:m0 + m, :]).then_inc(v_in[c], 16)

            def base(i, t, s):
                wait_count(act, turned, t + i * NT, 3, 3 - 6)
                if isinstance(t, int) and t == 0:
                    act.wait_ge(rows_in[i][1], 16)
                nc.scalar.activation(z[:, s, 0:N], rows[:, i % 2, 1, 0:N], ACT.Copy).then_inc(base_done, 1)

            def exps(i, t, s):
                act.wait_ge(neg_done, t + i * NT + 1)
                nc.scalar.activation(z[:, s, 0:N], z[:, s, 0:N], ACT.Exp, bias=neg_max[:, s:s + 1],
                                     accum_out=den[:, at_tile(t)]).then_inc(p_done, 1)
                if i == 0:
                    act.wait_ge(pos_done, t + 1)
                    act.dma_start(pos_dram[at_tile(t), :, :], pos[:, s, :]).then_inc(pos_stored[s], 16)

            def evacuate(i, t, s):
                wait_reuse(act, pv_done, t + i * NT)
                for c, (m0, n) in enumerate(CHUNKS):
                    wait_count(act, turned, t + i * NT, 3, c + 1)
                    nc.scalar.activation(pT[:, s, m0 * P:(m0 + n) * P], ps_p[c][:, 0:n * P],
                                         ACT.Copy).then_inc(pT_done, 1)

            def body(i, t, s):
                if isinstance(t, int) and t == 1 and i > 0:
                    act.wait_ge(pv_done, i * NT)
                    load_values(i)
                evacuate(i, t, s)
                do(base, shifted(i, t, s, 2))
                do(exps, shifted(i, t, s, 1))
            base(0, 0, 0)
            base(0, 1, 1)
            load_values(0)
            exps(0, 0, 0)
            loop(act, body)

        @block.tensor
        def _(pe):
            def turn(i, t, s):
                pe.wait_ge(scaled, t + i * NT + 1)
                for c, (m0, n) in enumerate(CHUNKS):
                    wait_count(pe, pT_done, t + i * NT, 3, c + 1 - 3)
                    for m in range(m0, m0 + n):
                        mm = nc.tensor.transpose(ps_p[c][:, (m - m0) * P:(m - m0 + 1) * P],
                                                 z[:, s, m * P:(m + 1) * P], k.ident[:, :])
                    mm.then_inc(turned, 1)

            def body(i, t, s):
                do(turn, shifted(i, t, s, 1))
                wait_reuse(pe, es_done, t + i * NT)
                for c, (m0, n) in enumerate(CHUNKS):
                    wait_count(pe, pT_done, t + i * NT, 3, c + 1)
                    if isinstance(t, int) and t == 0:
                        pe.wait_ge(v_in[c], 16 * (i + 1))
                    for m in range(m0, m0 + n):
                        mm = nc.tensor.matmul(ps_o[s][:, 0:D], pT[:, s, m * P:(m + 1) * P], v[:, m, :],
                                              start=(m == 0), stop=(m == NT - 1))
                mm.then_inc(pv_done, 1)
            pe.wait_ge(pad_done, 1)
            turn(0, 0, 0)
            loop(pe, body)

        @block.vector
        def _(dve):
            def cut_diagonal(i, t, s):
                wait_in(dve, a_in[s], t + i * NT, s)
                if isinstance(t, int) and t == NT - 1:
                    block_diag, off = a[:, s, t * P:N], k.offdiag[:, 0:N - t * P]
                else:
                    block_diag, off = a[:, s, bass.ds(t * P, P)], k.offdiag[:, :]
                nc.vector.tensor_tensor(block_diag, block_diag, off, ALU.mult).then_inc(cut, 1)

            def masks(i, t, s):
                n = t + i * NT
                dve.wait_ge(cut, n + 1)
                if i == 0:
                    wait_reuse(dve, chosen, t)
                    if inside(t, -2):
                        wait_stored(dve, pos_stored[s], t, s)
                    nc.vector.tensor_scalar(pos[:, s, :], a[:, s, :], 0.0, None, ALU.is_gt).then_inc(pos_done, 1)
                wait_reuse(dve, max_done, n, depth=1)
                nc.vector.tensor_scalar(mask[:, :], a[:, s, :], 0.0, -BIG, ALU.is_equal, ALU.mult).then_inc(mask_done, 1)

            def choose(i, t, s):
                if isinstance(t, int) and t == 0:
                    dve.wait_ge(rows_in[i][0], 16)
                dve.wait_ge(base_done, t + i * NT + 1)
                if i == 0:
                    wait_apart(dve, pos_done, t, 1, 1)
                else:
                    wait_in(dve, pos_in[s], t + (i - 1) * NT, s)
                    if not isinstance(t, int):
                        dve.nop(nofuse=True)
                nc.vector.copy_predicated(z[:, s, 0:N], pos[:, s, :], rows[:, i % 2, 0, 0:N]).then_inc(chosen, 1)

            def masked_max(i, t, s):
                n = t + i * NT
                dve.wait_ge(mask_done, n + 1)
                wait_apart(dve, chosen, n, 1, 1)
                nc.vector.tensor_tensor_reduce(out=z[:, s, 0:N], in0=z[:, s, 0:N], in1=mask[:, :], scale=1.0,
                                               scalar=-2 * BIG, op0=ALU.add, op1=ALU.max,
                                               accum_out=row_max[:, s:s + 1]).then_inc(max_done, 1)

            def negate(i, t, s):
                dve.wait_ge(max_done, t + i * NT + 1)
                nc.vector.tensor_scalar(neg_max[:, s:s + 1], row_max[:, s:s + 1], FLOOR, -1.0, ALU.max,
                                        ALU.mult).then_inc(neg_done, 1)

            def scale(i, t, s):
                dve.wait_ge(p_done, t + i * NT + 1)
                nc.vector.tensor_tensor(z[:, s, 0:N], z[:, s, 0:N], a[:, s, :], ALU.mult).then_inc(scaled, 1)

            def keep_sum(i, t, s):
                dve.wait_ge(p_done, t + i * NT + 1)
                nc.vector.tensor_scalar(den_safe[:, at_tile(t)], den[:, at_tile(t)], 0.5, float(HEADS), ALU.max,
                                        ALU.mult).then_inc(safe_done, 1)

            def invert(i, t, s):
                dve.wait_ge(safe_done, t + i * NT + 1)
                nc.vector.reciprocal(inv[:, at_tile(t)], den_safe[:, at_tile(t)]).then_inc(inv_done, 1)

            def add(i, t, s):
                dve.wait_ge(inv_done, t + i * NT + 1)
                dve.wait_ge(pv_done, t + i * NT + 1)
                if i == 0:
                    nc.vector.tensor_scalar(es[:, at_tile(t), :], ps_o[s][:, 0:D].unsqueeze(1), inv[:, at_tile(t)], None,
                                            ALU.mult).then_inc(es_done, 1)
                else:
                    nc.vector.scalar_tensor_tensor(out=es[:, at_tile(t), :], in0=ps_o[s][:, 0:D].unsqueeze(1),
                                                   scalar=inv[:, at_tile(t)], in1=es[:, at_tile(t), :],
                                                   op0=ALU.mult, op1=ALU.add).then_inc(es_done, 1)

            def body(i, t, s):
                ahead, later, before = (shifted(i, t, s, by) for by in (1, 2, -2))
                do(choose, ahead)
                do(keep_sum, before)
                do(masked_max, ahead)
                do(invert, before)
                do(negate, ahead)
                do(cut_diagonal, later)
                do(add, before)
                do(masks, later)
                do(scale, ahead)
            for t, stages in ((0, (cut_diagonal, masks, choose, masked_max, negate)), (1, (cut_diagonal, masks)), (0, (scale,))):
                for stage in stages:
                    stage(0, t, t)
            loop(dve, body)
            for t in (NT - 2, NT - 1):
                for stage in (keep_sum, invert, add):
                    stage(HEADS - 1, t, t % 2)


def signed_node(nc, k, ins, h_dram, es):
    with Phase(nc, "sg_node") as ph:
        h = ph.sb("h", [P, NT, D])
        h_in = ph.sem("h_in")
        gru = Gru(nc, k, ph, ins, "node", h, depth=2, state=h_dram, source=es)
        block = ph.block()

        @block.sync
        def _(sp):
            gru.fetch(sp, 0, 0)
            gru.load(sp)
            gru.fetch(sp, 1, 1)
            sp.dma_start(h[:, :, :], h_dram).then_inc(h_in, 16)
            with sp.Fori(1, NT // 2) as i:
                gru.fetch(sp, i * 2, 0)
                gru.fetch(sp, i * 2 + 1, 1)

        @block.tensor
        def _(pe):
            def body(t, s):
                if not last(t):
                    gru.pe_turn(pe, t + 1, 1 - s)
                gru.pe_gates(pe, t, s)
            pe.wait_ge(gru.w_in, 64)
            gru.pe_turn(pe, 0, 0)
            over_tiles(pe, body)

        @block.scalar
        def _(act):
            def body(t, s):
                if not last(t):
                    gru.act_keep(act, t + 1, 1 - s)
                gru.act_gates(act, t, s)
                gru.act_candidate(act, t, s)
            gru.act_keep(act, 0, 0)
            over_tiles(act, body)

        @block.vector
        def _(dve):
            gru.biases(dve)
            dve.wait_ge(h_in, 16)
            over_tiles(dve, lambda t, s: gru.dve(dve, t, s))
            gru.stats(dve, NT - 1)


def masked_attention(nc, k, ins):
    H, O = 4, D // 4
    q_dram = nc.dram_tensor("ma_q", (P, 2, C, 2, NP), BF16).ap()
    with Phase(nc, "ma") as keep:
        k_stack = keep.sb("k_stack", [P, 2, C, 3, NP], BF16)
        v = keep.sb("v", [P, NT, D])
        a = keep.sb("a", [P, 2, N])
        a_in = [keep.sem(f"a_in{s}") for s in range(2)]
        masked_in(nc, k, ins, q_dram, k_stack, v, a, a_in, H, O)
        masked_attend(nc, k, ins, q_dram, k_stack, v, a, a_in, H, O)


def masked_in(nc, k, ins, q_dram, k_stack, v, a, a_in, H, O):
    GROUP = 4
    STORES = 16
    with Phase(nc, "ma_in") as ph:
        w = ph.sb("w", [P, C, 3 * D])
        b_col = ph.sb("b_col", [P, 2, C])
        b_v = ph.sb("b_v", [P, D])
        hs = ph.sb("hs", [P, 2, D])
        hT = ph.sb("hT", [P, 2, D])
        rest = ph.sb("rest", [P, 2, 2, C, P])
        part = ph.sb("part", [P, 2, 2, C, 3, GROUP * P], BF16)
        ps_t = [ph.ps(f"ps_t{s}", [P, 512]) for s in range(2)]
        ps_qk = [[ph.ps(f"ps_{n}{s}", [P, 512]) for s in range(2)] for n in "qk"]
        ps_v = [ph.ps(f"ps_v{s}", [P, 512]) for s in range(2)]
        w_in, h_done, turned, hT_done, qk_mul, v_mul, q_done, k_done, v_done = (
            ph.sem(n) for n in ("w_in", "h_done", "turned", "hT_done", "qk_mul", "v_mul", "q_done", "k_done", "v_done"))
        first_done, rest_done, second_done, third_done = (
            ph.sem(n) for n in ("first_done", "rest_done", "second_done", "third_done"))
        stored = [ph.sem(f"stored{s}") for s in range(2)]
        stats = Stats(nc, k, ph, summed=True)
        block = ph.block()

        def of_tile(t, j):
            return part[:, t // GROUP % 2, :, :, j, t % GROUP * P:(t % GROUP + 1) * P]

        @block.sync
        def _(sp):
            sp.dma_start(w[:, :, :], ins["w3"]).then_inc(w_in, 16)
            sp.dma_start(b_col[:, :, :], ins["b3_col"]).then_inc(w_in, 16)
            sp.dma_start(b_v[:, :], ins["b3_v"]).then_inc(w_in, 16)
            prefetch(sp, a, ins["a_rows"], a_in)
            low, high = slice(0, O), slice(O, 2 * O)
            for t in range(0, NT, GROUP):
                slot, tiles = t // GROUP % 2, min(GROUP, NT - t)
                sp.wait_ge(third_done, t + tiles)
                nodes = slice(t * P, (t + tiles) * P)
                to_q = q_dram[:, :, :, :, nodes]
                for b, half in enumerate((low, high)):
                    of_q, of_k = (part[half, slot, j, :, :, 0:tiles * P] for j in range(2))
                    to_k = k_stack[:, b, :, :, nodes]
                    for r in range(2):
                        sp.dma_start(to_q[low, b, :, r, :], of_q[:, :, 0, :]).then_inc(stored[slot], 16)
                        sp.dma_start(to_q[high, b, :, r, :], of_q[:, :, 1 + r, :]).then_inc(stored[slot], 16)
                        sp.dma_start(to_k[high, :, r, :], of_k[:, :, r, :]).then_inc(stored[slot], 16)
                    sp.dma_start(to_k[high, :, 2, :], of_k[:, :, 0, :]).then_inc(stored[slot], 16)
                    sp.dma_start(to_k[low, :, :, :], of_k).then_inc(stored[slot], 16)
            for slot in range(2):
                sp.wait_ge(stored[slot], 16 * STORES * len(range(slot * GROUP, NT, 2 * GROUP)))

        @block.scalar
        def _(act):
            def normed(t, s):
                wait_reuse(act, turned, t)
                nc.scalar.activation(hs[:, s, :], k.x[:, at_tile(t), :], ACT.Relu,
                                     bias=k.nmr[:, at_tile(t)], scale=k.rstd[:, at_tile(t)]).then_inc(h_done, 1)

            def second(t):
                act.wait_ge(rest_done, t + 1)
                nc.scalar.activation(of_tile(t, 1), rest[:, t % 2, :, :, :], ACT.Copy).then_inc(second_done, 1)

            stats.on_act(act)
            act.wait_ge(stats.done, 1)
            normed(0, 0)
            normed(1, 1)
            act.wait_ge(w_in, 48)
            for t in range(NT):
                if t < NT - 2:
                    normed(t + 2, t % 2)
                if t > 0:
                    second(t - 1)
                act.wait_ge(qk_mul, t + 1)
                wait_reuse(act, third_done, t)
                for c in range(C):
                    nc.scalar.activation(rest[:, t % 2, 1, c, :], ps_qk[1][t % 2][:, c * P:(c + 1) * P],
                                         ACT.Identity, bias=b_col[:, 1, c:c + 1]).then_inc(k_done, 1)
                act.wait_ge(q_done, t + 1)
                act.wait_ge(k_done, C * (t + 1))
                if t % GROUP == 0 and t >= 2 * GROUP:
                    act.wait_ge(stored[t // GROUP % 2], 16 * STORES * (t // (2 * GROUP)))
                nc.scalar.activation(of_tile(t, 0), rest[:, t % 2, :, :, :], ACT.Copy).then_inc(first_done, 1)
            second(NT - 1)

        @block.tensor
        def _(pe):
            def turn(t, s):
                pe.wait_ge(h_done, t + 1)
                wait_reuse(pe, hT_done, t)
                for c in range(C):
                    mm = nc.tensor.transpose(ps_t[s][:, c * P:(c + 1) * P], hs[:, s, c * P:(c + 1) * P], k.ident[:, :])
                mm.then_inc(turned, 1)

            def body(t, s):
                if not last(t):
                    turn(t + 1, 1 - s)
                pe.wait_ge(hT_done, t + 1)
                wait_reuse(pe, q_done, t)
                wait_reuse(pe, k_done, t, per=C)
                for f in range(2 * C):
                    for c in range(C):
                        mm = nc.tensor.matmul(ps_qk[f // C][s][:, f % C * P:(f % C + 1) * P], w[:, c, f * P:(f + 1) * P],
                                              hT[:, s, c * P:(c + 1) * P], start=(c == 0), stop=(c == C - 1))
                mm.then_inc(qk_mul, 1)
                wait_reuse(pe, v_done, t)
                for c in range(C):
                    mm = nc.tensor.matmul(ps_v[s][:, 0:D], hT[:, s, c * P:(c + 1) * P], w[:, c, 2 * D:3 * D],
                                          start=(c == 0), stop=(c == C - 1))
                mm.then_inc(v_mul, 1)
            turn(0, 0)
            pe.wait_ge(w_in, 48)
            over_tiles(pe, body)

        @block.vector
        def _(dve):
            def fixed(t):
                dve.wait_ge(turned, t + 1)
                wait_reuse(dve, v_mul, t)
                nc.vector.tensor_copy(hT[:, t % 2, :], ps_t[t % 2][:, 0:D]).then_inc(hT_done, 1)

            def third(t):
                dve.wait_ge(second_done, t + 1)
                nc.vector.tensor_tensor(of_tile(t, 2), rest[:, t % 2, :, :, :], of_tile(t, 1),
                                        ALU.subtract).then_inc(third_done, 1)

            stats.on_dve(dve)
            dve.wait_ge(w_in, 48)
            fixed(0)
            for t in range(NT):
                if t < NT - 1:
                    fixed(t + 1)
                dve.wait_ge(qk_mul, t + 1)
                wait_reuse(dve, third_done, t)
                for c in range(C):
                    q_c = nc.vector.tensor_scalar(rest[:, t % 2, 0, c, :], ps_qk[0][t % 2][:, c * P:(c + 1) * P],
                                                  b_col[:, 0, c:c + 1], float(O) ** -0.5, ALU.add, ALU.mult)
                q_c.then_inc(q_done, 1)
                if t > 0:
                    third(t - 1)
                dve.wait_ge(v_mul, t + 1)
                nc.vector.tensor_tensor(v[:, t, :], ps_v[t % 2][:, 0:D], b_v[:, :], ALU.add).then_inc(v_done, 1)
                dve.wait_ge(first_done, t + 1)
                nc.vector.tensor_tensor(rest[:, t % 2, :, :, :], rest[:, t % 2, :, :, :], of_tile(t, 0),
                                        ALU.subtract).then_inc(rest_done, 1)
            third(NT - 1)


COLS = 512
PIECES = [(j * COLS, min(COLS, N - j * COLS)) for j in range((N + COLS - 1) // COLS)]
QUADS = [(m, min(4, NT - m)) for m in range(0, NT, 4)]
RING = 3
DVE_QUADS = (3, 5)
ACT_QUADS = tuple(c for c in range(len(QUADS)) if c not in DVE_QUADS)


def masked_attend(nc, k, ins, q_dram, k_stack, v, a, a_in, H, O):
    NPC, NQ = len(PIECES), len(QUADS)
    assert NPC % RING == 0 and NQ % RING == 0
    with Phase(nc, "ma_at") as ph:
        mask = ph.sb("mask", [P, N], BF16)
        q = ph.sb("q", [P, 2, 2 * H, P], BF16)
        z = ph.sb("z", [P, 2, NP])
        pT = ph.sb("pT", [P, 2, NP])
        gb = ph.sb("gb", [P, 1])
        wo = ph.sb("wo", [P, C, D])
        b_o = ph.sb("b_o", [P, D])
        part_max = ph.sb("part_max", [P, 2, NPC])
        row_max = ph.sb("row_max", [P, 2])
        neg_max = ph.sb("neg_max", [P, 2])
        den = ph.sb("den", [P, 2, H])
        inv = ph.sb("inv", [P, 2, H])
        o = ph.sb("o", [P, 2, D])
        oT = ph.sb("oT", [P, 2, D])
        ps_s = [ph.ps(f"ps_s{r}", [P, COLS]) for r in range(RING)]
        ps_p = [ph.ps(f"ps_p{r}", [P, 4 * P]) for r in range(RING)]
        ps_o = [ph.ps(f"ps_o{s}", [P, 512]) for s in range(2)]
        q_in = [ph.sem(f"q_in{s}") for s in range(2)]
        (w_in, pad_done, xb_done, mask_done, bias_done, scored, summed, max_done, neg_done, p_done, turned) = (
            ph.sem(n) for n in ("w_in", "pad_done", "xb_done", "mask_done", "bias_done", "scored", "summed",
                                "max_done", "neg_done", "p_done", "turned"))
        pT_act, pT_dve, pv_done, inv_done, o_done, o_turned, oT_done, out_done, x_done = (
            ph.sem(n) for n in ("pT_act", "pT_dve", "pv_done", "inv_done", "o_done", "o_turned", "oT_done", "out_done",
                                "x_done"))
        block = ph.block()

        def shifted(t, s, h, by):
            over, h = (h + by) // H, (h + by) % H
            if isinstance(t, int) and not 0 <= t + over < NT:
                return None
            return (t + over, (s + over) % 2, h) if over else (t, s, h)

        def do(stage, at):
            if at is not None:
                stage(*at)

        @block.sync
        def _(sp):
            sp.dma_start(gb[:, :], ins["gb"]).then_inc(w_in, 16)
            sp.dma_start(wo[:, :, :], ins["w_out"]).then_inc(w_in, 16)
            sp.dma_start(b_o[:, :], ins["b_out"]).then_inc(w_in, 16)

            def body(t, s):
                if not prefetched(t):
                    wait_count(sp, summed, t, H * NPC, H * NPC - 2 * H * NPC)
                    sp.dma_start(a[:, s, :], ins["a_rows"][at_tile(t), :, :]).then_inc(a_in[s], 16)
                wait_count(sp, scored, t, H * NPC, H * NPC - 2 * H * NPC)
                sp.dma_start(q[:, s, :, :],
                             q_dram[:, :, :, :, bass.ds(t * P, P)].rearrange("p b c r n -> p (b c r) n")).then_inc(q_in[s], 16)
            over_tiles(sp, body)

        @block.gpsimd
        def _(pool):
            nc.gpsimd.memset(z[:, :, N:NP], 0.0).then_inc(pad_done, 1)

        @block.scalar
        def _(act):
            def exps(t, s, h):
                wait_count(act, neg_done, t, H, h + 1)
                if h == 0:
                    wait_reuse(act, inv_done, t)
                nc.scalar.activation(z[:, h % 2, 0:N], z[:, h % 2, 0:N], ACT.Exp, bias=neg_max[:, h % 2:h % 2 + 1],
                                     accum_out=den[:, s, h:h + 1]).then_inc(p_done, 1)

            def evacuate(t, s, h):
                wait_count(act, pv_done, t, H, h + 1 - 2)
                for c in ACT_QUADS:
                    m0, n = QUADS[c]
                    wait_count(act, turned, t, NQ * H, NQ * h + c + 1)
                    nc.scalar.activation(pT[:, h % 2, m0 * P:(m0 + n) * P], ps_p[c % RING][:, 0:n * P],
                                         ACT.Copy).then_inc(pT_act, 1)

            def keep_o(t, s):
                act.wait_ge(o_turned, t + 1)
                wait_reuse(act, out_done, t)
                nc.scalar.activation(oT[:, s, :], ps_o[s][:, D:2 * D], ACT.Copy).then_inc(oT_done, 1)

            def body(t, s):
                for h in range(H):
                    exps(t, s, h)
                    evacuate(t, s, h)
                    if h == 2 and not (isinstance(t, int) and t == 0):
                        keep_o(t - 1, 1 - s)
            over_tiles(act, body)
            keep_o(NT - 1, 1)

        @block.tensor
        def _(pe):
            def scores(t, s, h):
                if h == 0:
                    wait_in(pe, q_in[s], t, s)
                for j, (c0, n) in enumerate(PIECES):
                    wait_count(pe, summed, t, H * NPC, NPC * h + j + 1 - RING)
                    for r in range(3):
                        mm = nc.tensor.matmul(ps_s[j % RING][:, 0:n], q[:, s, h % 2 * 4 + h // 2 * 2 + r // 2, :],
                                              k_stack[:, h % 2, h // 2, r, c0:c0 + n], start=(r == 0), stop=(r == 2))
                    mm.then_inc(scored, 1)

            def wait_bank(t, h, c):
                over, b = divmod(c - RING, NQ)
                sem, quads = (pT_dve, DVE_QUADS) if b in DVE_QUADS else (pT_act, ACT_QUADS)
                wait_count(pe, sem, t, len(quads) * H, len(quads) * (h + over) + quads.index(b) + 1)

            def turn(t, s, h):
                wait_count(pe, p_done, t, H, h + 1)
                for c, (m0, n) in enumerate(QUADS):
                    wait_bank(t, h, c)
                    for m in range(m0, m0 + n):
                        mm = nc.tensor.transpose(ps_p[c % RING][:, (m - m0) * P:(m - m0 + 1) * P],
                                                 z[:, h % 2, m * P:(m + 1) * P], k.ident[:, :])
                    mm.then_inc(turned, 1)

            def values(t, s, h):
                wait_count(pe, pT_act, t, len(ACT_QUADS) * H, len(ACT_QUADS) * (h + 1))
                wait_count(pe, pT_dve, t, len(DVE_QUADS) * H, len(DVE_QUADS) * (h + 1))
                if h == 0:
                    wait_reuse(pe, x_done, t)
                for m in range(NT):
                    mm = nc.tensor.matmul(ps_o[s][:, h * O:(h + 1) * O], pT[:, h % 2, m * P:(m + 1) * P],
                                          v[:, m, h * O:(h + 1) * O], start=(m == 0), stop=(m == NT - 1))
                mm.then_inc(pv_done, 1)

            def turn_o(t, s):
                pe.wait_ge(o_done, t + 1)
                for c in range(C):
                    mm = nc.tensor.transpose(ps_o[s][:, D + c * P:D + (c + 1) * P], o[:, s, c * P:(c + 1) * P], k.ident[:, :])
                mm.then_inc(o_turned, 1)

            def project(t, s):
                pe.wait_ge(oT_done, t + 1)
                for c in range(C):
                    mm = nc.tensor.matmul(ps_o[s][:, 0:D], oT[:, s, c * P:(c + 1) * P], wo[:, c, :],
                                          start=(c == 0), stop=(c == C - 1))
                mm.then_inc(out_done, 1)

            def body(t, s):
                for h in range(H):
                    do(scores, shifted(t, s, h, 1))
                    turn(t, s, h)
                    do(values, shifted(t, s, h, -1))
                    if h == 1 and not (isinstance(t, int) and t == 0):
                        turn_o(t - 1, 1 - s)
                    if h == 2 and not (isinstance(t, int) and t == 0):
                        project(t - 1, 1 - s)
            pe.wait_ge(w_in, 48)
            pe.wait_ge(pad_done, 1)
            scores(0, 0, 0)
            over_tiles(pe, body)
            values(NT - 1, 1, H - 1)
            turn_o(NT - 1, 1)
            project(NT - 1, 1)

        @block.vector
        def _(dve):
            def bias(t, s):
                wait_in(dve, a_in[s], t, s)
                wait_reuse(dve, bias_done, t, depth=1)
                nc.vector.tensor_scalar(mask[:, :], a[:, s, :], 0.0, -BIG, ALU.is_equal, ALU.mult).then_inc(mask_done, 1)
                dve.wait_ge(mask_done, t + 1)
                nc.vector.scalar_tensor_tensor(out=a[:, s, :], in0=a[:, s, :], scalar=gb[:, 0:1], in1=mask[:, :],
                                               op0=ALU.mult, op1=ALU.add).then_inc(bias_done, 1)

            def logits(t, s, h):
                if h == 0:
                    bias(t, s)
                    dve.wait_ge(bias_done, t + 1)
                wait_count(dve, turned, t, NQ * H, NQ * (h + 1 - 2))
                for j, (c0, n) in enumerate(PIECES):
                    wait_apart(dve, scored, t, H * NPC, NPC * h + j + 1)
                    nc.vector.tensor_tensor_reduce(out=z[:, h % 2, c0:c0 + n], in0=ps_s[j % RING][:, 0:n],
                                                   in1=a[:, s, c0:c0 + n], scale=1.0, scalar=-2 * BIG, op0=ALU.add,
                                                   op1=ALU.max, accum_out=part_max[:, h % 2, j:j + 1]).then_inc(summed, 1)
                wait_count(dve, summed, t, H * NPC, NPC * (h + 1))
                nc.vector.reduce_max(row_max[:, h % 2:h % 2 + 1], part_max[:, h % 2, :], AX.X).then_inc(max_done, 1)
                wait_count(dve, max_done, t, H, h + 1)
                nc.vector.tensor_scalar(neg_max[:, h % 2:h % 2 + 1], row_max[:, h % 2:h % 2 + 1], -1.0, None,
                                        ALU.mult).then_inc(neg_done, 1)

            def evacuate(t, s, h):
                wait_count(dve, pv_done, t, H, h + 1 - 2)
                for c in DVE_QUADS:
                    m0, n = QUADS[c]
                    wait_count(dve, turned, t, NQ * H, NQ * h + c + 1)
                    nc.vector.tensor_copy(pT[:, h % 2, m0 * P:(m0 + n) * P], ps_p[c % RING][:, 0:n * P]).then_inc(pT_dve, 1)

            def normalise(t, s):
                wait_count(dve, p_done, t, H, H)
                nc.vector.reciprocal(inv[:, s, :], den[:, s, :]).then_inc(inv_done, 1)
                dve.wait_ge(inv_done, t + 1)
                wait_count(dve, pv_done, t, H, H)
                wait_reuse(dve, o_turned, t)
                nc.vector.tensor_tensor(o[:, s, :].rearrange("p (h o) -> p h o", h=H),
                                        ps_o[s][:, 0:D].rearrange("p (h o) -> p h o", h=H),
                                        inv[:, s, :].unsqueeze(2).to_broadcast([P, H, O]), ALU.mult).then_inc(o_done, 1)

            def finish(t, s):
                dve.wait_ge(out_done, t + 1)
                nc.vector.tensor_tensor(k.x[:, at_tile(t), :], k.x[:, at_tile(t), :], ps_o[s][:, 0:D].unsqueeze(1),
                                        ALU.add).then_inc(x_done, 1)
                dve.wait_ge(x_done, t + 1)
                nc.vector.tensor_tensor(k.x[:, at_tile(t), :], k.x[:, at_tile(t), :], b_o[:, :].unsqueeze(1),
                                        ALU.add).then_inc(xb_done, 1)

            def body(t, s):
                for h in range(H):
                    do(logits, shifted(t, s, h, 1))
                    evacuate(t, s, h)
                    if h == 0 and not (isinstance(t, int) and t == 0):
                        normalise(t - 1, 1 - s)
                    if h == 3 and not (isinstance(t, int) and t == 0):
                        finish(t - 1, 1 - s)
            dve.wait_ge(w_in, 48)
            logits(0, 0, 0)
            over_tiles(dve, body)
            normalise(NT - 1, 1)
            finish(NT - 1, 1)


class Kept:
    pass


def program(nc, ins, out):
    k = Kept()
    with ExitStack() as ctx:
        def sb(name, shape, dt=F32):
            return ctx.enter_context(nc.sbuf_tensor(name, shape, dt))
        k.x = sb("x", [P, NT, D])
        k.ident = sb("ident", [P, P])
        k.offdiag = sb("offdiag", [P, P])
        k.ones = sb("ones", [P, P])
        k.eps = sb("eps", [P, 1])
        k.dis = sb("dis", [P, NT])
        k.diag = sb("diag", [P, NT])
        k.bn = sb("bn", [P, NT, 6])
        k.wa = sb("wa", [P, C, 2 * HEADS])
        k.rstd = sb("rstd", [P, NT])
        k.nmr = sb("nmr", [P, NT])
        load_constants(nc, k, ins)
        gcn(nc, k, ins)
        gat(nc, k, ins)
        signed_gat(nc, k, ins)
        masked_attention(nc, k, ins)
        with Phase(nc, "store") as ph:
            stored = ph.sem("stored")
            block = ph.block()

            @block.sync
            def _(sp):
                sp.dma_start(out, k.x[:, :, :]).then_inc(stored, 16)
                sp.wait_ge(stored, 16)


def kernel(**inputs):
    import numpy as np
    import concourse.bacc as bacc
    from concourse.bass_utils import run_bass_kernel_spmd

    x, adj = np.asarray(inputs["x"]), np.asarray(inputs["adj"])

    def rows(a, width):
        return np.ascontiguousarray(np.asarray(a).reshape(-1, P, width).transpose(1, 0, 2))

    def spread(a):
        a = np.asarray(a).reshape(1, -1)
        return np.ascontiguousarray(np.broadcast_to(a, (P, a.shape[1])))

    def stack(*vectors):
        return np.ascontiguousarray(np.stack([spread(v) for v in vectors], axis=1))

    adj_rows = np.zeros((NP, N), adj.dtype)
    adj_rows[:N] = adj
    adj_sq = np.zeros((NP, NP), adj.dtype)
    adj_sq[:N, :N] = adj
    x_pad = np.zeros((NP, D), x.dtype)
    x_pad[:N] = x
    arrays = {
        "x": rows(x_pad, D),
        "a_rows": adj_rows.reshape(NT, P, N),
        "at": np.ascontiguousarray(adj_sq.reshape(NT, P, NT, P).transpose(0, 3, 2, 1)).reshape(NT, P, NP),
        "w0": rows(inputs["L0_gnn_W"], D),
        "b0": spread(inputs["L0_gnn_b"]),
        "w1": rows(inputs["L1_gnn_weight"], D),
        "pw1": rows(np.asarray(inputs["L1_gnn_proj_w"]).T, D),
        "uv1": stack(inputs["L1_gnn_weight_u"], inputs["L1_gnn_weight_v"]),
        "b1": stack(inputs["L1_gnn_bias"], inputs["L1_gnn_proj_b"]),
    }
    diag = np.zeros((NP,), adj.dtype)
    diag[:N] = np.diagonal(adj)
    arrays["diag"] = np.ascontiguousarray(diag.reshape(NT, P).T)
    gat_w = np.asarray(inputs["L2_gnn_gat_W"])
    arrays["w2"] = np.ascontiguousarray(gat_w.reshape(HEADS, C, P, D).transpose(2, 0, 1, 3))
    gat_a = np.asarray(inputs["L2_gnn_gat_a"]).reshape(1, HEADS, 2, D)
    arrays["a2"] = np.ascontiguousarray(np.broadcast_to(gat_a, (P, HEADS, 2, D)))
    for cell in ("edge", "node"):
        for part in ("ih", "hh"):
            arrays[f"{cell}_w{part}"] = rows(np.asarray(inputs[f"L2_gnn_{cell}_W{part}"]).T, 3 * D)
            arrays[f"{cell}_b{part}"] = spread(inputs[f"L2_gnn_{cell}_b{part}"])
    arrays["w3"] = rows(inputs["L3_gnn_Wqkv"], 3 * D)
    bqkv = np.asarray(inputs["L3_gnn_bqkv"])
    arrays["b3_col"] = np.ascontiguousarray(bqkv[:2 * D].reshape(2, C, P).transpose(2, 0, 1))
    arrays["b3_v"] = spread(bqkv[2 * D:])
    arrays["gb"] = spread(inputs["L3_gnn_graph_bias"])
    arrays["w_out"] = rows(inputs["L3_gnn_Wout"], D)
    arrays["b_out"] = spread(inputs["L3_gnn_bout"])
    nc = bacc.Bacc("TRN2", target_bir_lowering=False, num_devices=1)
    ins = {n: nc.dram_tensor(f"in_{n}", a.shape, mybir.dt.from_np(a.dtype), kind="ExternalInput").ap()
           for n, a in arrays.items()}
    out = nc.dram_tensor("out_x", (P, NT, D), F32, kind="ExternalOutput").ap()
    program(nc, ins, out)
    r = run_bass_kernel_spmd(nc, [{f"in_{n}": a for n, a in arrays.items()}], core_ids=[0])
    got = r.results[0]["out_x"]
    return np.ascontiguousarray(got.transpose(1, 0, 2).reshape(NP, D)[:N])
```
